# Optimizing a Trainium2 kernel written in Bass

```python
import numpy as np
import jax
import jax.numpy as jnp

def _softmax(x, axis=-1):
    return jax.nn.softmax(x, axis=axis)

def _gelu(x):
    return jax.nn.gelu(x, approximate=True)

def _silu(x):
    return jax.nn.silu(x)

def _sigmoid(x):
    return jax.nn.sigmoid(x)

def _layernorm(x, axis=-1, eps=1e-05):
    m = jnp.mean(x, axis=axis, keepdims=True)
    v = jnp.var(x, axis=axis, keepdims=True)
    return (x - m) / jnp.sqrt(v + eps)

def _scatter_add(tgt, idx, src, axis=0):
    return tgt.at[idx].add(src)

def _segment_sum(src, seg, n):
    return jax.ops.segment_sum(src, seg, n)
kernel_name = 'mk_xattn_ffn_d2_seqx_r8_46f43a'

def setup_inputs(seed: int=0):
    np.random.seed(seed)
    _w = jnp.asarray

    def _rec_inputs():
        import jax
        import jax.numpy as jnp
        _rk = jax.random.key(seed)
        x = -0.0003929 + 0.9999 * jax.random.normal(jax.random.fold_in(_rk, 1), (16, 256, 128), jnp.float32)
        _lenS = 256 - jax.random.randint(jax.random.fold_in(_rk, 7), (16,), 0, max(1, 256 // 4) + 1, jnp.int32)
        _lenS2 = 1601 - jax.random.randint(jax.random.fold_in(_rk, 8), (16,), 0, max(1, 1601 // 4) + 1, jnp.int32)
        _ctx_1024P = jax.random.normal(jax.random.fold_in(_rk, 11), (16, 16, 128), jnp.float32)
        _ctx_1024c = jax.random.dirichlet(jax.random.fold_in(_rk, 511), 0.3 * jnp.ones((16,), jnp.float32), (16, 1601))
        _ctx_1024t = jnp.einsum('bsk,bkd->bsd', _ctx_1024c, _ctx_1024P)
        _ctx_1024t = _ctx_1024t * jax.lax.rsqrt(jnp.mean(jnp.square(_ctx_1024t)) + 1e-12) * 0.953939
        ctx_1024 = 2.81802e-05 + 1.00001 * (_ctx_1024t + 0.3 * jax.random.normal(jax.random.fold_in(_rk, 611), (16, 1601, 128), jnp.float32))
        itok_BxS_0_7 = jax.random.randint(jax.random.fold_in(_rk, 12), (16, 256), 0, 8, jnp.int32)
        itok_BxS_0_4092 = jax.random.randint(jax.random.fold_in(_rk, 13), (16, 256), 0, 4093, jnp.int32)
        return (x, ctx_1024, itok_BxS_0_7, itok_BxS_0_4092)
    x, ctx_1024, itok_BxS_0_7, itok_BxS_0_4092 = _rec_inputs()

    def _L0_xattn_setup():
        import math
        import jax, jax.numpy as jnp
        import numpy as np
        B, T, L, H = (4, 512, 512, 128)

        def _forward(hidden_states, advisor_states, advisor_ids, pointer_ids, Wqj, Wkj, Wvj, Wqi, Wki, Wvi, Wout, gain, council_weights):
            b, t, h = hidden_states.shape
            l = advisor_states.shape[1]
            inv_sqrt_h = 1.0 / math.sqrt(float(h))
            p = pointer_ids[:, :, None]
            indices = jnp.clip(jnp.concatenate([p, p + 1, p + 2], axis=-1), 0, l - 1)
            win_states = jax.vmap(lambda a, idx: a[idx])(advisor_states, indices)
            win_ids = jax.vmap(lambda a, idx: a[idx])(advisor_ids, indices)
            qj = hidden_states @ Wqj.T
            kj = win_states @ Wkj.T
            vj = win_states @ Wvj.T
            sj = jnp.einsum('bth,btwh->btw', qj, kj) * inv_sqrt_h
            l_rel, l_v1, l_v2 = (sj[:, :, 0], sj[:, :, 1], sj[:, :, 2])
            rel_ids = win_ids[:, :, 0]
            is_and = (rel_ids == 0).astype(sj.dtype)
            is_or = (rel_ids == 1).astype(sj.dtype)
            is_not = (rel_ids == 2).astype(sj.dtype)
            is_implies = (rel_ids == 3).astype(sj.dtype)
            is_xor = (rel_ids == 4).astype(sj.dtype)
            l_new = is_and * (l_v1 + l_v2) + is_or * jnp.maximum(l_v1, l_v2) + is_not * -l_v1 + is_implies * jnp.maximum(-l_v1, l_v2) + is_xor * jnp.abs(l_v1 - l_v2)
            mask_any = jnp.clip(is_and + is_or + is_not + is_implies + is_xor, 0.0, 1.0)
            l_final = mask_any * l_new + (1.0 - mask_any) * l_rel
            sj = jnp.stack([l_final, l_v1, l_v2], axis=-1)
            aj = jax.nn.softmax(sj, axis=-1)
            cj = jnp.einsum('btw,btwh->bth', aj, vj)
            qi = hidden_states @ Wqi.T
            ki = win_states @ Wki.T
            vi = win_states @ Wvi.T
            si = jnp.einsum('bth,btwh->btw', qi, ki) * inv_sqrt_h
            ai = jax.nn.softmax(si, axis=-1)
            ci = jnp.einsum('btw,btwh->bth', ai, vi)
            w = jax.nn.softmax(council_weights, axis=0)
            context = w[0] * cj + w[1] * ci
            return context @ Wout.T * gain
        key = jax.random.key(seed)
        ks = jax.random.split(key, 12)
        inp = {'hidden_states': jax.random.normal(ks[0], (B, T, H), jnp.float32), 'advisor_states': jax.random.normal(ks[1], (B, L, H), jnp.float32), 'advisor_ids': jax.random.randint(ks[2], (B, L), 0, 8, jnp.int32), 'pointer_ids': jax.random.randint(ks[3], (B, T), 0, L - 2, jnp.int32)}
        s = 1.0 / math.sqrt(H)
        names = ['Wqj', 'Wkj', 'Wvj', 'Wqi', 'Wki', 'Wvi', 'Wout']
        for i, n in enumerate(names):
            inp[n] = jax.random.normal(ks[4 + i], (H, H), jnp.float32) * s
        inp['gain'] = jnp.asarray(0.1, jnp.float32)
        inp['council_weights'] = jnp.ones((2,), jnp.float32)
        return inp
    _L0_xattn_all = _L0_xattn_setup()
    _L0_xattn_in = {k: v for k, v in _L0_xattn_all.items() if k in ('Wqj', 'Wkj', 'Wvj', 'Wqi', 'Wki', 'Wvi', 'Wout', 'gain', 'council_weights')}
    del _L0_xattn_all

    def _L0_ffn_setup():
        import jax, jax.numpy as jnp
        import numpy as np
        B, S, D, E, TOP_K = (2, 128, 128, 8, 2)
        H = 4 * D
        key = jax.random.key(seed)
        ks = jax.random.split(key, 12)
        sc = 0.02
        return {'x': jax.random.normal(ks[0], (B, S, D), jnp.float32), 'Wg': jax.random.normal(ks[1], (E, D), jnp.float32) * sc, 'bg': jnp.zeros((E,), jnp.float32), 'bias': jnp.zeros((E,), jnp.float32), 'W1': jax.random.normal(ks[2], (E, H, D), jnp.float32) * sc, 'b1': jnp.zeros((E, H), jnp.float32), 'W2': jax.random.normal(ks[3], (E, D, H), jnp.float32) * sc, 'b2': jnp.zeros((E, D), jnp.float32), 'Ws1': jax.random.normal(ks[4], (H, D), jnp.float32) * sc, 'bs1': jnp.zeros((H,), jnp.float32), 'Ws2': jax.random.normal(ks[5], (D, H), jnp.float32) * sc, 'bs2': jnp.zeros((D,), jnp.float32)}
    _L0_ffn_all = _L0_ffn_setup()
    _L0_ffn_in = {k: v for k, v in _L0_ffn_all.items() if k in ('Wg', 'bg', 'bias', 'W1', 'b1', 'W2', 'b2', 'Ws1', 'bs1', 'Ws2', 'bs2')}
    del _L0_ffn_all

    def _L1_xattn_setup():
        import jax, jax.numpy as jnp
        import numpy as np
        D_MODEL = 128
        NUM_HEADS = 16
        D_K = D_MODEL // NUM_HEADS

        def _split_heads(x):
            B, S, _ = x.shape
            return x.reshape(B, S, NUM_HEADS, D_K).transpose(0, 2, 1, 3)
        key = jax.random.key(seed)
        ks = jax.random.split(key, 11)
        B, S = (2, 256)
        scale = 1.0 / np.sqrt(D_MODEL)
        inp = {'q': jax.random.normal(ks[0], (B, S, D_MODEL), jnp.float32), 'k': jax.random.normal(ks[1], (B, S, D_MODEL), jnp.float32), 'v': jax.random.normal(ks[2], (B, S, D_MODEL), jnp.float32), 'Wq': jax.random.normal(ks[3], (D_MODEL, D_MODEL), jnp.float32) * scale, 'bq': jnp.zeros((D_MODEL,), jnp.float32), 'Wk': jax.random.normal(ks[4], (D_MODEL, D_MODEL), jnp.float32) * scale, 'bk': jnp.zeros((D_MODEL,), jnp.float32), 'Wv': jax.random.normal(ks[5], (D_MODEL, D_MODEL), jnp.float32) * scale, 'bv': jnp.zeros((D_MODEL,), jnp.float32), 'Wo': jax.random.normal(ks[6], (D_MODEL, D_MODEL), jnp.float32) * scale, 'bo': jnp.zeros((D_MODEL,), jnp.float32)}
        return inp
    _L1_xattn_all = _L1_xattn_setup()
    _L1_xattn_in = {k: v for k, v in _L1_xattn_all.items() if k in ('Wq', 'bq', 'Wk', 'bk', 'Wv', 'bv', 'Wo', 'bo')}
    del _L1_xattn_all

    def _L1_ffn_setup():
        import jax, jax.numpy as jnp
        import numpy as np
        BS, L, D = (4, 256, 128)
        H, E, K = (8, 16, 2)
        HD = D // H
        I = 512 // H
        key = jax.random.key(seed)
        ks = jax.random.split(key, 10)
        s = lambda k, shp, fan: jax.random.normal(k, shp, jnp.float32) / np.sqrt(fan)
        return {'x': jax.random.normal(ks[0], (BS, L, D), jnp.float32), 'Wm': s(ks[1], (D, D), D), 'bm': jnp.zeros((D,), jnp.float32), 'expert_emb': jax.random.normal(ks[2], (HD, E), jnp.float32), 'W1': s(ks[3], (E, HD, I), HD), 'b1': jnp.zeros((E, I), jnp.float32), 'W2': s(ks[4], (E, I, HD), I), 'b2': jnp.zeros((E, HD), jnp.float32), 'Wo': s(ks[5], (D, D), D), 'bo': jnp.zeros((D,), jnp.float32)}
    _L1_ffn_all = _L1_ffn_setup()
    _L1_ffn_in = {k: v for k, v in _L1_ffn_all.items() if k in ('Wm', 'bm', 'expert_emb', 'W1', 'b1', 'W2', 'b2', 'Wo', 'bo')}
    del _L1_ffn_all
    return {'x': x, 'ctx_1024': ctx_1024, 'itok_BxS_0_7': itok_BxS_0_7, 'itok_BxS_0_4092': itok_BxS_0_4092, 'L0_xattn_Wqj': _L0_xattn_in['Wqj'], 'L0_xattn_Wkj': _L0_xattn_in['Wkj'], 'L0_xattn_Wvj': _L0_xattn_in['Wvj'], 'L0_xattn_Wqi': _L0_xattn_in['Wqi'], 'L0_xattn_Wki': _L0_xattn_in['Wki'], 'L0_xattn_Wvi': _L0_xattn_in['Wvi'], 'L0_xattn_Wout': _L0_xattn_in['Wout'], 'L0_xattn_gain': _L0_xattn_in['gain'], 'L0_xattn_council_weights': _L0_xattn_in['council_weights'], 'L0_ffn_Wg': _L0_ffn_in['Wg'], 'L0_ffn_bg': _L0_ffn_in['bg'], 'L0_ffn_bias': _L0_ffn_in['bias'], 'L0_ffn_W1': _L0_ffn_in['W1'], 'L0_ffn_b1': _L0_ffn_in['b1'], 'L0_ffn_W2': _L0_ffn_in['W2'], 'L0_ffn_b2': _L0_ffn_in['b2'], 'L0_ffn_Ws1': _L0_ffn_in['Ws1'], 'L0_ffn_bs1': _L0_ffn_in['bs1'], 'L0_ffn_Ws2': _L0_ffn_in['Ws2'], 'L0_ffn_bs2': _L0_ffn_in['bs2'], 'L1_xattn_Wq': _L1_xattn_in['Wq'], 'L1_xattn_bq': _L1_xattn_in['bq'], 'L1_xattn_Wk': _L1_xattn_in['Wk'], 'L1_xattn_bk': _L1_xattn_in['bk'], 'L1_xattn_Wv': _L1_xattn_in['Wv'], 'L1_xattn_bv': _L1_xattn_in['bv'], 'L1_xattn_Wo': _L1_xattn_in['Wo'], 'L1_xattn_bo': _L1_xattn_in['bo'], 'L1_ffn_Wm': _L1_ffn_in['Wm'], 'L1_ffn_bm': _L1_ffn_in['bm'], 'L1_ffn_expert_emb': _L1_ffn_in['expert_emb'], 'L1_ffn_W1': _L1_ffn_in['W1'], 'L1_ffn_b1': _L1_ffn_in['b1'], 'L1_ffn_W2': _L1_ffn_in['W2'], 'L1_ffn_b2': _L1_ffn_in['b2'], 'L1_ffn_Wo': _L1_ffn_in['Wo'], 'L1_ffn_bo': _L1_ffn_in['bo']}

def reference(x, ctx_1024, itok_BxS_0_7, itok_BxS_0_4092, L0_xattn_Wqj, L0_xattn_Wkj, L0_xattn_Wvj, L0_xattn_Wqi, L0_xattn_Wki, L0_xattn_Wvi, L0_xattn_Wout, L0_xattn_gain, L0_xattn_council_weights, L0_ffn_Wg, L0_ffn_bg, L0_ffn_bias, L0_ffn_W1, L0_ffn_b1, L0_ffn_W2, L0_ffn_b2, L0_ffn_Ws1, L0_ffn_bs1, L0_ffn_Ws2, L0_ffn_bs2, L1_xattn_Wq, L1_xattn_bq, L1_xattn_Wk, L1_xattn_bk, L1_xattn_Wv, L1_xattn_bv, L1_xattn_Wo, L1_xattn_bo, L1_ffn_Wm, L1_ffn_bm, L1_ffn_expert_emb, L1_ffn_W1, L1_ffn_b1, L1_ffn_W2, L1_ffn_b2, L1_ffn_Wo, L1_ffn_bo):
    import jax
    import jax.numpy as jnp

    def _L0_xattn_ref(hidden_states, advisor_states, advisor_ids, pointer_ids, Wqj, Wkj, Wvj, Wqi, Wki, Wvi, Wout, gain, council_weights):
        import math
        import jax, jax.numpy as jnp
        import numpy as np
        B, T, L, H = (4, 512, 512, 128)

        def _forward(hidden_states, advisor_states, advisor_ids, pointer_ids, Wqj, Wkj, Wvj, Wqi, Wki, Wvi, Wout, gain, council_weights):
            b, t, h = hidden_states.shape
            l = advisor_states.shape[1]
            inv_sqrt_h = 1.0 / math.sqrt(float(h))
            p = pointer_ids[:, :, None]
            indices = jnp.clip(jnp.concatenate([p, p + 1, p + 2], axis=-1), 0, l - 1)
            win_states = jax.vmap(lambda a, idx: a[idx])(advisor_states, indices)
            win_ids = jax.vmap(lambda a, idx: a[idx])(advisor_ids, indices)
            qj = hidden_states @ Wqj.T
            kj = win_states @ Wkj.T
            vj = win_states @ Wvj.T
            sj = jnp.einsum('bth,btwh->btw', qj, kj) * inv_sqrt_h
            l_rel, l_v1, l_v2 = (sj[:, :, 0], sj[:, :, 1], sj[:, :, 2])
            rel_ids = win_ids[:, :, 0]
            is_and = (rel_ids == 0).astype(sj.dtype)
            is_or = (rel_ids == 1).astype(sj.dtype)
            is_not = (rel_ids == 2).astype(sj.dtype)
            is_implies = (rel_ids == 3).astype(sj.dtype)
            is_xor = (rel_ids == 4).astype(sj.dtype)
            l_new = is_and * (l_v1 + l_v2) + is_or * jnp.maximum(l_v1, l_v2) + is_not * -l_v1 + is_implies * jnp.maximum(-l_v1, l_v2) + is_xor * jnp.abs(l_v1 - l_v2)
            mask_any = jnp.clip(is_and + is_or + is_not + is_implies + is_xor, 0.0, 1.0)
            l_final = mask_any * l_new + (1.0 - mask_any) * l_rel
            sj = jnp.stack([l_final, l_v1, l_v2], axis=-1)
            aj = jax.nn.softmax(sj, axis=-1)
            cj = jnp.einsum('btw,btwh->bth', aj, vj)
            qi = hidden_states @ Wqi.T
            ki = win_states @ Wki.T
            vi = win_states @ Wvi.T
            si = jnp.einsum('bth,btwh->btw', qi, ki) * inv_sqrt_h
            ai = jax.nn.softmax(si, axis=-1)
            ci = jnp.einsum('btw,btwh->bth', ai, vi)
            w = jax.nn.softmax(council_weights, axis=0)
            context = w[0] * cj + w[1] * ci
            return context @ Wout.T * gain
        return _forward(hidden_states, advisor_states, advisor_ids, pointer_ids, Wqj, Wkj, Wvj, Wqi, Wki, Wvi, Wout, gain, council_weights)

    def _L0_ffn_ref(x, Wg, bg, bias, W1, b1, W2, b2, Ws1, bs1, Ws2, bs2):
        import jax, jax.numpy as jnp
        import numpy as np
        B, S, D, E, TOP_K = (2, 128, 128, 8, 2)
        H = 4 * D
        b, s, d = x.shape
        xf = x.reshape(-1, d)
        T = xf.shape[0]
        scores = jax.nn.sigmoid(xf @ Wg.T + bg + bias)
        top_scores, top_idx = jax.lax.top_k(scores, TOP_K)
        weights = jnp.zeros((T, E), scores.dtype)
        weights = weights.at[jnp.arange(T)[:, None], top_idx].add(top_scores)
        h = jax.nn.gelu(jnp.einsum('td,ehd->teh', xf, W1) + b1, approximate=False)
        eo = jnp.einsum('teh,edh->ted', h, W2) + b2
        combined = jnp.einsum('ted,te->td', eo, weights)
        shared = jax.nn.gelu(xf @ Ws1.T + bs1, approximate=False) @ Ws2.T + bs2
        return (shared + combined).reshape(b, s, d)

    def _L1_xattn_ref(q, k, v, Wq, bq, Wk, bk, Wv, bv, Wo, bo):
        import jax, jax.numpy as jnp
        import numpy as np
        D_MODEL = 128
        NUM_HEADS = 16
        D_K = D_MODEL // NUM_HEADS

        def _split_heads(x):
            B, S, _ = x.shape
            return x.reshape(B, S, NUM_HEADS, D_K).transpose(0, 2, 1, 3)
        B, S, _ = q.shape
        qh = _split_heads(q @ Wq + bq)
        kh = _split_heads(k @ Wk + bk)
        vh = _split_heads(v @ Wv + bv)
        scores = jnp.einsum('bhsd,bhtd->bhst', qh, kh) / np.sqrt(D_K)
        attn = jax.nn.softmax(scores, axis=-1)
        out = jnp.einsum('bhst,bhtd->bhsd', attn, vh)
        out = out.transpose(0, 2, 1, 3).reshape(B, S, D_MODEL)
        return out @ Wo + bo

    def _L1_ffn_ref(x, Wm, bm, expert_emb, W1, b1, W2, b2, Wo, bo):
        import jax, jax.numpy as jnp
        import numpy as np
        BS, L, D = (4, 256, 128)
        H, E, K = (8, 16, 2)
        HD = D // H
        I = 512 // H
        bs, L_, d = x.shape
        h = x @ Wm + bm
        t = h.reshape(bs * L_ * H, HD)
        logits = t @ expert_emb
        w = jax.nn.softmax(logits, axis=-1)
        topw, topi = jax.lax.top_k(w, K)
        hmid = jax.nn.gelu(jnp.einsum('td,edi->tei', t, W1) + b1, approximate=False)
        eo = jnp.einsum('tei,eio->teo', hmid, W2) + b2
        sel = jnp.take_along_axis(eo, topi[:, :, None], axis=1)
        comb = (sel * topw[:, :, None]).sum(axis=1)
        out = comb.reshape(bs, L_, d)
        return out @ Wo + bo
    x = x + _L0_xattn_ref(_layernorm(x, axis=-1), ctx_1024, itok_BxS_0_7, itok_BxS_0_4092, L0_xattn_Wqj, L0_xattn_Wkj, L0_xattn_Wvj, L0_xattn_Wqi, L0_xattn_Wki, L0_xattn_Wvi, L0_xattn_Wout, L0_xattn_gain, L0_xattn_council_weights)
    x = x + _L0_ffn_ref(_layernorm(x, axis=-1), L0_ffn_Wg, L0_ffn_bg, L0_ffn_bias, L0_ffn_W1, L0_ffn_b1, L0_ffn_W2, L0_ffn_b2, L0_ffn_Ws1, L0_ffn_bs1, L0_ffn_Ws2, L0_ffn_bs2)
    x = x + _L1_xattn_ref(_layernorm(x, axis=-1), ctx_1024, ctx_1024, L1_xattn_Wq, L1_xattn_bq, L1_xattn_Wk, L1_xattn_bk, L1_xattn_Wv, L1_xattn_bv, L1_xattn_Wo, L1_xattn_bo)
    x = x + _L1_ffn_ref(_layernorm(x, axis=-1), L1_ffn_Wm, L1_ffn_bm, L1_ffn_expert_emb, L1_ffn_W1, L1_ffn_b1, L1_ffn_W2, L1_ffn_b2, L1_ffn_Wo, L1_ffn_bo)
    return x

_drawn_inputs = setup_inputs


def setup_inputs(seed=0):
    import zlib

    import numpy as np

    out = dict(_drawn_inputs(seed))
    spreads = {'L0_xattn_council_weights': (1.0, 0.6),
     'L0_ffn_bg': (0.0, 0.1),
     'L0_ffn_bias': (0.0, 0.1),
     'L0_ffn_b1': (0.0, 0.287),
     'L0_ffn_b2': (0.0, 0.1),
     'L0_ffn_bs1': (0.0, 0.1),
     'L0_ffn_bs2': (0.0, 0.1),
     'L1_xattn_bq': (0.0, 0.274),
     'L1_xattn_bk': (0.0, 2.0),
     'L1_xattn_bv': (0.0, 0.1),
     'L1_xattn_bo': (0.0, 0.1),
     'L1_ffn_bm': (0.0, 0.1),
     'L1_ffn_b1': (0.0, 0.1),
     'L1_ffn_b2': (0.0, 0.1),
     'L1_ffn_bo': (0.0, 0.1)}
    factors = {'L0_xattn_Wqj': 12.804, 'L0_xattn_Wkj': 4.632, 'L0_xattn_Wqi': 3.56, 'L0_xattn_Wki': 3.552}
    for name, (base, spread) in spreads.items():
        noise = np.random.default_rng([zlib.crc32(name.encode()), seed]).standard_normal(out[name].shape)
        drawn = base * np.exp(spread * noise) if base else spread * noise
        out[name] = jnp.asarray(drawn.astype(out[name].dtype))
    for name, factor in factors.items():
        out[name] = (out[name] * factor).astype(out[name].dtype)
    return out
```

```python
from contextlib import ExitStack

import numpy as np
import concourse.bass as bass
from concourse import mybir

F32 = mybir.dt.float32
F32R = mybir.dt.float32r
I32 = mybir.dt.int32
ALU = mybir.AluOpType
ACT = mybir.ActivationFunctionType
AX = mybir.AxisListType.X

P = 128
BATCH, SEQ, D = 16, 256, 128
CTX = 1601
TOKENS = BATCH * SEQ
TILES = TOKENS // P
BT = 4
BLOCK = BT * P
BLOCKS = TILES // BT
EPS = 1e-5

WIN = 3
IDS = 256
SCORE_SCALE0 = 1.0 / float(np.sqrt(float(D)))

EXPERTS0, HID0 = 8, 4 * D
GROUPS0 = EXPERTS0 + 1
CH = HID0 // P

HEADS, DK = 16, 8
HG = 4
GROUPS = HEADS // HG
KT = -(-CTX // P)
CTXP = KT * P
QT = SEQ // P
VW = DK + 1
SCORE_SCALE1 = 1.0 / float(np.sqrt(DK))
SHIFT_ROW = 96
KCH = [(i, min(512, CTX - i)) for i in range(0, CTX, 512)]

H1, E1, HD1, I1 = 8, 16, 16, 64
PAIRS = E1 // 2
HP = H1 // 2


class Chain:

    def __init__(self, eng, sem):
        self.eng, self.sem, self.base, self.n = eng, sem, 0, 0

    def mark(self, ins):
        ins.then_inc(self.sem, 1)
        self.n += 1
        return ins

    def settle(self):
        self.eng.wait_ge(self.sem, self.base + self.n)

    def step(self, ins):
        self.mark(ins)
        self.settle()
        return ins

    def at(self, base):
        self.base, self.n = base, 0


def wait(eng, sem, value, k=0, ring=0):
    if isinstance(value, int) and value <= 0:
        return
    eng.wait_ge(sem, value)


def rounds(eng, count, body):
    body(0, 0, False, 0)
    with eng.Fori(0, (count - 2) // 2) as i:
        body(2 * i + 1, 1, False, i)
        body(2 * i + 2, 0, False, i + 1)
    body(count - 1, 1, True, (count - 2) // 2)


def program(nc, io, phases="ABCD"):
    with ExitStack() as top:
        x_sb = top.enter_context(nc.sbuf_tensor("x_sb", [P, TILES, D], F32))
        ident = top.enter_context(nc.sbuf_tensor("ident", [P, P], F32))
        w1t = top.enter_context(nc.sbuf_tensor("w1t", [P, GROUPS0 * HID0], F32)) if 0 else None
        loaded = top.enter_context(nc.semaphore("loaded"))
        x_rows = io["x"].rearrange("(t p) d -> p t d", p=P)
        out_rows = io["out"].rearrange("(t p) d -> p t d", p=P)
        if "A" not in phases:
            with nc.Block() as block:
                @block.sync
                def _(sp):
                    sp.dma_start(x_sb[:], x_rows).then_inc(loaded, 16)
                    sp.dma_start(ident[:], io["identity"]).then_inc(loaded, 16)
                    sp.wait_ge(loaded, 32)
        if "A" in phases:
            gather_attention(nc, io, x_sb, ident, x_rows, loaded)
        if "B" in phases:
            expert_layer(nc, io, x_sb, ident)
        if "C" in phases:
            head_attention(nc, io, x_sb, ident)
        if "D" in phases:
            head_experts(nc, io, x_sb, ident, out_rows)
            return
        stored = top.enter_context(nc.semaphore("stored"))
        with nc.Block() as block:
            @block.sync
            def _(sp):
                sp.dma_start(out_rows, x_sb[:]).then_inc(stored, 16)
                sp.wait_ge(stored, 16)


class Norm:

    def __init__(self, ctx, nc, tag):
        def sb(name, shape):
            return ctx.enter_context(nc.sbuf_tensor(f"{tag}_{name}", shape, F32))
        self.stats = sb("stats", [P, TILES, 6])
        self.mean = sb("mean", [P, TILES])
        self.var = sb("var", [P, TILES])
        self.std = sb("std", [P, TILES])
        self.tmp = sb("tmp", [P, TILES])
        self.rstd = sb("rstd", [P, TILES])
        self.var_ready = ctx.enter_context(nc.semaphore(f"{tag}_var_ready"))
        self.std_ready = ctx.enter_context(nc.semaphore(f"{tag}_std_ready"))

    def statistics(self, nc, dve, chain, x_sb):
        for t in range(TILES):
            chain.mark(nc.vector.bn_stats(self.stats[:, t, :], x_sb[:, t, :]))
        chain.settle()
        st = self.stats
        chain.mark(nc.vector.tensor_tensor(self.mean[:], st[:, :, 1], st[:, :, 4], ALU.add))
        chain.mark(nc.vector.tensor_tensor(self.tmp[:], st[:, :, 1], st[:, :, 4], ALU.subtract))
        chain.step(nc.vector.tensor_tensor(self.var[:], st[:, :, 2], st[:, :, 5], ALU.add))
        chain.mark(nc.vector.tensor_scalar(self.mean[:], self.mean[:], 0.5, None, ALU.mult))
        chain.mark(nc.vector.tensor_scalar(self.var[:], self.var[:], 1.0 / D, EPS, ALU.mult, ALU.add))
        chain.step(nc.vector.scalar_tensor_tensor(self.tmp[:], self.tmp[:], 0.25, self.tmp[:], ALU.mult, ALU.mult))
        chain.step(nc.vector.tensor_tensor(self.var[:], self.var[:], self.tmp[:], ALU.add))
        nc.vector.tensor_scalar(self.tmp[:], self.var[:], -0.5, None, ALU.mult).then_inc(self.var_ready, 1)
        dve.wait_ge(self.std_ready, 1)
        dve.wait_ge(self.var_ready, 1)
        chain.step(nc.vector.reciprocal(self.rstd[:], self.std[:]))
        chain.step(nc.vector.tensor_tensor(self.std[:], self.rstd[:], self.rstd[:], ALU.mult))
        chain.step(nc.vector.tensor_tensor(self.std[:], self.std[:], self.tmp[:], ALU.mult))
        chain.step(nc.vector.scalar_tensor_tensor(self.rstd[:], self.std[:], 1.5, self.rstd[:], ALU.add, ALU.mult))

    def root(self, nc, act):
        act.wait_ge(self.var_ready, 1)
        nc.scalar.activation(self.std[:], self.var[:], ACT.Sqrt).then_inc(self.std_ready, 1)

    def apply(self, nc, x_sb, t, out):
        return nc.vector.tensor_scalar(out, x_sb[:, bass.ds(t, 1), :].rearrange("p a d -> p (a d)"),
                                       self.mean[:, bass.ds(t, 1)], self.rstd[:, bass.ds(t, 1)],
                                       ALU.subtract, ALU.mult)


def gather_attention(nc, io, x_sb, ident, x_rows, loaded):
    with ExitStack() as ctx:
        def sb(name, shape, dt=F32):
            return ctx.enter_context(nc.sbuf_tensor("A_" + name, shape, dt))

        def ps(name, shape):
            return ctx.enter_context(nc.psum_tensor("A_" + name, shape, F32))

        def sem(name):
            return ctx.enter_context(nc.semaphore("A_" + name))

        DOTS = BT * 2 * WIN
        wq = sb("wq", [P, 2, D])
        wk = sb("wk", [P, 2, D])
        wv = sb("wv", [P, 2, D])
        wout = sb("wout", [P, D])
        gain = sb("gain", [P, 1])
        council = sb("council", [P, 2])
        ptr = sb("ptr", [P, TILES], I32)
        ids = sb("ids", [P, BATCH, IDS], I32)
        position = sb("position", [P, IDS])
        base = sb("base", [P, BATCH, QT], I32)
        index = sb("index", [P, TILES, WIN], I32)
        id_index = sb("id_index", [P, TILES])
        picked = sb("picked", [P, IDS])
        rel = sb("rel", [P, TILES])
        window = sb("window", [P, TILES, WIN, D])
        g_sb = sb("g", [P, 2, D])
        m_sb = sb("m", [P, 2, D])
        cw = sb("cw", [P, 8])
        xn = sb("xn", [P, 2, BT, D])
        xt = sb("xt", [P, 2, BT, P])
        junk = sb("junk", [P, DOTS, D])
        raw = sb("raw", [P, 2, WIN, TILES])
        logic = sb("logic", [P, 12, TILES])
        probs = sb("probs", [P, 2, WIN, TILES])
        soft = sb("soft", [P, 3, 2, TILES])
        z = sb("z", [P, 2, BT, 2, D])
        zt = sb("zt", [P, 2, BT, 2, P])
        norm = Norm(ctx, nc, "A")

        ps_t = [ps(f"ps_t{i}", [P, BT, P]) for i in range(2)]
        ps_u = [ps(f"ps_u{i}", [P, 2, 2, D]) for i in range(4)]
        ps_o = [ps(f"ps_o{i}", [P, BT, D]) for i in range(2)]

        s_ptr = sem("s_ptr")
        s_x = sem("s_x")
        s_w = sem("s_w")
        s_base = sem("s_base")
        s_index = sem("s_index")
        s_window = [sem(f"s_window{i}") for i in range(2)]
        s_gm = sem("s_gm")
        s_gm_used = sem("s_gm_used")
        s_cexp_in = sem("s_cexp_in")
        s_cexp = sem("s_cexp")
        s_xn = sem("s_xn")
        s_tr = sem("s_tr")
        s_xt = sem("s_xt")
        s_u = sem("s_u")
        s_dots = sem("s_dots")
        s_shifted = sem("s_shifted")
        s_exp = sem("s_exp")
        s_z = sem("s_z")
        s_ztr = sem("s_ztr")
        s_zt = sem("s_zt")
        s_o = sem("s_o")
        s_x1 = sem("s_x1")
        s_dve = sem("s_dve")

        ctx_rows = io["ctx"]
        with nc.Block() as block:
            @block.sync
            def _(sp):
                sp.dma_start(ptr[:], io["pointers"]).then_inc(s_ptr, 16)
                for h in range(2):
                    half = slice(h * TILES // 2, (h + 1) * TILES // 2)
                    sp.dma_start(x_sb[:, half, :], x_rows[:, half, :]).then_inc(s_x, 16)
                sp.dma_start(ident[:], io["identity"]).then_inc(s_w, 16)
                for i, n in enumerate("ji"):
                    sp.dma_start(wq[:, i, :], io["L0_xattn_Wq" + n]).then_inc(s_w, 16)
                    sp.dma_start(wk[:, i, :], io["L0_xattn_Wk" + n]).then_inc(s_w, 16)
                    sp.dma_start(wv[:, i, :], io["L0_xattn_Wv" + n]).then_inc(s_w, 16)
                sp.dma_start(wout[:], io["L0_xattn_WoutT"]).then_inc(s_w, 16)
                sp.dma_start(gain[:], io["L0_xattn_gain"].partition_broadcast(P)).then_inc(s_w, 16)
                sp.dma_start(council[:], io["L0_xattn_council_weights"].partition_broadcast(P)).then_inc(s_w, 16)
                sp.dma_start(position[:], io["positions"].partition_broadcast(P)).then_inc(s_w, 16)
                sp.dma_start(ids[:].rearrange("p b i -> p (b i)"),
                             io["ids"].partition_broadcast(P)).then_inc(s_w, 16)
            W_ALL = 16 * 12

            @block.gpsimd
            def _(pool):
                nc.gpsimd.iota(base[:], [[CTX, BATCH], [0, QT]], base=0, channel_multiplier=0).then_inc(s_base, 1)
                pool.wait_ge(s_index, WIN)
                for t in range(TILES):
                    if t % BT == 0:
                        wait(pool, s_dots, DOTS * (t // BT - 1))
                    for w in range(WIN):
                        nc.gpsimd.indirect_dma_start(
                            window[:, t, w, :], None, ctx_rows,
                            bass.IndirectOffsetOnAxis(index[:, t, w:w + 1], axis=0)).then_inc(
                                s_window[t // BT % 2], 16)

            @block.vector
            def _(dve):
                chain = Chain(dve, s_dve)
                dve.wait_ge(s_ptr, 16)
                dve.wait_ge(s_base, 1)
                for w in range(WIN):
                    chain.mark(nc.vector.tensor_scalar(index[:, :, w], ptr[:], float(w), 0.0, ALU.add, ALU.max))
                chain.mark(nc.vector.tensor_scalar(id_index[:], ptr[:], 0.0, float(IDS - 1), ALU.max, ALU.min))
                chain.settle()
                for w in range(WIN):
                    nc.vector.scalar_tensor_tensor(index[:, :, w], index[:, :, w], float(CTX - 1),
                                                   base[:].rearrange("p b q -> p (b q)"),
                                                   ALU.min, ALU.add).then_inc(s_index, 1)
                dve.wait_ge(s_x, 32)
                norm.statistics(nc, dve, chain, x_sb)
                dve.wait_ge(s_w, W_ALL)
                for t in range(TILES):
                    chain.step(nc.vector.scalar_tensor_tensor(
                        picked[:], position[:], id_index[:, t:t + 1], ids[:, t // QT, :],
                        ALU.is_equal, ALU.mult, accum_out=rel[:, t:t + 1]))
                chain.step(nc.vector.tensor_tensor(cw[:, 0:1], council[:, 0:1], council[:, 1:2], ALU.max))
                nc.vector.tensor_scalar(cw[:, 1:3], council[:], cw[:, 0:1], None, ALU.subtract).then_inc(s_cexp_in, 1)
                dve.wait_ge(s_cexp, 1)
                chain.step(nc.vector.tensor_tensor(cw[:, 5:6], cw[:, 3:4], cw[:, 4:5], ALU.add))
                chain.step(nc.vector.reciprocal(cw[:, 6:7], cw[:, 5:6]))
                chain.step(nc.vector.tensor_tensor(cw[:, 6:7], cw[:, 6:7], gain[:], ALU.mult))
                chain.step(nc.vector.tensor_scalar(cw[:, 3:5], cw[:, 3:5], cw[:, 6:7], None, ALU.mult))
                dve.wait_ge(s_gm, 1)
                nc.vector.tensor_copy(g_sb[:], ps_o[0][:, 0:2, :]).then_inc(s_gm_used, 1)
                for i in range(2):
                    nc.vector.tensor_scalar(m_sb[:, i, :], ps_o[0][:, 2 + i, :], cw[:, 3 + i:4 + i], None,
                                            ALU.mult).then_inc(s_gm_used, 1)

                def normalize(k, parity):
                    wait(dve, s_tr, k - 1)
                    for i in range(BT):
                        norm.apply(nc, x_sb, k * BT + i, xn[:, parity, i, :]).then_inc(s_xn, 1)

                normalize(0, 0)

                def dots(k, parity, last, turn):
                    if not last:
                        normalize(k + 1, 1 - parity)
                    dve.wait_ge(s_window[parity], 16 * WIN * BT * (turn + 1))
                    wait(dve, s_dots, DOTS * k)
                    for i in range(BT):
                        if i % 2 == 0:
                            dve.wait_ge(s_u, 2 * k + i // 2 + 1)
                        for q in range(2):
                            for w in range(WIN):
                                nc.vector.tensor_tensor_reduce(
                                    junk[:, (i * 2 + q) * WIN + w, :],
                                    window[:, bass.ds(k * BT + i, 1), w, :].rearrange("p a d -> p (a d)"),
                                    ps_u[2 * parity + i // 2][:, i % 2, q, :], SCORE_SCALE0, 0.0, ALU.mult, ALU.add,
                                    raw[:, q, w, bass.ds(k * BT + i, 1)]).then_inc(s_dots, 1)

                for k in range(BLOCKS):
                    dots(k, k % 2, k == BLOCKS - 1, k // 2)
                dve.wait_ge(s_dots, DOTS * BLOCKS)
                V = nc.vector
                rule, value = [logic[:, i, :] for i in range(5)], [logic[:, 5 + i, :] for i in range(5)]
                any_rule, keep = logic[:, 10, :], logic[:, 11, :]
                l0, l1, l2 = (raw[:, 0, w, :] for w in range(WIN))
                for c in range(5):
                    chain.mark(V.tensor_scalar(rule[c], rel[:], float(c), None, ALU.is_equal))
                chain.mark(V.tensor_tensor(value[0], l1, l2, ALU.add))
                chain.mark(V.tensor_tensor(value[1], l1, l2, ALU.max))
                chain.mark(V.tensor_scalar(value[2], l1, -1.0, None, ALU.mult))
                chain.mark(V.scalar_tensor_tensor(value[3], l1, -1.0, l2, ALU.mult, ALU.max))
                chain.step(V.tensor_tensor(value[4], l1, l2, ALU.subtract))
                chain.step(V.scalar_tensor_tensor(value[4], value[4], -1.0, value[4], ALU.mult, ALU.max))
                chain.mark(V.tensor_tensor(any_rule, rule[0], rule[1], ALU.add))
                for c in range(5):
                    chain.mark(V.tensor_tensor(value[c], rule[c], value[c], ALU.mult))
                for c in range(2, 5):
                    chain.settle()
                    chain.mark(V.tensor_tensor(any_rule, any_rule, rule[c], ALU.add))
                for c in range(1, 5):
                    chain.settle()
                    chain.mark(V.tensor_tensor(value[0], value[0], value[c], ALU.add))
                chain.step(V.tensor_scalar(keep, any_rule, -1.0, 1.0, ALU.mult, ALU.add))
                chain.step(V.tensor_tensor(l0, l0, keep, ALU.mult))
                chain.step(V.tensor_tensor(value[0], value[0], any_rule, ALU.mult))
                chain.step(V.tensor_tensor(l0, l0, value[0], ALU.add))
                top_score, total, inverse = (soft[:, i, :, :] for i in range(3))
                chain.step(V.tensor_tensor(top_score, raw[:, :, 0, :], raw[:, :, 1, :], ALU.max))
                chain.step(V.tensor_tensor(top_score, top_score, raw[:, :, 2, :], ALU.max))
                for w in range(WIN):
                    V.tensor_tensor(probs[:, :, w, :], raw[:, :, w, :], top_score, ALU.subtract).then_inc(s_shifted, 1)
                dve.wait_ge(s_exp, 1)
                chain.step(V.tensor_tensor(total, probs[:, :, 0, :], probs[:, :, 1, :], ALU.add))
                chain.step(V.tensor_tensor(total, total, probs[:, :, 2, :], ALU.add))
                chain.step(V.reciprocal(inverse, total))
                for w in range(WIN):
                    chain.mark(V.tensor_tensor(probs[:, :, w, :], probs[:, :, w, :], inverse, ALU.mult))
                chain.settle()
                before_mix = chain.base + chain.n
                MIX = WIN * 2 * BT

                def mixes(k, parity, last, turn):
                    wait(dve, s_ztr, 2 * k - 1)
                    chain.at(before_mix + MIX * k)
                    for w in range(WIN):
                        for i in range(BT):
                            row = window[:, bass.ds(k * BT + i, 1), w, :].rearrange("p a d -> p (a d)")
                            for q in range(2):
                                to, weight = z[:, parity, i, q, :], probs[:, q, w, bass.ds(k * BT + i, 1)]
                                if w == 0:
                                    chain.mark(V.tensor_scalar(to, row, weight, None, ALU.mult))
                                else:
                                    ins = V.scalar_tensor_tensor(to, row, weight, to, ALU.mult, ALU.add)
                                    chain.mark(ins) if w < WIN - 1 else ins.then_inc(s_z, 1)
                        if w < WIN - 1:
                            chain.settle()

                def add_to_stream(k, parity):
                    dve.wait_ge(s_o, k + 1)
                    to = x_sb[:, bass.ds(k * BT, BT), :]
                    V.tensor_tensor(to, to, ps_o[parity][:], ALU.add).then_inc(s_x1, 1)

                MIX = 2 * BT * (WIN - 1)
                mixes(0, 0, False, 0)
                with dve.Fori(0, (BLOCKS - 2) // 2) as i:
                    mixes(2 * i + 1, 1, False, i)
                    add_to_stream(2 * i, 0)
                    mixes(2 * i + 2, 0, False, i + 1)
                    add_to_stream(2 * i + 1, 1)
                mixes(BLOCKS - 1, 1, True, 0)
                add_to_stream(BLOCKS - 2, 0)
                add_to_stream(BLOCKS - 1, 1)
                dve.wait_ge(s_x1, BLOCKS)

            @block.scalar
            def _(act):
                norm.root(nc, act)
                act.wait_ge(s_cexp_in, 1)
                nc.scalar.activation(cw[:, 3:5], cw[:, 1:3], ACT.Exp).then_inc(s_cexp, 1)

                def turned(k, parity, last, turn):
                    act.wait_ge(s_tr, k + 1)
                    nc.scalar.copy(xt[:, parity, :, :], ps_t[parity][:]).then_inc(s_xt, 1)

                rounds(act, BLOCKS, turned)
                act.wait_ge(s_shifted, WIN)
                nc.scalar.activation(probs[:], probs[:], ACT.Exp).then_inc(s_exp, 1)

                def mixed(k, parity, last, turn):
                    for half in range(2):
                        act.wait_ge(s_ztr, 2 * k + half + 1)
                        nc.scalar.copy(zt[:, parity, 2 * half:2 * half + 2, :, :],
                                       ps_u[2 * parity + half][:]).then_inc(s_zt, 1)

                rounds(act, BLOCKS, mixed)

            @block.tensor
            def _(pe):
                pe.wait_ge(s_w, W_ALL)
                for i in range(2):
                    nc.tensor.matmul(ps_o[0][:, i, :], wq[:, i, :], wk[:, i, :], start=True, stop=True)
                for i in range(2):
                    last_product = nc.tensor.matmul(ps_o[0][:, 2 + i, :], wv[:, i, :], wout[:], start=True, stop=True)
                last_product.then_inc(s_gm, 1)

                def queries(k, parity, last, turn):
                    pe.wait_ge(s_xn, BT * (k + 1))
                    wait(pe, s_xt, k)
                    for i in range(BT):
                        tr = nc.tensor.transpose(ps_t[parity][:, i, :], xn[:, parity, i, :], ident[:])
                    tr.then_inc(s_tr, 1)
                    pe.wait_ge(s_xt, k + 1)
                    if isinstance(k, int) and k == 0:
                        pe.wait_ge(s_gm_used, 1)
                    for half in range(2):
                        wait(pe, s_dots, DOTS * (k - 1) + (0 if isinstance(k, int) else 1))
                        for i in range(2):
                            u = nc.tensor.matmul(ps_u[2 * parity + half][:, i, :, :], xt[:, parity, 2 * half + i, :],
                                                 g_sb[:], start=True, stop=True)
                        u.then_inc(s_u, 1)

                rounds(pe, BLOCKS, queries)
                pe.wait_ge(s_gm_used, 3)
                pe.wait_ge(s_dots, DOTS * BLOCKS)

                def outputs(k, parity, last, turn):
                    wait(pe, s_zt, 2 * k - 1)
                    for half in range(2):
                        pe.wait_ge(s_z, 2 * BT * k + 4 * half + 4)
                        for i in range(4):
                            tr = nc.tensor.transpose(ps_u[2 * parity + half][:, i // 2, i % 2, :],
                                                     z[:, parity, 2 * half + i // 2, i % 2, :], ident[:])
                        tr.then_inc(s_ztr, 1)
                    pe.wait_ge(s_zt, 2 * k + 2)
                    for i in range(BT):
                        for q in range(2):
                            o = nc.tensor.matmul(ps_o[parity][:, i, :], zt[:, parity, i, q, :], m_sb[:, q, :],
                                                 start=(q == 0), stop=(q == 1))
                    o.then_inc(s_o, 1)

                rounds(pe, BLOCKS, outputs)


def expert_layer(nc, io, x_sb, ident):
    with ExitStack() as ctx:
        def sb(name, shape, dt=F32):
            return ctx.enter_context(nc.sbuf_tensor("B_" + name, shape, dt))

        def ps(name, shape):
            return ctx.enter_context(nc.psum_tensor("B_" + name, shape, F32))

        def sem(name):
            return ctx.enter_context(nc.semaphore("B_" + name))

        w_up = sb("w_up", [P, GROUPS0, HID0])
        w_down = sb("w_down", [P, GROUPS0, CH, D])
        b_up = sb("b_up", [P, GROUPS0 * CH])
        b_down = sb("b_down", [GROUPS0, D])
        w_gate = sb("w_gate", [P, EXPERTS0])
        b_gate = sb("b_gate", [P, 2, EXPERTS0])
        order = sb("order", [P, EXPERTS0])
        norm = Norm(ctx, nc, "B")
        xn = sb("xn", [P, 2, BT, D])
        xt = sb("xt", [P, 2, BT, P])
        score = sb("score", [P, BT, EXPERTS0])
        left = sb("left", [P, BT, EXPERTS0])
        best = sb("best", [P, BT])
        hit = sb("hit", [P, BT, EXPERTS0])
        chosen = sb("chosen", [P, 2, BT, EXPERTS0])
        gate = sb("gate", [P, 2, BT, GROUPS0])
        gate_t = sb("gate_t", [GROUPS0, 2, BLOCK])
        HB = 3
        hidden = sb("hidden", [P, HB, CH, BLOCK])
        acc = sb("acc", [P, BT, D])

        ps_t = ps("ps_t", [P, BT, P])
        ps_g = ps("ps_g", [P, BLOCK])
        ps_h = [ps(f"ps_h{i}", [P, BLOCK]) for i in range(CH)]
        ps_e = [ps(f"ps_e{i}", [P, BT, D]) for i in range(2)]

        s_w = sem("s_w")
        s_xn = sem("s_xn")
        s_tr = sem("s_tr")
        s_xt = sem("s_xt")
        s_logit = sem("s_logit")
        s_z = sem("s_z")
        s_sig = sem("s_sig")
        s_gate = sem("s_gate")
        s_gtr = sem("s_gtr")
        s_gt = sem("s_gt")
        s_up = sem("s_up")
        s_hid = sem("s_hid")
        s_down = sem("s_down")
        s_acc = sem("s_acc")
        s_dve = sem("s_dve")
        s_x2 = sem("s_x2")

        UPS = GROUPS0 * CH
        with nc.Block() as block:
            @block.sync
            def _(sp):
                for to, name in ((w_gate[:], "L0_ffn_WgT"), (b_up[:], "L0_ffn_b_up"), (b_down[:], "L0_ffn_b_down")):
                    sp.dma_start(to, io[name]).then_inc(s_w, 16)
                for i, name in enumerate(("bg", "bias")):
                    sp.dma_start(b_gate[:, i, :], io["L0_ffn_" + name].partition_broadcast(P)).then_inc(s_w, 16)
                sp.dma_start(order[:], io["order0"].partition_broadcast(P)).then_inc(s_w, 16)
                sp.dma_start(w_up[:], io["L0_ffn_w_up"]).then_inc(s_w, 16)
                sp.dma_start(w_down[:], io["L0_ffn_w_down"]).then_inc(s_w, 16)
            W_ALL = 16 * 8

            @block.tensor
            def _(pe):
                def turn_block(k, parity):
                    pe.wait_ge(s_xn, BT * (k + 1))
                    wait(pe, s_xt, k)
                    for i in range(BT):
                        tr = nc.tensor.transpose(ps_t[:, i, :], xn[:, parity, i, :], ident[:])
                    tr.then_inc(s_tr, 1)

                def logits(k, parity):
                    pe.wait_ge(s_xt, k + 1)
                    wait(pe, s_gt, k)
                    for i in range(BT):
                        lg = nc.tensor.matmul(ps_g[:, i * EXPERTS0:(i + 1) * EXPERTS0], xt[:, parity, i, :],
                                              w_gate[:], start=True, stop=True)
                    lg.then_inc(s_logit, 1)

                def up(k, parity, e):
                    for c in range(CH):
                        u = e * CH + c
                        wait(pe, s_hid, UPS * k + u - CH + 1)
                        nc.tensor.matmul(ps_h[c][:], w_up[:, e, c * P:(c + 1) * P],
                                         xt[:, parity, :, :].rearrange("p i t -> p (i t)"),
                                         start=True, stop=True).then_inc(s_up, 1)

                def down(k, parity, e):
                    pe.wait_ge(s_hid, UPS * k + (e + 1) * CH)
                    wait(pe, s_acc, BT * (GROUPS0 * k + max(0, e - 1)))
                    for i in range(BT):
                        for c in range(CH):
                            dn = nc.tensor.matmul(ps_e[e % 2][:, i, :], hidden[:, e % HB, c, i * P:(i + 1) * P],
                                                  w_down[:, e, c, :], start=(c == 0),
                                                  stop=(c == CH - 1 and e < EXPERTS0))
                        if e == EXPERTS0:
                            dn = nc.tensor.matmul(ps_e[e % 2][:, i, :], gate_t[:, parity, i * P:(i + 1) * P],
                                                  b_down[:], start=False, stop=True)
                    dn.then_inc(s_down, 1)

                def experts(k, parity, last, turn):
                    for e in range(GROUPS0):
                        up(k, parity, e)
                        if e > 0:
                            down(k, parity, e - 1)
                        if e == 3:
                            pe.wait_ge(s_gate, k + 1)
                            for i in range(BT):
                                tr = nc.tensor.transpose(ps_g[0:GROUPS0, i * P:(i + 1) * P],
                                                         gate[:, parity, i, :], ident[:])
                            tr.then_inc(s_gtr, 1)
                        if e == 5 and not last:
                            turn_block(k + 1, 1 - parity)
                        if e == 6 and not last:
                            logits(k + 1, 1 - parity)
                    pe.wait_ge(s_gt, k + 1)
                    down(k, parity, GROUPS0 - 1)

                pe.wait_ge(s_w, W_ALL)
                turn_block(0, 0)
                logits(0, 0)
                rounds(pe, BLOCKS, experts)

            @block.scalar
            def _(act):
                norm.root(nc, act)

                def turned(k, parity):
                    act.wait_ge(s_tr, k + 1)
                    wait(act, s_down, GROUPS0 * (k - 1))
                    nc.scalar.copy(xt[:, parity, :, :], ps_t[:]).then_inc(s_xt, 1)

                def sigmoid(k):
                    act.wait_ge(s_z, k + 1)
                    nc.scalar.activation(score[:], score[:], ACT.Sigmoid).then_inc(s_sig, 1)

                def gelus(k, parity, last, turn):
                    for e in range(GROUPS0):
                        wait(act, s_down, GROUPS0 * k + e - HB + 1)
                        for c in range(CH):
                            u = e * CH + c
                            act.wait_ge(s_up, UPS * k + u + 1)
                            nc.scalar.activation(hidden[:, e % HB, c, :], ps_h[c][:], ACT.Gelu,
                                                 bias=b_up[:, u:u + 1]).then_inc(s_hid, 1)
                        if e == 3:
                            act.wait_ge(s_gtr, k + 1)
                            nc.scalar.copy(gate_t[:, parity, :], ps_g[0:GROUPS0, :]).then_inc(s_gt, 1)
                        if e == 5 and not last:
                            turned(k + 1, 1 - parity)
                    if not last:
                        sigmoid(k + 1)

                turned(0, 0)
                sigmoid(0)
                rounds(act, BLOCKS, gelus)

            @block.vector
            def _(dve):
                chain = Chain(dve, s_dve)
                V = nc.vector
                norm.statistics(nc, dve, chain, x_sb)
                for parity in range(2):
                    chain.mark(V.memset(gate[:, parity, :, EXPERTS0:], 1.0))
                chain.settle()
                setup = chain.n
                dve.wait_ge(s_w, W_ALL)

                def normalize(k, parity):
                    wait(dve, s_tr, k - 1)
                    for i in range(BT):
                        norm.apply(nc, x_sb, k * BT + i, xn[:, parity, i, :]).then_inc(s_xn, 1)

                def scores(k):
                    dve.wait_ge(s_logit, k + 1)
                    chain.at(setup + STEPS * k)
                    for i in range(2):
                        src = ps_g[:, 0:BT * EXPERTS0].rearrange("p (i e) -> p i e", i=BT) if i == 0 else score[:]
                        ins = V.tensor_tensor(score[:], src, b_gate[:, i:i + 1, :].to_broadcast([P, BT, EXPERTS0]),
                                              ALU.add)
                        chain.step(ins) if i == 0 else ins.then_inc(s_z, 1)
                    dve.wait_ge(s_sig, k + 1)

                def gates(k, parity):
                    wide = [P, BT, EXPERTS0]
                    for n in range(2):
                        src = score if n == 0 else left
                        chain.step(V.tensor_reduce(best[:], src[:], AX, ALU.max))
                        chain.step(V.tensor_tensor(hit[:], src[:], best[:].unsqueeze(2).to_broadcast(wide), ALU.is_equal))
                        chain.step(V.tensor_tensor(hit[:], hit[:], order[:].unsqueeze(1).to_broadcast(wide), ALU.mult))
                        chain.step(V.tensor_reduce(best[:], hit[:], AX, ALU.max))
                        chain.step(V.tensor_tensor(chosen[:, n], hit[:], best[:].unsqueeze(2).to_broadcast(wide), ALU.is_equal))
                        if n == 0:
                            chain.step(V.scalar_tensor_tensor(left[:], chosen[:, 0], -2.0, score[:], ALU.mult, ALU.add))
                    chain.step(V.tensor_tensor(chosen[:, 0], chosen[:, 0], chosen[:, 1], ALU.add))
                    V.tensor_tensor(gate[:, parity, :, 0:EXPERTS0], chosen[:, 0], score[:], ALU.mult).then_inc(s_gate, 1)
                    assert chain.n == STEPS, chain.n
                    dve.wait_ge(s_gate, k + 1)
                STEPS = 1 + 5 * 2 + 1 + 1

                def sums(k, parity, last, turn):
                    scores(k)
                    gates(k, parity)
                    for e in range(GROUPS0):
                        dve.wait_ge(s_down, GROUPS0 * k + e + 1)
                        if e > 0 or not (isinstance(k, int) and k == 0):
                            dve.wait_ge(s_acc, BT * (GROUPS0 * k + e))
                        if e == EXPERTS0:
                            V.tensor_tensor(acc[:], acc[:], ps_e[e % 2][:], ALU.add).then_inc(s_acc, BT)
                            dve.wait_ge(s_acc, BT * GROUPS0 * (k + 1))
                            to = x_sb[:, bass.ds(k * BT, BT), :]
                            V.tensor_tensor(to, to, acc[:], ALU.add).then_inc(s_x2, 1)
                            dve.wait_ge(s_x2, k + 1)
                            continue
                        for i in range(BT):
                            g = gate[:, parity, i, e:e + 1]
                            if e == 0:
                                ins = V.tensor_scalar(acc[:, i, :], ps_e[0][:, i, :], g, None, ALU.mult)
                            else:
                                ins = V.scalar_tensor_tensor(acc[:, i, :], ps_e[e % 2][:, i, :], g, acc[:, i, :],
                                                             ALU.mult, ALU.add)
                            ins.then_inc(s_acc, 1)
                        if e == 1 and not last:
                            normalize(k + 1, 1 - parity)

                normalize(0, 0)
                rounds(dve, BLOCKS, sums)


def head_attention(nc, io, x_sb, ident):
    EXP_LIMIT = 60.0
    UNITS = GROUPS * KT
    PRING = 4
    LAG = 2
    with ExitStack() as ctx:
        def sb(name, shape, dt=F32):
            return ctx.enter_context(nc.sbuf_tensor("C_" + name, shape, dt))

        def ps(name, shape):
            return ctx.enter_context(nc.psum_tensor("C_" + name, shape, F32))

        def sem(name):
            return ctx.enter_context(nc.semaphore("C_" + name))

        wq = sb("wq", [P, D])
        wk = sb("wk", [P, D])
        wv = sb("wv", [P, D])
        wo = sb("wo", [P, GROUPS, D])
        bqk = sb("bqk", [P, 2])
        bv = sb("bv", [P, D])
        bo = sb("bo", [P, D])
        mask = sb("mask", [P, HG])
        spread_den = sb("spread_den", [P, P])
        head_sum = sb("head_sum", [P, HEADS])
        ones = sb("ones", [P, 1])
        place_m = sb("place_m", [HEADS, GROUPS, P])
        place_m_r = sb("place_m_r", [HEADS, GROUPS, P], F32R)
        place_r = sb("place_r", [P, 2, GROUPS, P], F32R)
        norm = Norm(ctx, nc, "C")
        ctx_t = sb("ctx_t", [P, 2, CTX])
        k_t = sb("k_t", [P, CTX])
        k_hi = sb("k_hi", [P, CTX], F32R)
        k_lo = sb("k_lo", [P, CTX], F32R)
        ends = sb("ends", [P, 4])
        keys = sb("keys", [P, 2, GROUPS, CTXP], F32R)
        values = sb("values", [P, 2, KT, HEADS, VW])
        xn = sb("xn", [P, QT, D])
        xt = sb("xt", [P, QT, P])
        q_t = sb("q_t", [P, SEQ])
        q_hi = sb("q_hi", [P, SEQ], F32R)
        q_lo = sb("q_lo", [P, SEQ], F32R)
        q_bound = sb("q_bound", [P, SEQ])
        queries = sb("queries", [P, 2, GROUPS, HG, SEQ], F32R)
        over = sb("over", [P, 2])
        flag = sb("flag", [1, 2], I32)
        top_part = sb("top_part", [P, QT, HEADS, len(KCH)])
        top_m = sb("top_m", [P, QT, HEADS])
        minus_m = sb("minus_m", [HEADS, SEQ], F32R)
        probs = sb("probs", [P, PRING, HG, SEQ])
        o_t = sb("o_t", [P, GROUPS, SEQ])
        inv = sb("inv", [P, GROUPS, SEQ])

        ps_s = [ps(f"ps_s{i}", [P, HG, SEQ]) for i in range(2)]
        ps_o = [ps(f"ps_o{i}", [P, SEQ]) for i in range(2)]
        ps_p = ps("ps_p", [P, 512])
        ps_f = ps("ps_f", [P, 512])

        s_w = sem("s_w")
        s_const = sem("s_const")
        s_ctx = [sem(f"s_ctx{i}") for i in range(2)]
        s_split = sem("s_split")
        s_placed = [sem(f"s_placed{i}") for i in range(2)]
        s_xn = sem("s_xn")
        s_job = sem("s_job")
        s_job_done = sem("s_job_done")
        s_score = sem("s_score")
        s_exp = sem("s_exp")
        s_av = sem("s_av")
        s_o_read = sem("s_o_read")
        s_fin = sem("s_fin")
        s_fin_read = sem("s_fin_read")
        s_top = sem("s_top")
        s_top_read = sem("s_top_read")
        s_dve = sem("s_dve")
        s_dve_fin = sem("s_dve_fin")
        s_seen_pe = sem("s_seen_pe")
        s_seen_dve = sem("s_seen_dve")

        JOBS = ([("turn", 0), ("query", 0)] + [("key", i) for i in range(len(KCH))]
                + [("value", i) for i in range(0, KT, 4)] + [("place_query", g) for g in range(GROUPS)]
                + [("bound", 0), ("count", 0)])
        NJ = len(JOBS)
        SPLIT_JOB = 2 + len(KCH) - 1
        FIN_AT = {3: 0, 7: 1, 11: 2}
        JOB_AT = {12 + i + (9 if i > SPLIT_JOB else 0): i for i in range(NJ)}
        MAXIMA_AT = max(JOB_AT) + 1
        assert MAXIMA_AT < UNITS
        TOPS = HEADS * QT * len(KCH)
        TOP_FILLS = TOPS + 1 + GROUPS
        TOP_READS = TOPS + 2 + GROUPS

        def top_rounds():
            n = 0
            for h in range(HEADS):
                for qt in range(QT):
                    for i, (at, width) in enumerate(KCH):
                        yield n, h, qt, i, at, width
                        n += 1

        with nc.Block() as block:
            @block.sync
            def _(sp):
                loads = [(wq, "L1_xattn_Wq"), (wk, "L1_xattn_Wk"), (wv, "L1_xattn_Wv"), (wo, "L1_xattn_Wo_strips"),
                         (bqk, "L1_xattn_bqk"), (mask, "head_mask"),
                         (spread_den, "spread_den"), (head_sum, "head_sum"), (place_m, "place_m"), (probs, "place")]
                for to, name in loads:
                    sp.dma_start(to[:] if name != "place" else to[:, 0, :, :].rearrange("p h q -> p (h q)"),
                                 io[name] if name != "place" else io[name].rearrange("p a g r -> p (a g r)")).then_inc(s_w, 16)
                for to, name in ((bv, "bv"), (bo, "bo")):
                    sp.dma_start(to[:], io["L1_xattn_" + name].partition_broadcast(P)).then_inc(s_w, 16)
                for p in range(2):
                    sp.dma_start(ctx_t[:, p, :], io["ctx_t"][p]).then_inc(s_ctx[p], 16)

                def place(p, parity, load):
                    sp.wait_ge(s_split, p + 1)
                    for g in range(GROUPS):
                        for product, part in enumerate((k_hi, k_hi, k_lo)):
                            sp.dma_start(keys[32 * product:32 * product + 32, parity, g, 0:CTX].bitcast(F32),
                                         part[32 * g:32 * g + 32, 0:CTX].bitcast(F32)).then_inc(s_placed[parity], 16)
                    if load:
                        sp.wait_ge(s_job_done, NJ * (p + 1))
                        sp.dma_start(ctx_t[:, parity, :], io["ctx_t"][bass.ds(p + 2, 1)].rearrange(
                            "b p c -> p (b c)")).then_inc(s_ctx[parity], 16)

                place(0, 0, True)
                with sp.Fori(0, (BATCH - 4) // 2) as i:
                    place(2 * i + 1, 1, True)
                    place(2 * i + 2, 0, True)
                place(BATCH - 3, 1, True)
                place(BATCH - 2, 0, False)
                place(BATCH - 1, 1, False)
            W_ALL = 16 * 12

            def loaded(eng, parity, turn):
                eng.wait_ge(s_ctx[parity], 16 * (turn + 1))

            def placed(eng, parity, turn):
                eng.wait_ge(s_placed[parity], 16 * 3 * GROUPS * (turn + 1))

            @block.tensor
            def _(pe):
                T = nc.tensor

                def place_query(parity, g, shifted=False):
                    T.matmul(ps_p[:, 0:SEQ], place_r[:, 0, g, :], q_hi[:], start=True, stop=False)
                    m = T.matmul(ps_p[:, 0:SEQ], place_r[:, 1, g, :], q_lo[:], start=False, stop=not shifted)
                    if shifted:
                        m = T.matmul(ps_p[:, 0:SEQ], place_m_r[:, g, :], minus_m[:], start=False, stop=True)
                    return m

                def job(p, parity, turn, n):
                    kind, arg = JOBS[n]
                    wait(pe, s_job_done, NJ * p + n)
                    if kind == "turn":
                        pe.wait_ge(s_xn, QT * (p + 1))
                        for i in range(QT):
                            m = T.transpose(ps_p[:, i * P:(i + 1) * P], xn[:, i, :], ident[:])
                    elif kind == "query":
                        m = T.matmul(ps_p[:, 0:SEQ], wq[:], xt[:].rearrange("p i t -> p (i t)"), start=True, stop=True)
                    elif kind == "key":
                        if arg == 0:
                            loaded(pe, parity, turn)
                        at, width = KCH[arg]
                        m = T.matmul(ps_p[:, 0:width], wk[:], ctx_t[:, parity, at:at + width], start=True, stop=True)
                    elif kind == "value":
                        for kt in range(arg, min(arg + 4, KT)):
                            rows = min(P, CTX - kt * P)
                            m = T.matmul(ps_p[0:rows, (kt - arg) * D:(kt - arg + 1) * D],
                                         ctx_t[:, parity, kt * P:kt * P + rows], wv[:], start=True, stop=True)
                    elif kind == "place_query":
                        m = place_query(parity, arg)
                    elif kind == "bound":
                        m = T.matmul(ps_p[0:HEADS, 0:SEQ], head_sum[:], q_bound[:], start=True, stop=True)
                    else:
                        m = T.matmul(ps_p[0:1, 0:1], over[:, 1:2], ones[:], start=True, stop=True)
                    m.then_inc(s_job, 1)

                def maxima(p, parity, turn):
                    pe.wait_ge(s_job_done, NJ * (p + 1))
                    pe.sem_inc(s_seen_pe, 1)
                    wide = pe.value_load(flag[0:1, parity:parity + 1], min_val=0, max_val=HEADS)
                    with pe.If(wide > 0):
                        placed(pe, parity, turn)
                        for n, h, qt, i, at, width in top_rounds():
                            wait(pe, s_top_read, TOP_READS * p + n)
                            T.matmul(ps_p[:, 0:width + width % 2],
                                     queries[:, parity, h // HG, h % HG, qt * P:(qt + 1) * P],
                                     keys[:, parity, h // HG, at:at + width + width % 2],
                                     start=True, stop=True).then_inc(s_top, 1)
                        pe.wait_ge(s_top_read, TOP_READS * p + TOPS + 1)
                        for qt in range(QT):
                            m = T.transpose(ps_p[0:HEADS, qt * P:(qt + 1) * P], top_m[:, qt, :], ident[:])
                        m.then_inc(s_top, 1)
                        for g in range(GROUPS):
                            pe.wait_ge(s_top_read, TOP_READS * p + TOPS + 2 + g)
                            place_query(parity, g, True).then_inc(s_top, 1)
                    with pe.Else():
                        pe.sem_inc(s_top, TOP_FILLS)

                def scores(k, parity, n):
                    g, kt = divmod(n, KT)
                    wait(pe, s_exp, UNITS * k + n - 1)
                    for j in range(HG):
                        m = T.matmul(ps_s[n % 2][:, j, :], keys[:, parity, g, kt * P:(kt + 1) * P],
                                     queries[:, parity, g, j, :], start=True, stop=True)
                    m.then_inc(s_score, 1)

                def weigh(k, parity, n):
                    g, kt = divmod(n, KT)
                    pe.wait_ge(s_exp, UNITS * k + n + 1)
                    if kt == 0:
                        wait(pe, s_o_read, GROUPS * k + g - 1)
                    for j in range(HG):
                        m = T.matmul(ps_o[g % 2][32 * j:32 * j + VW, :], values[:, parity, kt, g * HG + j, :],
                                     probs[:, n % PRING, j, :], start=(kt == 0), stop=(kt == KT - 1))
                    m.then_inc(s_av, 1)
                    return m

                def finish(b, step):
                    wait(pe, s_fin_read, 3 * b + step)
                    if step < 2:
                        pe.wait_ge(s_o_read, GROUPS * (b + 1))
                        m = T.matmul(ps_f[:], spread_den[:],
                                     o_t[:, 2 * step:2 * step + 2, :].rearrange("p g q -> p (g q)"), start=True, stop=True)
                    else:
                        for qt in range(QT):
                            for g in range(GROUPS):
                                m = T.matmul(ps_f[:, qt * D:(qt + 1) * D], o_t[:, g, qt * P:(qt + 1) * P], wo[:, g, :],
                                             start=(g == 0), stop=(g == GROUPS - 1))
                    m.then_inc(s_fin, 1)

                def attend(k, parity, last, turn):
                    first = isinstance(k, int) and k == 0
                    for n in range(UNITS):
                        if n == 0:
                            pe.wait_ge(s_job_done, NJ * (k + 1))
                            pe.wait_ge(s_top_read, TOP_READS * (k + 1))
                            placed(pe, parity, turn)
                        scores(k, parity, n)
                        if n >= LAG:
                            weigh(k, parity, n - LAG)
                        elif not first:
                            weigh(k - 1, 1 - parity, UNITS - LAG + n)
                        if n in FIN_AT and not first:
                            finish(k - 1, FIN_AT[n])
                        if n in JOB_AT and not last:
                            job(k + 1, 1 - parity, turn + parity, JOB_AT[n])
                        if n == MAXIMA_AT and not last:
                            maxima(k + 1, 1 - parity, turn + parity)

                pe.wait_ge(s_w, W_ALL)
                pe.wait_ge(s_const, 1)
                for n in range(NJ):
                    job(0, 0, 0, n)
                maxima(0, 0, 0)
                rounds(pe, BATCH, attend)
                for n in range(UNITS - LAG, UNITS):
                    weigh(BATCH - 1, 1, n)
                for step in range(3):
                    finish(BATCH - 1, step)

            @block.scalar
            def _(act):
                norm.root(nc, act)

                def exps(k, parity, last, turn):
                    for n in range(UNITS):
                        act.wait_ge(s_score, UNITS * k + n + 1)
                        wait(act, s_av, UNITS * k + n - PRING + 1)
                        nc.scalar.activation(probs[:, n % PRING, :, :], ps_s[n % 2][:], ACT.Exp,
                                             scale=SCORE_SCALE1).then_inc(s_exp, 1)

                rounds(act, BATCH, exps)

            @block.vector
            def _(dve):
                chain = Chain(dve, s_dve)
                V = nc.vector
                rows = CTX - (KT - 1) * P
                chain.mark(V.memset(keys[:, :, :, CTX:].bitcast(F32), 0.0))
                chain.step(V.memset(keys[SHIFT_ROW:, :, :, 0:CTX].bitcast(F32), 0.0))
                chain.mark(V.memset(keys[SHIFT_ROW:SHIFT_ROW + HG, :, :, 0:CTX].bitcast(F32), 1.0))
                chain.mark(V.memset(values[:], 0.0))
                chain.mark(V.memset(ones[:], 1.0))
                for bank in ps_o:
                    chain.mark(V.memset(bank[:], 0.0))
                chain.settle()
                for parity in range(2):
                    chain.mark(V.memset(values[:, parity, 0:KT - 1, :, DK:], 1.0))
                    chain.mark(V.memset(values[0:rows, parity, KT - 1, :, DK:], 1.0))
                dve.wait_ge(s_w, W_ALL)
                chain.mark(V.tensor_copy(place_m_r[:], place_m[:]))
                chain.step(V.tensor_copy(place_r[:].rearrange("p a g r -> p (a g r)"),
                                         probs[:, 0, :, :].rearrange("p h q -> p (h q)")))
                V.memset(over[:], 0.0).then_inc(s_const, 1)
                dve.wait_ge(s_const, 1)
                norm.statistics(nc, dve, chain, x_sb)
                setup = chain.n

                def place_query(parity, g, sem_):
                    V.tensor_tensor(queries[:, parity, g, :, :],
                                    ps_p[:, 0:SEQ].unsqueeze(1).to_broadcast([P, HG, SEQ]),
                                    mask[:].unsqueeze(2).to_broadcast([P, HG, SEQ]), ALU.mult).then_inc(sem_, 1)

                def job(p, parity, turn, n):
                    kind, arg = JOBS[n]
                    first = isinstance(p, int) and p == 0
                    if kind == "turn":
                        wait(dve, s_job, NJ * (p - 1) + 1)
                        for i in range(QT):
                            norm.apply(nc, x_sb, QT * p + i, xn[:, i, :]).then_inc(s_xn, 1)
                    dve.wait_ge(s_job, NJ * p + n + 1)
                    done = None
                    if kind == "turn":
                        done = V.tensor_copy(xt[:].rearrange("p i t -> p (i t)"), ps_p[:, 0:SEQ])
                    elif kind == "query":
                        chain.step(V.tensor_scalar(q_t[:], ps_p[:, 0:SEQ], bqk[:, 0:1], None, ALU.add))
                        chain.mark(V.tensor_copy(q_hi[:], q_t[:]))
                        chain.step(V.scalar_tensor_tensor(q_bound[:], q_t[:], -1.0, q_t[:], ALU.mult, ALU.max))
                        done = V.tensor_tensor(q_lo[:], q_t[:], q_hi[:].bitcast(F32), ALU.subtract)
                    elif kind == "key":
                        at, width = KCH[arg]
                        evac = V.tensor_scalar(k_t[:, at:at + width], ps_p[:, 0:width], bqk[:, 1:2], None, ALU.add)
                        done = evac
                        if arg == len(KCH) - 1:
                            done = None
                            evac.then_inc(s_job_done, 1)
                            dve.wait_ge(s_job_done, NJ * p + n + 1)
                            k = k_t[:, 0:CTX]
                            chain.mark(V.tensor_reduce(ends[:, 0:1], k, AX, ALU.max))
                            chain.step(V.tensor_reduce(ends[:, 1:2], k, AX, ALU.min))
                            chain.mark(V.tensor_tensor(ends[:, 2:3], ends[:, 0:1], ends[:, 1:2], ALU.add))
                            chain.step(V.tensor_tensor(ends[:, 3:4], ends[:, 0:1], ends[:, 1:2], ALU.subtract))
                            chain.step(V.tensor_scalar(ends[:, 2:4], ends[:, 2:4], 0.5, None, ALU.mult))
                            chain.mark(V.tensor_scalar(q_bound[:], q_bound[:], ends[:, 3:4], None, ALU.mult))
                            chain.step(V.tensor_scalar(k, k, ends[:, 2:3], None, ALU.subtract))
                            if not first:
                                placed(dve, 1 - parity, turn - 1 + parity)
                            chain.step(V.tensor_copy(k_hi[:, 0:CTX], k))
                            V.tensor_tensor(k_lo[:, 0:CTX], k, k_hi[:, 0:CTX].bitcast(F32),
                                            ALU.subtract).then_inc(s_split, 1)
                    elif kind == "value":
                        n_kt = min(arg + 4, KT) - arg
                        r = P if n_kt == 4 else rows
                        done = V.tensor_tensor(
                            values[0:r, parity, arg:arg + n_kt, :, 0:DK],
                            ps_p[0:r, 0:n_kt * D].rearrange("p (k h d) -> p k h d", k=n_kt, h=HEADS),
                            bv[0:r, :].rearrange("p (h d) -> p h d", h=HEADS).unsqueeze(1).to_broadcast([r, n_kt, HEADS, DK]),
                            ALU.add)
                    elif kind == "place_query":
                        place_query(parity, arg, s_job_done)
                    elif kind == "bound":
                        chain.step(V.tensor_reduce(over[0:HEADS, 0:1], ps_p[0:HEADS, 0:SEQ], AX, ALU.max))
                        done = V.tensor_scalar(over[0:HEADS, 1:2], over[0:HEADS, 0:1], EXP_LIMIT / SCORE_SCALE1, None, ALU.is_gt)
                    else:
                        done = V.tensor_copy(flag[0:1, parity:parity + 1], ps_p[0:1, 0:1])
                    if done is not None:
                        done.then_inc(s_job_done, 1)
                JOB_STEPS = 3 + 8 + 1

                def prepare(p, parity, turn, n):
                    if n == 0:
                        chain.at(setup + JOB_STEPS * p)
                    job(p, parity, turn, n)
                    if n == NJ - 1:
                        assert chain.n == JOB_STEPS, chain.n

                def maxima(p, parity):
                    dve.wait_ge(s_job_done, NJ * (p + 1))
                    dve.sem_inc(s_seen_dve, 1)
                    wide = dve.value_load(flag[0:1, parity:parity + 1], min_val=0, max_val=HEADS)
                    with dve.If(wide > 0):
                        for n, h, qt, i, at, width in top_rounds():
                            dve.wait_ge(s_top, TOP_FILLS * p + n + 1)
                            V.tensor_reduce(top_part[:, qt, h, i:i + 1], ps_p[:, 0:width], AX,
                                            ALU.max).then_inc(s_top_read, 1)
                        dve.wait_ge(s_top_read, TOP_READS * p + TOPS)
                        V.tensor_reduce(top_m[:], top_part[:], AX, ALU.max, negate=True).then_inc(s_top_read, 1)
                        dve.wait_ge(s_top, TOP_FILLS * p + TOPS + 1)
                        V.tensor_copy(minus_m[:], ps_p[0:HEADS, 0:SEQ]).then_inc(s_top_read, 1)
                        for g in range(GROUPS):
                            dve.wait_ge(s_top, TOP_FILLS * p + TOPS + 2 + g)
                            place_query(parity, g, s_top_read)
                    with dve.Else():
                        dve.sem_inc(s_top_read, TOP_READS)

                def take_o(b, g):
                    dve.wait_ge(s_av, UNITS * b + KT * (g + 1))
                    V.tensor_copy(o_t[:, g, :], ps_o[g % 2][:]).then_inc(s_o_read, 1)

                def finish(b, step):
                    dve.wait_ge(s_fin, 3 * b + step + 1)
                    if step < 2:
                        half = slice(2 * step, 2 * step + 2)
                        fin.step(V.reciprocal(inv[:, half, :].rearrange("p g q -> p (g q)"), ps_f[:]))
                        V.tensor_tensor(o_t[:, half, :], o_t[:, half, :], inv[:, half, :],
                                        ALU.mult).then_inc(s_fin_read, 1)
                    else:
                        to = x_sb[:, bass.ds(QT * b, QT), :]
                        fin.step(V.tensor_tensor(to, to, ps_f[:].rearrange("p (i d) -> p i d", i=BT)[:, 0:QT, :], ALU.add))
                        V.tensor_tensor(to, to, bo[:].unsqueeze(1).to_broadcast([P, QT, D]),
                                        ALU.add).then_inc(s_fin_read, 1)
                fin = Chain(dve, s_dve_fin)

                def attend(k, parity, last, turn):
                    first = isinstance(k, int) and k == 0
                    for n in range(UNITS):
                        if n > LAG and n % KT == LAG - 1:
                            take_o(k, n // KT - 1)
                        elif n == LAG - 1 and not first:
                            take_o(k - 1, GROUPS - 1)
                        if n in FIN_AT and not first:
                            fin.at(3 * (k - 1) + FIN_AT[n])
                            finish(k - 1, FIN_AT[n])
                        if n in JOB_AT and not last:
                            prepare(k + 1, 1 - parity, turn + parity, JOB_AT[n])
                        if n == MAXIMA_AT and not last:
                            maxima(k + 1, 1 - parity)

                for n in range(NJ):
                    prepare(0, 0, 0, n)
                maxima(0, 0)
                rounds(dve, BATCH, attend)
                take_o(BATCH - 1, GROUPS - 1)
                for step in range(3):
                    fin.at(3 * (BATCH - 1) + step)
                    finish(BATCH - 1, step)
                dve.wait_ge(s_fin_read, 3 * BATCH)


def head_experts(nc, io, x_sb, ident, out_rows):
    with ExitStack() as ctx:
        def sb(name, shape, dt=F32):
            return ctx.enter_context(nc.sbuf_tensor("D_" + name, shape, dt))

        def ps(name, shape):
            return ctx.enter_context(nc.psum_tensor("D_" + name, shape, F32))

        def sem(name):
            return ctx.enter_context(nc.semaphore("D_" + name))

        EG = 2
        QUADS = HP * EG
        UNITS = QUADS * 4
        RING = 8
        CHOICES = [P, BT * H1, E1]

        wm = sb("wm", [P, D])
        bm = sb("bm", [P, 1])
        emb = sb("emb", [P, P])
        w_up = sb("w_up", [P, 2, PAIRS, P])
        w_up_r = sb("w_up_r", [P, 2, PAIRS, P], F32R)
        part = sb("part", [P, 2])
        b_up = sb("b_up", [P, PAIRS])
        w_down = sb("w_down", [P, PAIRS, 32])
        b_down = sb("b_down", [P, EG])
        wo = sb("wo", [P, H1, D])
        bo = sb("bo", [P, D])
        order = sb("order", [P, E1])
        place_t = sb("place_t", [P, 2, HP, P], F32R)
        place_g = sb("place_g", [P, H1, EG, P], F32R)
        norm = Norm(ctx, nc, "D")
        xn = sb("xn", [P, BT, D])
        xt = sb("xt", [P, BLOCK])
        h_t = sb("h_t", [P, BLOCK])
        h_hi = sb("h_hi", [P, BLOCK], F32R)
        h_lo = sb("h_lo", [P, BLOCK], F32R)
        up_in = sb("up_in", [P, 2, HP, BLOCK], F32R)
        weight = sb("weight", CHOICES)
        left = sb("left", CHOICES)
        hit = sb("hit", CHOICES)
        chosen = sb("chosen", [P, 2] + CHOICES[1:])
        best = sb("best", CHOICES[:2])
        total = sb("total", CHOICES[:2])
        gate_hi = sb("gate_hi", [P, BLOCK], F32R)
        gate_lo = sb("gate_lo", [P, BLOCK], F32R)
        gate = sb("gate", [P, 2, H1, EG, BLOCK])
        hidden = sb("hidden", [P, RING, 2, BLOCK])
        gated = sb("gated", [P, 2, 2, BLOCK])

        ps_p = ps("ps_p", [P, BLOCK])
        ps_u = [ps(f"ps_u{i}", [P, 2, BLOCK]) for i in range(2)]
        ps_e = [ps(f"ps_e{i}", [P, BLOCK]) for i in range(2)]
        ps_o = ps("ps_o", [P, BT, D])

        s_w = sem("s_w")
        s_const = sem("s_const")
        s_xn = sem("s_xn")
        s_job = sem("s_job")
        s_job_done = sem("s_job_done")
        s_shifted = sem("s_shifted")
        s_exp = sem("s_exp")
        s_up = sem("s_up")
        s_hid = sem("s_hid")
        s_down = sem("s_down")
        s_gated = sem("s_gated")
        s_wo = sem("s_wo")
        s_x4 = sem("s_x4")
        s_dve = sem("s_dve")
        s_dve_x = sem("s_dve_x")
        s_out = sem("s_out")

        JOBS = ([("turn", 0), ("project", 0)] + [("place_up", i) for i in range(HP)] + [("logit", 0), ("turn_gate", 0)]
                + [("place_gate", (h, eg)) for h in range(H1) for eg in range(EG)])
        NJ = len(JOBS)
        GATE_JOB = 7
        JOB_AT = {i + (7 if i >= GATE_JOB else 0): i for i in range(NJ)}
        assert max(JOB_AT) < UNITS
        EXP_AT = 9
        DOWN_AT = {(4 * (v + 1) + 1) % UNITS: v for v in range(QUADS)}
        OUT_AT = {(4 * (v + 1) + 3) % UNITS: v for v in range(QUADS)}
        X_AT = 4

        with nc.Block() as block:
            @block.sync
            def _(sp):
                for to, name in ((wm, "Wm"), (bm, "bm"), (emb, "emb"), (w_up, "w_up"), (b_up, "b_up"), (part, "part"),
                                 (w_down, "w_down"), (b_down, "b_down"), (wo, "wo")):
                    sp.dma_start(to[:], io["L1_ffn_" + name]).then_inc(s_w, 16)
                sp.dma_start(bo[:], io["L1_ffn_bo"].partition_broadcast(P)).then_inc(s_w, 16)
                sp.dma_start(order[:], io["order1"].partition_broadcast(P)).then_inc(s_w, 16)
                sp.dma_start(hidden[:, 0, :, :].rearrange("p a b -> p (a b)"),
                             io["place_t"].rearrange("p a b c -> p (a b c)")).then_inc(s_w, 16)
                sp.dma_start(hidden[:, 1:3, :, :].rearrange("p a b c -> p (a b c)"),
                             io["place_g"].rearrange("p a b c -> p (a b c)")).then_inc(s_w, 16)
                with sp.Fori(0, BLOCKS) as k:
                    sp.wait_ge(s_x4, k + 1)
                    sp.dma_start(out_rows[:, bass.ds(k * BT, BT), :],
                                 x_sb[:, bass.ds(k * BT, BT), :]).then_inc(s_out, 16)
                sp.wait_ge(s_out, 16 * BLOCKS)
            W_ALL = 16 * 13

            @block.tensor
            def _(pe):
                T = nc.tensor

                def job(p, parity, n):
                    kind, arg = JOBS[n]
                    wait(pe, s_job_done, NJ * p + n)
                    if kind == "turn":
                        pe.wait_ge(s_xn, BT * (p + 1))
                        for i in range(BT):
                            m = T.transpose(ps_p[:, i * P:(i + 1) * P], xn[:, i, :], ident[:])
                    elif kind == "project":
                        m = T.matmul(ps_p[:], wm[:], xt[:], start=True, stop=True)
                    elif kind == "place_up":
                        T.matmul(ps_p[:], place_t[:, 0, arg, :], h_hi[:], start=True, stop=False)
                        m = T.matmul(ps_p[:], place_t[:, 1, arg, :], h_lo[:], start=False, stop=True)
                    elif kind == "logit":
                        for i in range(BT):
                            m = T.matmul(ps_p[:, i * P:(i + 1) * P], h_t[:, i * P:(i + 1) * P], emb[:],
                                         start=True, stop=True)
                    elif kind == "turn_gate":
                        for i in range(BT):
                            m = T.transpose(ps_p[:, i * P:(i + 1) * P],
                                            weight[:, i * H1:(i + 1) * H1, :].rearrange("p h e -> p (h e)"), ident[:])
                    else:
                        h, eg = arg
                        T.matmul(ps_p[:], place_g[:, h, eg, :], gate_hi[:], start=True, stop=False)
                        m = T.matmul(ps_p[:], place_g[:, h, eg, :], gate_lo[:], start=False, stop=True)
                    m.then_inc(s_job, 1)

                def up(k, parity, u):
                    hp, pair = divmod(u, PAIRS)
                    wait(pe, s_hid, UNITS * k + u - 1)
                    for s in range(2):
                        m = T.matmul(ps_u[u % 2][:, s, :], w_up_r[:, s, pair, :], up_in[:, parity, hp, :],
                                     start=True, stop=True)
                    m.then_inc(s_up, 1)

                def down(k, v):
                    pe.wait_ge(s_hid, UNITS * k + 4 * v + 4)
                    wait(pe, s_gated, QUADS * k + v)
                    for s in range(2):
                        for i in range(4):
                            m = T.matmul(ps_e[s][32 * i:32 * i + 32, :], w_down[:, v % EG * 4 + i, :],
                                         hidden[:, (4 * v + i) % RING, s, :], start=True, stop=True)
                    m.then_inc(s_down, 1)

                def out(k, v):
                    pe.wait_ge(s_gated, QUADS * k + v + 1)
                    if v == 0:
                        wait(pe, s_x4, k)
                    for s in range(2):
                        for i in range(BT):
                            m = T.matmul(ps_o[:, i, :], gated[:, v % 2, s, i * P:(i + 1) * P], wo[:, v // EG * 2 + s, :],
                                         start=(v == 0 and s == 0 and i == 0), stop=(v == QUADS - 1 and s == 1),
                                         skip_group_check=True)
                    m.then_inc(s_wo, 1)

                def experts(k, parity, last, turn):
                    first = isinstance(k, int) and k == 0
                    pe.wait_ge(s_job_done, NJ * (k + 1))
                    for u in range(UNITS):
                        up(k, parity, u)
                        for table, visit in ((DOWN_AT, down), (OUT_AT, out)):
                            if u in table:
                                v = table[u]
                                if v < QUADS - 1:
                                    visit(k, v)
                                elif not first:
                                    visit(k - 1, v)
                        if u in JOB_AT and not last:
                            job(k + 1, 1 - parity, JOB_AT[u])

                pe.wait_ge(s_w, W_ALL)
                pe.wait_ge(s_const, 1)
                for n in range(NJ):
                    job(0, 0, n)
                rounds(pe, BLOCKS, experts)
                down(BLOCKS - 1, QUADS - 1)
                out(BLOCKS - 1, QUADS - 1)

            @block.scalar
            def _(act):
                norm.root(nc, act)

                def exponent(p):
                    act.wait_ge(s_shifted, p + 1)
                    nc.scalar.activation(weight[:], weight[:], ACT.Exp).then_inc(s_exp, 1)

                def gelus(k, parity, last, turn):
                    for u in range(UNITS):
                        act.wait_ge(s_up, UNITS * k + u + 1)
                        wait(act, s_down, QUADS * k + u // 4 - 1)
                        nc.scalar.activation(hidden[:, u % RING, :, :], ps_u[u % 2][:], ACT.Gelu,
                                             bias=b_up[:, u % PAIRS:u % PAIRS + 1]).then_inc(s_hid, 1)
                        if u == EXP_AT and not last:
                            exponent(k + 1)

                exponent(0)
                rounds(act, BLOCKS, gelus)

            @block.vector
            def _(dve):
                chain = Chain(dve, s_dve)
                V = nc.vector
                dve.wait_ge(s_w, W_ALL)
                chain.mark(V.tensor_copy(place_t[:].rearrange("p a b c -> p (a b c)"),
                                         hidden[:, 0, :, :].rearrange("p a b -> p (a b)")))
                chain.mark(V.tensor_copy(place_g[:].rearrange("p a b c -> p (a b c)"),
                                         hidden[:, 1:3, :, :].rearrange("p a b c -> p (a b c)")))
                lo_part = hidden[:, 3:5, :, :].rearrange("p a b c -> p (a b c)")
                flat = w_up[:].rearrange("p s e i -> p (s e i)")
                hi_part = w_up_r[:].rearrange("p s e i -> p (s e i)")
                chain.step(V.tensor_copy(hi_part, flat))
                chain.step(V.tensor_tensor(lo_part, flat, hi_part.bitcast(F32), ALU.subtract))
                chain.step(V.tensor_scalar(lo_part, lo_part, part[:, 1:2], None, ALU.mult))
                V.scalar_tensor_tensor(hi_part, hi_part.bitcast(F32), part[:, 0:1], lo_part, ALU.mult,
                                       ALU.add).then_inc(s_const, 1)
                dve.wait_ge(s_const, 1)
                norm.statistics(nc, dve, chain, x_sb)
                setup = chain.n

                def bc(small):
                    return small.unsqueeze(2).to_broadcast(CHOICES)

                def job(p, parity, n):
                    kind, arg = JOBS[n]
                    if kind == "turn":
                        wait(dve, s_job, NJ * (p - 1) + 1)
                        for i in range(BT):
                            norm.apply(nc, x_sb, BT * p + i, xn[:, i, :]).then_inc(s_xn, 1)
                    dve.wait_ge(s_job, NJ * p + n + 1)
                    if kind == "turn":
                        done = V.tensor_copy(xt[:], ps_p[:])
                    elif kind == "project":
                        chain.step(V.tensor_scalar(h_t[:], ps_p[:], bm[:], None, ALU.add))
                        chain.step(V.tensor_copy(h_hi[:], h_t[:]))
                        done = V.tensor_tensor(h_lo[:], h_t[:], h_hi[:].bitcast(F32), ALU.subtract)
                    elif kind == "place_up":
                        done = V.tensor_copy(up_in[:, parity, arg, :], ps_p[:])
                    elif kind == "logit":
                        logits = ps_p[:].rearrange("p (a e) -> p a e", e=E1)
                        chain.step(V.tensor_reduce(best[:], logits, AX, ALU.max))
                        V.tensor_tensor(weight[:], logits, bc(best[:]), ALU.subtract).then_inc(s_shifted, 1)
                        dve.wait_ge(s_exp, p + 1)
                        chain.step(V.tensor_reduce(total[:], weight[:], AX, ALU.add))
                        chain.step(V.reciprocal(total[:], total[:]))
                        chain.step(V.tensor_tensor(weight[:], weight[:], bc(total[:]), ALU.mult))
                        wide_order = order[:].unsqueeze(1).to_broadcast(CHOICES)
                        for r in range(2):
                            src = weight if r == 0 else left
                            chain.step(V.tensor_reduce(best[:], src[:], AX, ALU.max))
                            chain.step(V.tensor_tensor(hit[:], src[:], bc(best[:]), ALU.is_equal))
                            chain.step(V.tensor_tensor(hit[:], hit[:], wide_order, ALU.mult))
                            chain.step(V.tensor_reduce(best[:], hit[:], AX, ALU.max))
                            chain.step(V.tensor_tensor(chosen[:, r], hit[:], bc(best[:]), ALU.is_equal))
                            if r == 0:
                                chain.step(V.scalar_tensor_tensor(left[:], chosen[:, 0], -2.0, weight[:], ALU.mult,
                                                                  ALU.add))
                        chain.step(V.tensor_tensor(chosen[:, 0], chosen[:, 0], chosen[:, 1], ALU.add))
                        done = V.tensor_tensor(weight[:], weight[:], chosen[:, 0], ALU.mult)
                    elif kind == "turn_gate":
                        chain.step(V.tensor_copy(gate_hi[:], ps_p[:]))
                        done = V.tensor_tensor(gate_lo[:], ps_p[:], gate_hi[:].bitcast(F32), ALU.subtract)
                    else:
                        done = V.tensor_copy(gate[:, parity, arg[0], arg[1], :], ps_p[:])
                    done.then_inc(s_job_done, 1)
                JOB_STEPS = 2 + 4 + 11 + 1 + 1

                def prepare(p, parity, n):
                    if n == 0:
                        chain.at(setup + JOB_STEPS * p)
                    job(p, parity, n)
                    if n == NJ - 1:
                        assert chain.n == JOB_STEPS, chain.n

                def gating(k, parity, v):
                    dve.wait_ge(s_down, QUADS * k + v + 1)
                    wait(dve, s_wo, QUADS * k + v - 1)
                    for s in range(2):
                        ins = V.scalar_tensor_tensor(gated[:, v % 2, s, :], ps_e[s][:], b_down[:, v % EG:v % EG + 1],
                                                     gate[:, parity, v // EG * 2 + s, v % EG, :], ALU.add, ALU.mult)
                    ins.then_inc(s_gated, 1)

                def add_to_stream(k):
                    dve.wait_ge(s_wo, QUADS * (k + 1))
                    to = x_sb[:, bass.ds(BT * k, BT), :]
                    V.tensor_tensor(to, to, ps_o[:], ALU.add).then_inc(s_dve_x, 1)
                    dve.wait_ge(s_dve_x, k + 1)
                    V.tensor_tensor(to, to, bo[:].unsqueeze(1).to_broadcast([P, BT, D]), ALU.add).then_inc(s_x4, 1)

                def experts(k, parity, last, turn):
                    first = isinstance(k, int) and k == 0
                    for u in range(UNITS):
                        if u in DOWN_AT:
                            v = DOWN_AT[u]
                            if v < QUADS - 1:
                                gating(k, parity, v)
                            elif not first:
                                gating(k - 1, 1 - parity, v)
                        if u == X_AT and not first:
                            add_to_stream(k - 1)
                        if u in JOB_AT and not last:
                            prepare(k + 1, 1 - parity, JOB_AT[u])

                for n in range(NJ):
                    prepare(0, 0, n)
                rounds(dve, BLOCKS, experts)
                gating(BLOCKS - 1, 1, QUADS - 1)
                add_to_stream(BLOCKS - 1)


_OUT = "out"


def kernel(**inputs):
    import concourse.bacc as bacc
    from concourse.bass_utils import run_bass_kernel_spmd

    arrays, shape = lay_out(inputs)
    nc = bacc.Bacc("TRN2", target_bir_lowering=False, num_devices=1)
    io = {n: nc.dram_tensor(n + "_dram", a.shape, mybir.dt.from_np(a.dtype), kind="ExternalInput").ap()
          for n, a in arrays.items()}
    io[_OUT] = nc.dram_tensor("out_dram", (TOKENS, D), F32, kind="ExternalOutput").ap()
    program(nc, io)
    r = run_bass_kernel_spmd(nc, [{n + "_dram": a for n, a in arrays.items()}], core_ids=[0])
    return r.results[0]["out_dram"].reshape(shape)


def lay_out(inputs):
    c = np.ascontiguousarray
    x = np.asarray(inputs["x"])
    a = {"x": c(x.reshape(TOKENS, D))}
    ctx = np.asarray(inputs["ctx_1024"])
    a["ctx"] = c(ctx.reshape(BATCH * CTX, D))
    a["pointers"] = c(np.asarray(inputs["itok_BxS_0_4092"]).reshape(TILES, P).T)
    a["ids"] = c(np.asarray(inputs["itok_BxS_0_7"]).reshape(TOKENS))
    a["positions"] = np.arange(IDS, dtype=np.float32)
    a["identity"] = np.eye(P, dtype=np.float32)
    for n in ("Wqj", "Wkj", "Wvj", "Wqi", "Wki", "Wvi"):
        a["L0_xattn_" + n] = c(np.asarray(inputs["L0_xattn_" + n]))
    a["L0_xattn_WoutT"] = c(np.asarray(inputs["L0_xattn_Wout"]).T)
    a["L0_xattn_gain"] = c(np.asarray(inputs["L0_xattn_gain"]).reshape(1))
    a["L0_xattn_council_weights"] = c(np.asarray(inputs["L0_xattn_council_weights"]))

    def get(name):
        return np.asarray(inputs[name])

    a["L0_ffn_w_up"] = c(np.concatenate([get("L0_ffn_W1"), get("L0_ffn_Ws1")[None]]).transpose(2, 0, 1))
    down = np.concatenate([get("L0_ffn_W2"), get("L0_ffn_Ws2")[None]])
    a["L0_ffn_w_down"] = c(down.reshape(GROUPS0, D, CH, P).transpose(3, 0, 2, 1))
    a["L0_ffn_b_up"] = c(np.concatenate([get("L0_ffn_b1"), get("L0_ffn_bs1")[None]]).reshape(GROUPS0 * CH, P).T)
    a["L0_ffn_b_down"] = c(np.concatenate([get("L0_ffn_b2"), get("L0_ffn_bs2")[None]]))
    a["L0_ffn_WgT"] = c(get("L0_ffn_Wg").T)
    a["L0_ffn_bg"], a["L0_ffn_bias"] = c(get("L0_ffn_bg")), c(get("L0_ffn_bias"))
    a["order0"] = np.arange(EXPERTS0, 0, -1, dtype=np.float32)

    ctx = ctx.reshape(BATCH, CTX, D)
    a["ctx_t"] = c(ctx.transpose(0, 2, 1))
    for n in ("Wq", "Wk", "Wv"):
        a["L1_xattn_" + n] = c(get("L1_xattn_" + n))
    a["L1_xattn_bqk"] = c(np.stack([get("L1_xattn_bq"), get("L1_xattn_bk")], axis=1))
    a["L1_xattn_bv"], a["L1_xattn_bo"] = c(get("L1_xattn_bv")), c(get("L1_xattn_bo"))
    strips = np.zeros((HG, 32, GROUPS, D), np.float32)
    strips[:, 0:DK] = get("L1_xattn_Wo").reshape(GROUPS, HG, DK, D).transpose(1, 2, 0, 3)
    a["L1_xattn_Wo_strips"] = strips.reshape(P, GROUPS, D)
    mask = np.zeros((P, HG), np.float32)
    den = np.zeros((P, P), np.float32)
    place = np.zeros((P, 2, GROUPS, P), np.float32)
    place_m = np.zeros((HEADS, GROUPS, P), np.float32)
    for h in range(HEADS):
        g, j = divmod(h, HG)
        den[32 * j + DK, 32 * j:32 * j + 32] = 1
        place_m[h, g, SHIFT_ROW + j] = 1
        mask[SHIFT_ROW + j, j] = 1
        for d in range(DK):
            for product, part in enumerate((0, 1, 0)):
                row = 32 * product + DK * j + d
                place[h * DK + d, part, g, row] = 1
                mask[row, j] = 1
    a["head_mask"] = mask
    a["spread_den"], a["place"], a["place_m"] = den, place, place_m
    a["head_sum"] = np.repeat(np.eye(HEADS, dtype=np.float32), DK, axis=0)

    blank = np.zeros
    f = np.float32
    a["L1_ffn_Wm"], a["L1_ffn_bm"] = c(get("L1_ffn_Wm")), c(get("L1_ffn_bm")[:, None])
    emb, emb_bd = get("L1_ffn_expert_emb"), blank((H1, HD1, H1, E1), f)
    w1, w_up = get("L1_ffn_W1").reshape(PAIRS, 2, HD1, I1), blank((2, 4, HD1, 2, PAIRS, 2, I1), f)
    w2, w_down = get("L1_ffn_W2").reshape(PAIRS, 2, I1, HD1), blank((2, I1, PAIRS, 2, HD1), f)
    place_t, place_g = blank((H1, HD1, 2, HP, 2, 4, HD1), f), blank((H1, E1, H1, 2, E1 // 2, HD1), f)
    for h in range(H1):
        emb_bd[h, :, h] = emb
        for d in range(HD1):
            for product in range(4):
                place_t[h, d, product % 2, h // 2, h % 2, product, d] = 1
        for e in range(E1):
            place_g[h, e, h, e // 8, e % 8, :] = 1
    for s in range(2):
        for product in range(4):
            w_up[s, product, :, s] = w1.transpose(2, 0, 1, 3)
        w_down[s, :, :, s] = w2[:, s].transpose(1, 0, 2)
    a["L1_ffn_emb"] = emb_bd.reshape(P, P)
    a["L1_ffn_w_up"] = w_up.reshape(P, 2, PAIRS, P)
    a["L1_ffn_w_down"] = w_down.reshape(P, PAIRS, 32)
    a["place_t"], a["place_g"] = place_t.reshape(P, 2, HP, P), place_g.reshape(P, H1, 2, P)
    low = np.tile(np.repeat(np.array([0, 0, 1, 1], f), HD1), 2)
    a["L1_ffn_part"] = c(np.stack([1 - low, low], axis=1))
    a["L1_ffn_b_up"] = c(get("L1_ffn_b1").reshape(PAIRS, P).T)
    a["L1_ffn_b_down"] = c(get("L1_ffn_b2").reshape(2, P).T)
    a["L1_ffn_wo"] = c(np.tile(get("L1_ffn_Wo").reshape(H1, HD1, D).transpose(1, 0, 2), (8, 1, 1)))
    a["L1_ffn_bo"] = c(get("L1_ffn_bo"))
    a["order1"] = np.arange(E1, 0, -1, dtype=np.float32)
    return a, x.shape
```

```python
from contextlib import ExitStack

import numpy as np
import concourse.bass as bass
from concourse import mybir

F32 = mybir.dt.float32
F32R = mybir.dt.float32r
I32 = mybir.dt.int32
ALU = mybir.AluOpType
ACT = mybir.ActivationFunctionType
AX = mybir.AxisListType.X

P = 128
BATCH, SEQ, D = 16, 256, 128
CTX = 1601
TOKENS = BATCH * SEQ
TILES = TOKENS // P
BT = 4
BLOCK = BT * P
BLOCKS = TILES // BT
EPS = 1e-5

WIN = 3
IDS = 256
SCORE_SCALE0 = 1.0 / float(np.sqrt(float(D)))

EXPERTS0, HID0 = 8, 4 * D
GROUPS0 = EXPERTS0 + 1
CH = HID0 // P

HEADS, DK = 16, 8
HG = 4
GROUPS = HEADS // HG
KT = -(-CTX // P)
CTXP = KT * P
QT = SEQ // P
SCORE_SCALE1 = 1.0 / float(np.sqrt(DK))
SHIFT_ROW = 96
KCH = [(i, min(512, CTX - i)) for i in range(0, CTX, 512)]

H1, E1, HD1, I1 = 8, 16, 16, 64
PAIRS = E1 // 2
HP = H1 // 2


class Chain:

    def __init__(self, eng, sem):
        self.eng, self.sem, self.base, self.n = eng, sem, 0, 0

    def mark(self, ins):
        ins.then_inc(self.sem, 1)
        self.n += 1
        return ins

    def settle(self):
        self.eng.wait_ge(self.sem, self.base + self.n)

    def step(self, ins):
        self.mark(ins)
        self.settle()
        return ins

    def at(self, base):
        self.base, self.n = base, 0


def wait(eng, sem, value, k=0, ring=0):
    if isinstance(value, int) and value <= 0:
        return
    eng.wait_ge(sem, value)


def rounds(eng, count, body):
    body(0, 0, False, 0)
    with eng.Fori(0, (count - 2) // 2) as i:
        body(2 * i + 1, 1, False, i)
        body(2 * i + 2, 0, False, i + 1)
    body(count - 1, 1, True, (count - 2) // 2)


def program(nc, io, phases="ABCD"):
    with ExitStack() as top:
        x_sb = top.enter_context(nc.sbuf_tensor("x_sb", [P, TILES, D], F32))
        ident = top.enter_context(nc.sbuf_tensor("ident", [P, P], F32))
        w1t = top.enter_context(nc.sbuf_tensor("w1t", [P, GROUPS0 * HID0], F32)) if 0 else None
        loaded = top.enter_context(nc.semaphore("loaded"))
        x_rows = io["x"].rearrange("(t p) d -> p t d", p=P)
        out_rows = io["out"].rearrange("(t p) d -> p t d", p=P)
        if "A" not in phases:
            with nc.Block() as block:
                @block.sync
                def _(sp):
                    sp.dma_start(x_sb[:], x_rows).then_inc(loaded, 16)
                    sp.dma_start(ident[:], io["identity"]).then_inc(loaded, 16)
                    sp.wait_ge(loaded, 32)
        if "A" in phases:
            gather_attention(nc, io, x_sb, ident, x_rows, loaded)
        if "B" in phases:
            expert_layer(nc, io, x_sb, ident)
        if "C" in phases:
            head_attention(nc, io, x_sb, ident)
        if "D" in phases:
            head_experts(nc, io, x_sb, ident, out_rows)
            return
        stored = top.enter_context(nc.semaphore("stored"))
        with nc.Block() as block:
            @block.sync
            def _(sp):
                sp.dma_start(out_rows, x_sb[:]).then_inc(stored, 16)
                sp.wait_ge(stored, 16)


class Norm:

    def __init__(self, ctx, nc, tag):
        def sb(name, shape):
            return ctx.enter_context(nc.sbuf_tensor(f"{tag}_{name}", shape, F32))
        self.stats = sb("stats", [P, TILES, 6])
        self.mean = sb("mean", [P, TILES])
        self.var = sb("var", [P, TILES])
        self.std = sb("std", [P, TILES])
        self.tmp = sb("tmp", [P, TILES])
        self.rstd = sb("rstd", [P, TILES])
        self.var_ready = ctx.enter_context(nc.semaphore(f"{tag}_var_ready"))
        self.std_ready = ctx.enter_context(nc.semaphore(f"{tag}_std_ready"))

    def statistics(self, nc, dve, chain, x_sb):
        for t in range(TILES):
            chain.mark(nc.vector.bn_stats(self.stats[:, t, :], x_sb[:, t, :]))
        chain.settle()
        st = self.stats
        chain.mark(nc.vector.tensor_tensor(self.mean[:], st[:, :, 1], st[:, :, 4], ALU.add))
        chain.mark(nc.vector.tensor_tensor(self.tmp[:], st[:, :, 1], st[:, :, 4], ALU.subtract))
        chain.step(nc.vector.tensor_tensor(self.var[:], st[:, :, 2], st[:, :, 5], ALU.add))
        chain.mark(nc.vector.tensor_scalar(self.mean[:], self.mean[:], 0.5, None, ALU.mult))
        chain.mark(nc.vector.tensor_scalar(self.var[:], self.var[:], 1.0 / D, EPS, ALU.mult, ALU.add))
        chain.step(nc.vector.scalar_tensor_tensor(self.tmp[:], self.tmp[:], 0.25, self.tmp[:], ALU.mult, ALU.mult))
        chain.step(nc.vector.tensor_tensor(self.var[:], self.var[:], self.tmp[:], ALU.add))
        nc.vector.tensor_scalar(self.tmp[:], self.var[:], -0.5, None, ALU.mult).then_inc(self.var_ready, 1)
        dve.wait_ge(self.std_ready, 1)
        dve.wait_ge(self.var_ready, 1)
        chain.step(nc.vector.reciprocal(self.rstd[:], self.std[:]))
        chain.step(nc.vector.tensor_tensor(self.std[:], self.rstd[:], self.rstd[:], ALU.mult))
        chain.step(nc.vector.tensor_tensor(self.std[:], self.std[:], self.tmp[:], ALU.mult))
        chain.step(nc.vector.scalar_tensor_tensor(self.rstd[:], self.std[:], 1.5, self.rstd[:], ALU.add, ALU.mult))

    def root(self, nc, act):
        act.wait_ge(self.var_ready, 1)
        nc.scalar.activation(self.std[:], self.var[:], ACT.Sqrt).then_inc(self.std_ready, 1)

    def apply(self, nc, x_sb, t, out):
        return nc.vector.tensor_scalar(out, x_sb[:, bass.ds(t, 1), :].rearrange("p a d -> p (a d)"),
                                       self.mean[:, bass.ds(t, 1)], self.rstd[:, bass.ds(t, 1)],
                                       ALU.subtract, ALU.mult)


def gather_attention(nc, io, x_sb, ident, x_rows, loaded):
    with ExitStack() as ctx:
        def sb(name, shape, dt=F32):
            return ctx.enter_context(nc.sbuf_tensor("A_" + name, shape, dt))

        def ps(name, shape):
            return ctx.enter_context(nc.psum_tensor("A_" + name, shape, F32))

        def sem(name):
            return ctx.enter_context(nc.semaphore("A_" + name))

        DOTS = BT * 2 * WIN
        wq = sb("wq", [P, 2, D])
        wk = sb("wk", [P, 2, D])
        wv = sb("wv", [P, 2, D])
        wout = sb("wout", [P, D])
        gain = sb("gain", [P, 1])
        council = sb("council", [P, 2])
        ptr = sb("ptr", [P, TILES], I32)
        ids = sb("ids", [P, BATCH, IDS], I32)
        position = sb("position", [P, IDS])
        base = sb("base", [P, BATCH, QT], I32)
        index = sb("index", [P, TILES, WIN], I32)
        id_index = sb("id_index", [P, TILES])
        picked = sb("picked", [P, IDS])
        rel = sb("rel", [P, TILES])
        window = sb("window", [P, TILES, WIN, D])
        g_sb = sb("g", [P, 2, D])
        m_sb = sb("m", [P, 2, D])
        cw = sb("cw", [P, 8])
        xn = sb("xn", [P, 2, BT, D])
        xt = sb("xt", [P, 2, BT, P])
        junk = sb("junk", [P, DOTS, D])
        raw = sb("raw", [P, 2, WIN, TILES])
        logic = sb("logic", [P, 12, TILES])
        probs = sb("probs", [P, 2, WIN, TILES])
        soft = sb("soft", [P, 3, 2, TILES])
        z = sb("z", [P, 2, BT, 2, D])
        zt = sb("zt", [P, 2, BT, 2, P])
        norm = Norm(ctx, nc, "A")

        ps_t = [ps(f"ps_t{i}", [P, BT, P]) for i in range(2)]
        ps_u = [ps(f"ps_u{i}", [P, 2, 2, D]) for i in range(4)]
        ps_o = [ps(f"ps_o{i}", [P, BT, D]) for i in range(2)]

        s_ptr = sem("s_ptr")
        s_x = sem("s_x")
        s_w = sem("s_w")
        s_base = sem("s_base")
        s_index = sem("s_index")
        s_window = [sem(f"s_window{i}") for i in range(2)]
        s_gm = sem("s_gm")
        s_gm_used = sem("s_gm_used")
        s_cexp_in = sem("s_cexp_in")
        s_cexp = sem("s_cexp")
        s_xn = sem("s_xn")
        s_tr = sem("s_tr")
        s_xt = sem("s_xt")
        s_u = sem("s_u")
        s_dots = sem("s_dots")
        s_shifted = sem("s_shifted")
        s_exp = sem("s_exp")
        s_z = sem("s_z")
        s_ztr = sem("s_ztr")
        s_zt = sem("s_zt")
        s_o = sem("s_o")
        s_x1 = sem("s_x1")
        s_dve = sem("s_dve")

        ctx_rows = io["ctx"]
        with nc.Block() as block:
            @block.sync
            def _(sp):
                sp.dma_start(ptr[:], io["pointers"]).then_inc(s_ptr, 16)
                for h in range(2):
                    half = slice(h * TILES // 2, (h + 1) * TILES // 2)
                    sp.dma_start(x_sb[:, half, :], x_rows[:, half, :]).then_inc(s_x, 16)
                sp.dma_start(ident[:], io["identity"]).then_inc(s_w, 16)
                for i, n in enumerate("ji"):
                    sp.dma_start(wq[:, i, :], io["L0_xattn_Wq" + n]).then_inc(s_w, 16)
                    sp.dma_start(wk[:, i, :], io["L0_xattn_Wk" + n]).then_inc(s_w, 16)
                    sp.dma_start(wv[:, i, :], io["L0_xattn_Wv" + n]).then_inc(s_w, 16)
                sp.dma_start(wout[:], io["L0_xattn_WoutT"]).then_inc(s_w, 16)
                sp.dma_start(gain[:], io["L0_xattn_gain"].partition_broadcast(P)).then_inc(s_w, 16)
                sp.dma_start(council[:], io["L0_xattn_council_weights"].partition_broadcast(P)).then_inc(s_w, 16)
                sp.dma_start(position[:], io["positions"].partition_broadcast(P)).then_inc(s_w, 16)
                sp.dma_start(ids[:].rearrange("p b i -> p (b i)"),
                             io["ids"].partition_broadcast(P)).then_inc(s_w, 16)
            W_ALL = 16 * 12

            @block.gpsimd
            def _(pool):
                nc.gpsimd.iota(base[:], [[CTX, BATCH], [0, QT]], base=0, channel_multiplier=0).then_inc(s_base, 1)
                pool.wait_ge(s_index, WIN)
                for t in range(TILES):
                    if t % BT == 0:
                        wait(pool, s_dots, DOTS * (t // BT - 1))
                    for w in range(WIN):
                        nc.gpsimd.indirect_dma_start(
                            window[:, t, w, :], None, ctx_rows,
                            bass.IndirectOffsetOnAxis(index[:, t, w:w + 1], axis=0)).then_inc(
                                s_window[t // BT % 2], 16)

            @block.vector
            def _(dve):
                chain = Chain(dve, s_dve)
                dve.wait_ge(s_ptr, 16)
                dve.wait_ge(s_base, 1)
                for w in range(WIN):
                    chain.mark(nc.vector.tensor_scalar(index[:, :, w], ptr[:], float(w), 0.0, ALU.add, ALU.max))
                chain.mark(nc.vector.tensor_scalar(id_index[:], ptr[:], 0.0, float(IDS - 1), ALU.max, ALU.min))
                chain.settle()
                for w in range(WIN):
                    nc.vector.scalar_tensor_tensor(index[:, :, w], index[:, :, w], float(CTX - 1),
                                                   base[:].rearrange("p b q -> p (b q)"),
                                                   ALU.min, ALU.add).then_inc(s_index, 1)
                dve.wait_ge(s_x, 32)
                norm.statistics(nc, dve, chain, x_sb)
                dve.wait_ge(s_w, W_ALL)
                for t in range(TILES):
                    chain.step(nc.vector.scalar_tensor_tensor(
                        picked[:], position[:], id_index[:, t:t + 1], ids[:, t // QT, :],
                        ALU.is_equal, ALU.mult, accum_out=rel[:, t:t + 1]))
                chain.step(nc.vector.tensor_tensor(cw[:, 0:1], council[:, 0:1], council[:, 1:2], ALU.max))
                nc.vector.tensor_scalar(cw[:, 1:3], council[:], cw[:, 0:1], None, ALU.subtract).then_inc(s_cexp_in, 1)
                dve.wait_ge(s_cexp, 1)
                chain.step(nc.vector.tensor_tensor(cw[:, 5:6], cw[:, 3:4], cw[:, 4:5], ALU.add))
                chain.step(nc.vector.reciprocal(cw[:, 6:7], cw[:, 5:6]))
                chain.step(nc.vector.tensor_tensor(cw[:, 6:7], cw[:, 6:7], gain[:], ALU.mult))
                chain.step(nc.vector.tensor_scalar(cw[:, 3:5], cw[:, 3:5], cw[:, 6:7], None, ALU.mult))
                dve.wait_ge(s_gm, 1)
                nc.vector.tensor_copy(g_sb[:], ps_o[0][:, 0:2, :]).then_inc(s_gm_used, 1)
                for i in range(2):
                    nc.vector.tensor_scalar(m_sb[:, i, :], ps_o[0][:, 2 + i, :], cw[:, 3 + i:4 + i], None,
                                            ALU.mult).then_inc(s_gm_used, 1)

                def normalize(k, parity):
                    wait(dve, s_tr, k - 1)
                    for i in range(BT):
                        norm.apply(nc, x_sb, k * BT + i, xn[:, parity, i, :]).then_inc(s_xn, 1)

                normalize(0, 0)

                def dots(k, parity, last, turn):
                    if not last:
                        normalize(k + 1, 1 - parity)
                    dve.wait_ge(s_window[parity], 16 * WIN * BT * (turn + 1))
                    wait(dve, s_dots, DOTS * k)
                    for i in range(BT):
                        if i % 2 == 0:
                            dve.wait_ge(s_u, 2 * k + i // 2 + 1)
                        for q in range(2):
                            for w in range(WIN):
                                nc.vector.tensor_tensor_reduce(
                                    junk[:, (i * 2 + q) * WIN + w, :],
                                    window[:, bass.ds(k * BT + i, 1), w, :].rearrange("p a d -> p (a d)"),
                                    ps_u[2 * parity + i // 2][:, i % 2, q, :], SCORE_SCALE0, 0.0, ALU.mult, ALU.add,
                                    raw[:, q, w, bass.ds(k * BT + i, 1)]).then_inc(s_dots, 1)

                for k in range(BLOCKS):
                    dots(k, k % 2, k == BLOCKS - 1, k // 2)
                dve.wait_ge(s_dots, DOTS * BLOCKS)
                V = nc.vector
                rule, value = [logic[:, i, :] for i in range(5)], [logic[:, 5 + i, :] for i in range(5)]
                any_rule, keep = logic[:, 10, :], logic[:, 11, :]
                l0, l1, l2 = (raw[:, 0, w, :] for w in range(WIN))
                for c in range(5):
                    chain.mark(V.tensor_scalar(rule[c], rel[:], float(c), None, ALU.is_equal))
                chain.mark(V.tensor_tensor(value[0], l1, l2, ALU.add))
                chain.mark(V.tensor_tensor(value[1], l1, l2, ALU.max))
                chain.mark(V.tensor_scalar(value[2], l1, -1.0, None, ALU.mult))
                chain.mark(V.scalar_tensor_tensor(value[3], l1, -1.0, l2, ALU.mult, ALU.max))
                chain.step(V.tensor_tensor(value[4], l1, l2, ALU.subtract))
                chain.step(V.scalar_tensor_tensor(value[4], value[4], -1.0, value[4], ALU.mult, ALU.max))
                chain.mark(V.tensor_tensor(any_rule, rule[0], rule[1], ALU.add))
                for c in range(5):
                    chain.mark(V.tensor_tensor(value[c], rule[c], value[c], ALU.mult))
                for c in range(2, 5):
                    chain.settle()
                    chain.mark(V.tensor_tensor(any_rule, any_rule, rule[c], ALU.add))
                for c in range(1, 5):
                    chain.settle()
                    chain.mark(V.tensor_tensor(value[0], value[0], value[c], ALU.add))
                chain.step(V.tensor_scalar(keep, any_rule, -1.0, 1.0, ALU.mult, ALU.add))
                chain.step(V.tensor_tensor(l0, l0, keep, ALU.mult))
                chain.step(V.tensor_tensor(value[0], value[0], any_rule, ALU.mult))
                chain.step(V.tensor_tensor(l0, l0, value[0], ALU.add))
                top_score, total, inverse = (soft[:, i, :, :] for i in range(3))
                chain.step(V.tensor_tensor(top_score, raw[:, :, 0, :], raw[:, :, 1, :], ALU.max))
                chain.step(V.tensor_tensor(top_score, top_score, raw[:, :, 2, :], ALU.max))
                for w in range(WIN):
                    V.tensor_tensor(probs[:, :, w, :], raw[:, :, w, :], top_score, ALU.subtract).then_inc(s_shifted, 1)
                dve.wait_ge(s_exp, 1)
                chain.step(V.tensor_tensor(total, probs[:, :, 0, :], probs[:, :, 1, :], ALU.add))
                chain.step(V.tensor_tensor(total, total, probs[:, :, 2, :], ALU.add))
                chain.step(V.reciprocal(inverse, total))
                for w in range(WIN):
                    chain.mark(V.tensor_tensor(probs[:, :, w, :], probs[:, :, w, :], inverse, ALU.mult))
                chain.settle()
                before_mix = chain.base + chain.n
                MIX = WIN * 2 * BT

                def mixes(k, parity, last, turn):
                    wait(dve, s_ztr, 2 * k - 1)
                    chain.at(before_mix + MIX * k)
                    for w in range(WIN):
                        for i in range(BT):
                            row = window[:, bass.ds(k * BT + i, 1), w, :].rearrange("p a d -> p (a d)")
                            for q in range(2):
                                to, weight = z[:, parity, i, q, :], probs[:, q, w, bass.ds(k * BT + i, 1)]
                                if w == 0:
                                    chain.mark(V.tensor_scalar(to, row, weight, None, ALU.mult))
                                else:
                                    ins = V.scalar_tensor_tensor(to, row, weight, to, ALU.mult, ALU.add)
                                    chain.mark(ins) if w < WIN - 1 else ins.then_inc(s_z, 1)
                        if w < WIN - 1:
                            chain.settle()

                def add_to_stream(k, parity):
                    dve.wait_ge(s_o, k + 1)
                    to = x_sb[:, bass.ds(k * BT, BT), :]
                    V.tensor_tensor(to, to, ps_o[parity][:], ALU.add).then_inc(s_x1, 1)

                MIX = 2 * BT * (WIN - 1)
                mixes(0, 0, False, 0)
                with dve.Fori(0, (BLOCKS - 2) // 2) as i:
                    mixes(2 * i + 1, 1, False, i)
                    add_to_stream(2 * i, 0)
                    mixes(2 * i + 2, 0, False, i + 1)
                    add_to_stream(2 * i + 1, 1)
                mixes(BLOCKS - 1, 1, True, 0)
                add_to_stream(BLOCKS - 2, 0)
                add_to_stream(BLOCKS - 1, 1)
                dve.wait_ge(s_x1, BLOCKS)

            @block.scalar
            def _(act):
                norm.root(nc, act)
                act.wait_ge(s_cexp_in, 1)
                nc.scalar.activation(cw[:, 3:5], cw[:, 1:3], ACT.Exp).then_inc(s_cexp, 1)

                def turned(k, parity, last, turn):
                    act.wait_ge(s_tr, k + 1)
                    nc.scalar.copy(xt[:, parity, :, :], ps_t[parity][:]).then_inc(s_xt, 1)

                rounds(act, BLOCKS, turned)
                act.wait_ge(s_shifted, WIN)
                nc.scalar.activation(probs[:], probs[:], ACT.Exp).then_inc(s_exp, 1)

                def mixed(k, parity, last, turn):
                    for half in range(2):
                        act.wait_ge(s_ztr, 2 * k + half + 1)
                        nc.scalar.copy(zt[:, parity, 2 * half:2 * half + 2, :, :],
                                       ps_u[2 * parity + half][:]).then_inc(s_zt, 1)

                rounds(act, BLOCKS, mixed)

            @block.tensor
            def _(pe):
                pe.wait_ge(s_w, W_ALL)
                for i in range(2):
                    nc.tensor.matmul(ps_o[0][:, i, :], wq[:, i, :], wk[:, i, :], start=True, stop=True)
                for i in range(2):
                    last_product = nc.tensor.matmul(ps_o[0][:, 2 + i, :], wv[:, i, :], wout[:], start=True, stop=True)
                last_product.then_inc(s_gm, 1)

                def queries(k, parity, last, turn):
                    pe.wait_ge(s_xn, BT * (k + 1))
                    wait(pe, s_xt, k)
                    for i in range(BT):
                        tr = nc.tensor.transpose(ps_t[parity][:, i, :], xn[:, parity, i, :], ident[:])
                    tr.then_inc(s_tr, 1)
                    pe.wait_ge(s_xt, k + 1)
                    if isinstance(k, int) and k == 0:
                        pe.wait_ge(s_gm_used, 1)
                    for half in range(2):
                        wait(pe, s_dots, DOTS * (k - 1) + (0 if isinstance(k, int) else 1))
                        for i in range(2):
                            u = nc.tensor.matmul(ps_u[2 * parity + half][:, i, :, :], xt[:, parity, 2 * half + i, :],
                                                 g_sb[:], start=True, stop=True)
                        u.then_inc(s_u, 1)

                rounds(pe, BLOCKS, queries)
                pe.wait_ge(s_gm_used, 3)
                pe.wait_ge(s_dots, DOTS * BLOCKS)

                def outputs(k, parity, last, turn):
                    wait(pe, s_zt, 2 * k - 1)
                    for half in range(2):
                        pe.wait_ge(s_z, 2 * BT * k + 4 * half + 4)
                        for i in range(4):
                            tr = nc.tensor.transpose(ps_u[2 * parity + half][:, i // 2, i % 2, :],
                                                     z[:, parity, 2 * half + i // 2, i % 2, :], ident[:])
                        tr.then_inc(s_ztr, 1)
                    pe.wait_ge(s_zt, 2 * k + 2)
                    for i in range(BT):
                        for q in range(2):
                            o = nc.tensor.matmul(ps_o[parity][:, i, :], zt[:, parity, i, q, :], m_sb[:, q, :],
                                                 start=(q == 0), stop=(q == 1))
                    o.then_inc(s_o, 1)

                rounds(pe, BLOCKS, outputs)


def expert_layer(nc, io, x_sb, ident):
    with ExitStack() as ctx:
        def sb(name, shape, dt=F32):
            return ctx.enter_context(nc.sbuf_tensor("B_" + name, shape, dt))

        def ps(name, shape):
            return ctx.enter_context(nc.psum_tensor("B_" + name, shape, F32))

        def sem(name):
            return ctx.enter_context(nc.semaphore("B_" + name))

        w_up = sb("w_up", [P, GROUPS0, HID0])
        w_up_hi = sb("w_up_hi", [P, GROUPS0, HID0], F32R)
        w_up_lo = sb("w_up_lo", [P, GROUPS0, HID0], F32R)
        w_down = sb("w_down", [P, GROUPS0, CH, D])
        b_up = sb("b_up", [P, GROUPS0 * CH])
        b_down = sb("b_down", [GROUPS0, D])
        w_gate = sb("w_gate", [P, EXPERTS0])
        b_gate = sb("b_gate", [P, 2, EXPERTS0])
        order = sb("order", [P, EXPERTS0])
        norm = Norm(ctx, nc, "B")
        xn = sb("xn", [P, 2, BT, D])
        xt = sb("xt", [P, BT, P])
        xt_hi = sb("xt_hi", [P, 2, BT, P], F32R)
        xt_lo = sb("xt_lo", [P, 2, BT, P], F32R)
        score = sb("score", [P, BT, EXPERTS0])
        left = sb("left", [P, BT, EXPERTS0])
        best = sb("best", [P, BT])
        hit = sb("hit", [P, BT, EXPERTS0])
        chosen = sb("chosen", [P, 2, BT, EXPERTS0])
        gate = sb("gate", [P, 2, BT, GROUPS0])
        gate_t = sb("gate_t", [GROUPS0, 2, BLOCK])
        HB = 3
        hidden = sb("hidden", [P, HB, CH, BLOCK])
        acc = sb("acc", [P, BT, D])

        ps_t = ps("ps_t", [P, BT, P])
        ps_g = ps("ps_g", [P, BLOCK])
        ps_h = [ps(f"ps_h{i}", [P, BLOCK]) for i in range(CH)]
        ps_e = [ps(f"ps_e{i}", [P, BT, D]) for i in range(2)]

        s_w = sem("s_w")
        s_w_down = sem("s_w_down")
        s_xn = sem("s_xn")
        s_tr = sem("s_tr")
        s_xt = sem("s_xt")
        s_xt_hi = sem("s_xt_hi")
        s_parts = sem("s_parts")
        s_w_hi = sem("s_w_hi")
        s_w_lo = sem("s_w_lo")
        s_logit = sem("s_logit")
        s_z = sem("s_z")
        s_sig = sem("s_sig")
        s_gate = sem("s_gate")
        s_gtr = sem("s_gtr")
        s_gt = sem("s_gt")
        s_up = sem("s_up")
        s_hid = sem("s_hid")
        s_down = sem("s_down")
        s_acc = sem("s_acc")
        s_dve = sem("s_dve")
        s_x2 = sem("s_x2")

        UPS = GROUPS0 * CH
        with nc.Block() as block:
            @block.sync
            def _(sp):
                for to, name in ((w_gate[:], "L0_ffn_WgT"), (b_up[:], "L0_ffn_b_up"), (b_down[:], "L0_ffn_b_down")):
                    sp.dma_start(to, io[name]).then_inc(s_w, 16)
                for i, name in enumerate(("bg", "bias")):
                    sp.dma_start(b_gate[:, i, :], io["L0_ffn_" + name].partition_broadcast(P)).then_inc(s_w, 16)
                sp.dma_start(order[:], io["order0"].partition_broadcast(P)).then_inc(s_w, 16)
                sp.dma_start(w_up[:], io["L0_ffn_w_up"]).then_inc(s_w, 16)
                sp.dma_start(w_down[:], io["L0_ffn_w_down"]).then_inc(s_w_down, 16)
            W_ALL = 16 * 7

            @block.tensor
            def _(pe):
                def turn_block(k, parity):
                    pe.wait_ge(s_xn, BT * (k + 1))
                    wait(pe, s_xt, k)
                    for i in range(BT):
                        tr = nc.tensor.transpose(ps_t[:, i, :], xn[:, parity, i, :], ident[:])
                    tr.then_inc(s_tr, 1)

                def logits(k, parity):
                    pe.wait_ge(s_xt, k + 1)
                    wait(pe, s_gt, k)
                    for i in range(BT):
                        lg = nc.tensor.matmul(ps_g[:, i * EXPERTS0:(i + 1) * EXPERTS0], xt[:, i, :],
                                              w_gate[:], start=True, stop=True)
                    lg.then_inc(s_logit, 1)

                def up(k, parity, e):
                    for c in range(CH):
                        u = e * CH + c
                        wait(pe, s_hid, UPS * k + u - CH + 1)
                        for n, (w, x) in enumerate(((w_up_hi, xt_hi), (w_up_hi, xt_lo), (w_up_lo, xt_hi))):
                            m = nc.tensor.matmul(ps_h[c][:], w[:, e, c * P:(c + 1) * P],
                                                 x[:, parity, :, :].rearrange("p i t -> p (i t)"),
                                                 start=(n == 0), stop=(n == 2))
                        m.then_inc(s_up, 1)

                def down(k, parity, e):
                    pe.wait_ge(s_hid, UPS * k + (e + 1) * CH)
                    wait(pe, s_acc, BT * (GROUPS0 * k + max(0, e - 1)))
                    for i in range(BT):
                        for c in range(CH):
                            dn = nc.tensor.matmul(ps_e[e % 2][:, i, :], hidden[:, e % HB, c, i * P:(i + 1) * P],
                                                  w_down[:, e, c, :], start=(c == 0),
                                                  stop=(c == CH - 1 and e < EXPERTS0))
                        if e == EXPERTS0:
                            dn = nc.tensor.matmul(ps_e[e % 2][:, i, :], gate_t[:, parity, i * P:(i + 1) * P],
                                                  b_down[:], start=False, stop=True)
                    dn.then_inc(s_down, 1)

                def experts(k, parity, last, turn):
                    first = isinstance(k, int) and k == 0
                    pe.wait_ge(s_parts, k + 1)
                    for e in range(GROUPS0):
                        if first:
                            pe.wait_ge(s_w_lo, e + 1)
                            if e == 1:
                                pe.wait_ge(s_w_down, 16)
                        up(k, parity, e)
                        if e > 0:
                            down(k, parity, e - 1)
                        if e == 3:
                            pe.wait_ge(s_gate, k + 1)
                            for i in range(BT):
                                tr = nc.tensor.transpose(ps_g[0:GROUPS0, i * P:(i + 1) * P],
                                                         gate[:, parity, i, :], ident[:])
                            tr.then_inc(s_gtr, 1)
                        if e == 5 and not last:
                            turn_block(k + 1, 1 - parity)
                        if e == 6 and not last:
                            logits(k + 1, 1 - parity)
                    pe.wait_ge(s_gt, k + 1)
                    down(k, parity, GROUPS0 - 1)

                pe.wait_ge(s_w, W_ALL)
                turn_block(0, 0)
                logits(0, 0)
                rounds(pe, BLOCKS, experts)

            @block.scalar
            def _(act):
                norm.root(nc, act)

                def turned(k, parity):
                    act.wait_ge(s_tr, k + 1)
                    wait(act, s_logit, k)
                    wait(act, s_parts, k)
                    nc.scalar.copy(xt[:], ps_t[:]).then_inc(s_xt, 1)

                def sigmoid(k):
                    act.wait_ge(s_z, k + 1)
                    nc.scalar.activation(score[:], score[:], ACT.Sigmoid).then_inc(s_sig, 1)

                def gelus(k, parity, last, turn):
                    for e in range(GROUPS0):
                        wait(act, s_down, GROUPS0 * k + e - HB + 1)
                        for c in range(CH):
                            u = e * CH + c
                            act.wait_ge(s_up, UPS * k + u + 1)
                            nc.scalar.activation(hidden[:, e % HB, c, :], ps_h[c][:], ACT.Gelu,
                                                 bias=b_up[:, u:u + 1]).then_inc(s_hid, 1)
                        if e == 3:
                            act.wait_ge(s_gtr, k + 1)
                            nc.scalar.copy(gate_t[:, parity, :], ps_g[0:GROUPS0, :]).then_inc(s_gt, 1)
                        if e == 5 and not last:
                            turned(k + 1, 1 - parity)
                    if not last:
                        sigmoid(k + 1)

                turned(0, 0)
                sigmoid(0)
                rounds(act, BLOCKS, gelus)

            @block.gpsimd
            def _(pool):
                for e in range(GROUPS0):
                    pool.wait_ge(s_w_hi, e + 1)
                    nc.gpsimd.tensor_tensor(w_up_lo[:, e, :], w_up[:, e, :], w_up_hi[:, e, :].bitcast(F32),
                                            ALU.subtract).then_inc(s_w_lo, 1)

            @block.vector
            def _(dve):
                chain = Chain(dve, s_dve)
                V = nc.vector
                norm.statistics(nc, dve, chain, x_sb)
                for parity in range(2):
                    chain.mark(V.memset(gate[:, parity, :, EXPERTS0:], 1.0))
                chain.settle()
                setup = chain.n
                dve.wait_ge(s_w, W_ALL)

                def normalize(k, parity):
                    wait(dve, s_tr, k - 1)
                    for i in range(BT):
                        norm.apply(nc, x_sb, k * BT + i, xn[:, parity, i, :]).then_inc(s_xn, 1)

                def scores(k):
                    dve.wait_ge(s_logit, k + 1)
                    chain.at(setup + STEPS * k)
                    for i in range(2):
                        src = ps_g[:, 0:BT * EXPERTS0].rearrange("p (i e) -> p i e", i=BT) if i == 0 else score[:]
                        ins = V.tensor_tensor(score[:], src, b_gate[:, i:i + 1, :].to_broadcast([P, BT, EXPERTS0]),
                                              ALU.add)
                        chain.step(ins) if i == 0 else ins.then_inc(s_z, 1)
                    dve.wait_ge(s_sig, k + 1)

                def gates(k, parity):
                    wide = [P, BT, EXPERTS0]
                    for n in range(2):
                        src = score if n == 0 else left
                        chain.step(V.tensor_reduce(best[:], src[:], AX, ALU.max))
                        chain.step(V.tensor_tensor(hit[:], src[:], best[:].unsqueeze(2).to_broadcast(wide), ALU.is_equal))
                        chain.step(V.tensor_tensor(hit[:], hit[:], order[:].unsqueeze(1).to_broadcast(wide), ALU.mult))
                        chain.step(V.tensor_reduce(best[:], hit[:], AX, ALU.max))
                        chain.step(V.tensor_tensor(chosen[:, n], hit[:], best[:].unsqueeze(2).to_broadcast(wide), ALU.is_equal))
                        if n == 0:
                            chain.step(V.scalar_tensor_tensor(left[:], chosen[:, 0], -2.0, score[:], ALU.mult, ALU.add))
                    chain.step(V.tensor_tensor(chosen[:, 0], chosen[:, 0], chosen[:, 1], ALU.add))
                    V.tensor_tensor(gate[:, parity, :, 0:EXPERTS0], chosen[:, 0], score[:], ALU.mult).then_inc(s_gate, 1)
                    assert chain.n == STEPS, chain.n
                    dve.wait_ge(s_gate, k + 1)
                STEPS = 1 + 5 * 2 + 1 + 1

                def split_inputs(k, parity):
                    dve.wait_ge(s_xt, k + 1)
                    V.tensor_copy(xt_hi[:, parity], xt[:]).then_inc(s_xt_hi, 1)
                    dve.wait_ge(s_xt_hi, k + 1)
                    V.tensor_tensor(xt_lo[:, parity], xt[:], xt_hi[:, parity].bitcast(F32),
                                    ALU.subtract).then_inc(s_parts, 1)

                def sums(k, parity, last, turn):
                    scores(k)
                    gates(k, parity)
                    for e in range(GROUPS0):
                        dve.wait_ge(s_down, GROUPS0 * k + e + 1)
                        if e > 0 or not (isinstance(k, int) and k == 0):
                            dve.wait_ge(s_acc, BT * (GROUPS0 * k + e))
                        if e == EXPERTS0:
                            V.tensor_tensor(acc[:], acc[:], ps_e[e % 2][:], ALU.add).then_inc(s_acc, BT)
                            dve.wait_ge(s_acc, BT * GROUPS0 * (k + 1))
                            to = x_sb[:, bass.ds(k * BT, BT), :]
                            V.tensor_tensor(to, to, acc[:], ALU.add).then_inc(s_x2, 1)
                            dve.wait_ge(s_x2, k + 1)
                            continue
                        for i in range(BT):
                            g = gate[:, parity, i, e:e + 1]
                            if e == 0:
                                ins = V.tensor_scalar(acc[:, i, :], ps_e[0][:, i, :], g, None, ALU.mult)
                            else:
                                ins = V.scalar_tensor_tensor(acc[:, i, :], ps_e[e % 2][:, i, :], g, acc[:, i, :],
                                                             ALU.mult, ALU.add)
                            ins.then_inc(s_acc, 1)
                        if e == 1 and not last:
                            normalize(k + 1, 1 - parity)
                        if e == 6 and not last:
                            split_inputs(k + 1, 1 - parity)

                normalize(0, 0)
                for e in range(GROUPS0):
                    V.tensor_copy(w_up_hi[:, e, :], w_up[:, e, :]).then_inc(s_w_hi, 1)
                split_inputs(0, 0)
                rounds(dve, BLOCKS, sums)


def head_attention(nc, io, x_sb, ident):
    EXP_LIMIT = 60.0
    UNITS = GROUPS * KT
    PRING = 4
    LAG = 2
    with ExitStack() as ctx:
        def sb(name, shape, dt=F32):
            return ctx.enter_context(nc.sbuf_tensor("C_" + name, shape, dt))

        def ps(name, shape):
            return ctx.enter_context(nc.psum_tensor("C_" + name, shape, F32))

        def sem(name):
            return ctx.enter_context(nc.semaphore("C_" + name))

        wq = sb("wq", [P, D])
        wk = sb("wk", [P, D])
        wv = sb("wv", [P, D])
        wo = sb("wo", [P, GROUPS, D])
        bqk = sb("bqk", [P, 2])
        bv = sb("bv", [P, D])
        bo = sb("bo", [P, D])
        mask = sb("mask", [P, HG])
        head_sum = sb("head_sum", [P, HEADS])
        ones = sb("ones", [P, 1])
        place_m = sb("place_m", [HEADS, GROUPS, P])
        place_m_r = sb("place_m_r", [HEADS, GROUPS, P], F32R)
        place_r = sb("place_r", [P, 2, GROUPS, P], F32R)
        norm = Norm(ctx, nc, "C")
        ctx_t = sb("ctx_t", [P, 2, CTX])
        k_t = sb("k_t", [P, CTX])
        k_hi = sb("k_hi", [P, CTX], F32R)
        k_lo = sb("k_lo", [P, CTX], F32R)
        ends = sb("ends", [P, 4])
        keys = sb("keys", [P, 2, GROUPS, CTXP], F32R)
        values = sb("values", [P, 2, KT, HEADS, 2 * DK])
        xn = sb("xn", [P, QT, D])
        xt = sb("xt", [P, QT, P])
        q_t = sb("q_t", [P, SEQ])
        q_hi = sb("q_hi", [P, SEQ], F32R)
        q_lo = sb("q_lo", [P, SEQ], F32R)
        q_bound = sb("q_bound", [P, SEQ])
        queries = sb("queries", [P, 2, GROUPS, HG, SEQ], F32R)
        over = sb("over", [P, 2])
        flag = sb("flag", [1, 2], I32)
        top_part = sb("top_part", [P, QT, HEADS, len(KCH)])
        top_m = sb("top_m", [P, QT, HEADS])
        minus_m = sb("minus_m", [HEADS, SEQ], F32R)
        probs = sb("probs", [P, PRING, HG, SEQ])
        o_t = sb("o_t", [P, GROUPS, SEQ])
        den_t = sb("den_t", [P, GROUPS, SEQ])

        ps_s = [ps(f"ps_s{i}", [P, HG, SEQ]) for i in range(2)]
        ps_o = [ps(f"ps_o{i}", [P, SEQ]) for i in range(2)]
        ps_p = ps("ps_p", [P, 512])
        ps_f = ps("ps_f", [P, 512])

        s_w = sem("s_w")
        s_wk = sem("s_wk")
        s_const = sem("s_const")
        s_ctx = [sem(f"s_ctx{i}") for i in range(2)]
        s_split = sem("s_split")
        s_placed = [sem(f"s_placed{i}") for i in range(2)]
        s_xn = sem("s_xn")
        s_job = sem("s_job")
        s_job_done = sem("s_job_done")
        s_score = sem("s_score")
        s_exp = sem("s_exp")
        s_av = sem("s_av")
        s_o_read = sem("s_o_read")
        s_den = sem("s_den")
        s_fin = sem("s_fin")
        s_fin_read = sem("s_fin_read")
        s_top = sem("s_top")
        s_top_read = sem("s_top_read")
        s_dve = sem("s_dve")
        s_pool = sem("s_pool")
        s_dve_fin = sem("s_dve_fin")
        s_seen_pe = sem("s_seen_pe")
        s_seen_dve = sem("s_seen_dve")

        JOBS = ([("turn", 0), ("query", 0)] + [("key", i) for i in range(len(KCH))]
                + [("value", i) for i in range(0, KT, 4)] + [("place_query", g) for g in range(GROUPS)]
                + [("bound", 0), ("count", 0)])
        FIRST_JOBS = JOBS[2:2 + len(KCH)] + JOBS[:2] + JOBS[2 + len(KCH):]
        NJ = len(JOBS)
        JOB_AT = dict(zip((4, 5, 15, 17, 19, 21, 24, 31, 32, 33, 36, 38, 40, 42, 44, 46), range(NJ)))
        assert len(JOB_AT) == NJ
        FIN_AT = {6: 0, 7: 1, 14: 2}
        TAKE_AT = {18: 0, 15 + KT: 1, 15 + 2 * KT: 2, 2: 3}
        MAXIMA_AT = max(JOB_AT) + 1
        assert MAXIMA_AT < UNITS
        TOPS = HEADS * QT * len(KCH)
        TOP_FILLS = TOPS + 1 + GROUPS
        TOP_READS = TOPS + 2 + GROUPS

        def top_rounds():
            n = 0
            for h in range(HEADS):
                for qt in range(QT):
                    for i, (at, width) in enumerate(KCH):
                        yield n, h, qt, i, at, width
                        n += 1

        with nc.Block() as block:
            @block.sync
            def _(sp):
                loads = [(wq, "L1_xattn_Wq"), (wv, "L1_xattn_Wv"), (wo, "L1_xattn_Wo_strips"),
                         (mask, "head_mask"),
                         (head_sum, "head_sum"), (place_m, "place_m"), (probs, "place")]
                for to, name in ((wk, "Wk"), (bqk, "bqk")):
                    sp.dma_start(to[:], io["L1_xattn_" + name]).then_inc(s_wk, 16)
                sp.dma_start(ctx_t[:, 0, :], io["ctx_t"][0]).then_inc(s_ctx[0], 16)
                for to, name in loads:
                    sp.dma_start(to[:] if name != "place" else to[:, 0, :, :].rearrange("p h q -> p (h q)"),
                                 io[name] if name != "place" else io[name].rearrange("p a g r -> p (a g r)")).then_inc(s_w, 16)
                for to, name in ((bv, "bv"), (bo, "bo")):
                    sp.dma_start(to[:], io["L1_xattn_" + name].partition_broadcast(P)).then_inc(s_w, 16)
                sp.dma_start(ctx_t[:, 1, :], io["ctx_t"][1]).then_inc(s_ctx[1], 16)

                def move_sums(b):
                    sp.wait_ge(s_o_read, GROUPS * (b + 1))
                    for j in range(HG):
                        sp.dma_start(den_t[32 * j:32 * j + DK, :, :],
                                     o_t[32 * j + DK:32 * j + 2 * DK, :, :]).then_inc(s_den, 16)

                def place(p, parity, load, sums=True):
                    if sums:
                        move_sums(p - 2)
                    sp.wait_ge(s_split, p + 1)
                    for g in range(GROUPS):
                        for product, part in enumerate((k_hi, k_hi, k_lo)):
                            sp.dma_start(keys[32 * product:32 * product + 32, parity, g, 0:CTX].bitcast(F32),
                                         part[32 * g:32 * g + 32, 0:CTX].bitcast(F32)).then_inc(s_placed[parity], 16)
                    if load:
                        sp.wait_ge(s_job_done, NJ * (p + 1))
                        sp.dma_start(ctx_t[:, parity, :], io["ctx_t"][bass.ds(p + 2, 1)].rearrange(
                            "b p c -> p (b c)")).then_inc(s_ctx[parity], 16)

                place(0, 0, True, False)
                place(1, 1, True, False)
                with sp.Fori(1, BATCH // 2 - 1) as i:
                    place(2 * i, 0, True)
                    place(2 * i + 1, 1, True)
                place(BATCH - 2, 0, False)
                place(BATCH - 1, 1, False)
                move_sums(BATCH - 2)
                move_sums(BATCH - 1)
            W_ALL = 16 * 9

            def loaded(eng, parity, turn):
                eng.wait_ge(s_ctx[parity], 16 * (turn + 1))

            def placed(eng, parity, turn):
                eng.wait_ge(s_placed[parity], 16 * 3 * GROUPS * (turn + 1))

            @block.tensor
            def _(pe):
                T = nc.tensor

                def place_query(parity, g, shifted=False):
                    T.matmul(ps_p[:, 0:SEQ], place_r[:, 0, g, :], q_hi[:], start=True, stop=False)
                    m = T.matmul(ps_p[:, 0:SEQ], place_r[:, 1, g, :], q_lo[:], start=False, stop=not shifted)
                    if shifted:
                        m = T.matmul(ps_p[:, 0:SEQ], place_m_r[:, g, :], minus_m[:], start=False, stop=True)
                    return m

                def job(p, parity, turn, n, kind, arg):
                    wait(pe, s_job_done, NJ * p + n)
                    if kind == "turn":
                        pe.wait_ge(s_xn, QT * (p + 1))
                        for i in range(QT):
                            m = T.transpose(ps_p[:, i * P:(i + 1) * P], xn[:, i, :], ident[:])
                    elif kind == "query":
                        m = T.matmul(ps_p[:, 0:SEQ], wq[:], xt[:].rearrange("p i t -> p (i t)"), start=True, stop=True)
                    elif kind == "key":
                        if arg == 0:
                            loaded(pe, parity, turn)
                        at, width = KCH[arg]
                        m = T.matmul(ps_p[:, 0:width], wk[:], ctx_t[:, parity, at:at + width], start=True, stop=True)
                    elif kind == "value":
                        for kt in range(arg, min(arg + 4, KT)):
                            rows = min(P, CTX - kt * P)
                            m = T.matmul(ps_p[0:rows, (kt - arg) * D:(kt - arg + 1) * D],
                                         ctx_t[:, parity, kt * P:kt * P + rows], wv[:], start=True, stop=True)
                    elif kind == "place_query":
                        m = place_query(parity, arg)
                    elif kind == "bound":
                        m = T.matmul(ps_p[0:HEADS, 0:SEQ], head_sum[:], q_bound[:], start=True, stop=True)
                    else:
                        m = T.matmul(ps_p[0:1, 0:1], over[:, 1:2], ones[:], start=True, stop=True)
                    m.then_inc(s_job, 1)

                def maxima(p, parity, turn):
                    pe.wait_ge(s_job_done, NJ * (p + 1))
                    pe.sem_inc(s_seen_pe, 1)
                    wide = pe.value_load(flag[0:1, parity:parity + 1], min_val=0, max_val=HEADS)
                    with pe.If(wide > 0):
                        placed(pe, parity, turn)
                        for n, h, qt, i, at, width in top_rounds():
                            wait(pe, s_top_read, TOP_READS * p + n)
                            T.matmul(ps_p[:, 0:width + width % 2],
                                     queries[:, parity, h // HG, h % HG, qt * P:(qt + 1) * P],
                                     keys[:, parity, h // HG, at:at + width + width % 2],
                                     start=True, stop=True).then_inc(s_top, 1)
                        pe.wait_ge(s_top_read, TOP_READS * p + TOPS + 1)
                        for qt in range(QT):
                            m = T.transpose(ps_p[0:HEADS, qt * P:(qt + 1) * P], top_m[:, qt, :], ident[:])
                        m.then_inc(s_top, 1)
                        for g in range(GROUPS):
                            pe.wait_ge(s_top_read, TOP_READS * p + TOPS + 2 + g)
                            place_query(parity, g, True).then_inc(s_top, 1)
                    with pe.Else():
                        pe.sem_inc(s_top, TOP_FILLS)

                def scores(k, parity, n):
                    g, kt = divmod(n, KT)
                    wait(pe, s_exp, UNITS * k + n - 1)
                    for j in range(HG):
                        m = T.matmul(ps_s[n % 2][:, j, :], keys[:, parity, g, kt * P:(kt + 1) * P],
                                     queries[:, parity, g, j, :], start=True, stop=True)
                    m.then_inc(s_score, 1)

                def weigh(k, parity, n):
                    g, kt = divmod(n, KT)
                    pe.wait_ge(s_exp, UNITS * k + n + 1)
                    if kt == 0:
                        wait(pe, s_o_read, GROUPS * k + g - 1)
                    for j in range(HG):
                        m = T.matmul(ps_o[g % 2][32 * j:32 * j + 2 * DK, :], values[:, parity, kt, g * HG + j, :],
                                     probs[:, n % PRING, j, :], start=(kt == 0), stop=(kt == KT - 1))
                    m.then_inc(s_av, 1)
                    return m

                def finish(b):
                    pe.wait_ge(s_fin_read, 3 * b + 2)
                    for qt in range(QT):
                        for g in range(GROUPS):
                            m = T.matmul(ps_f[:, qt * D:(qt + 1) * D], o_t[:, g, qt * P:(qt + 1) * P], wo[:, g, :],
                                         start=(g == 0), stop=(g == GROUPS - 1))
                    m.then_inc(s_fin, 1)

                def attend(k, parity, last, turn):
                    first = isinstance(k, int) and k == 0
                    for n in range(UNITS):
                        if n == 0:
                            pe.wait_ge(s_job_done, NJ * (k + 1))
                            pe.wait_ge(s_top_read, TOP_READS * (k + 1))
                            placed(pe, parity, turn)
                        scores(k, parity, n)
                        if n >= LAG:
                            weigh(k, parity, n - LAG)
                        elif not first:
                            weigh(k - 1, 1 - parity, UNITS - LAG + n)
                        if FIN_AT.get(n) == 2 and not first:
                            finish(k - 1)
                        if n in JOB_AT and not last:
                            job(k + 1, 1 - parity, turn + parity, JOB_AT[n], *JOBS[JOB_AT[n]])
                        if n == MAXIMA_AT and not last:
                            maxima(k + 1, 1 - parity, turn + parity)

                pe.wait_ge(s_wk, 32)
                for n, (kind, arg) in enumerate(FIRST_JOBS):
                    if kind == "turn":
                        pe.wait_ge(s_w, W_ALL)
                        pe.wait_ge(s_const, 2)
                    job(0, 0, 0, n, kind, arg)
                maxima(0, 0, 0)
                rounds(pe, BATCH, attend)
                for n in range(UNITS - LAG, UNITS):
                    weigh(BATCH - 1, 1, n)
                finish(BATCH - 1)

            @block.scalar
            def _(act):
                norm.root(nc, act)

                def exps(k, parity, last, turn):
                    for n in range(UNITS):
                        act.wait_ge(s_score, UNITS * k + n + 1)
                        wait(act, s_av, UNITS * k + n - PRING + 1)
                        nc.scalar.activation(probs[:, n % PRING, :, :], ps_s[n % 2][:], ACT.Exp,
                                             scale=SCORE_SCALE1).then_inc(s_exp, 1)

                rounds(act, BATCH, exps)

            @block.gpsimd
            def _(pool):
                G = nc.gpsimd
                chain = Chain(pool, s_pool)
                chain.step(G.memset(keys[:, :, :, CTX:].bitcast(F32), 0.0))
                chain.step(G.memset(keys[SHIFT_ROW:, :, :, 0:CTX].bitcast(F32), 1.0))
                chain.step(G.memset(values[:, :, 0:KT - 1].rearrange("p a k h v -> p a (k h v)"), 1.0))
                chain.step(G.memset(values[:, :, KT - 1].rearrange("p a h v -> p a (h v)"), 0.0))
                for parity in range(2):
                    chain.step(G.memset(values[0:CTX - (KT - 1) * P, parity, KT - 1, :, DK:], 1.0))
                pool.sem_inc(s_const, 1)

            @block.vector
            def _(dve):
                chain = Chain(dve, s_dve)
                V = nc.vector
                rows = CTX - (KT - 1) * P
                for bank in ps_o:
                    chain.mark(V.memset(bank[:], 0.0))
                chain.mark(V.memset(den_t[:], 1.0))
                chain.mark(V.memset(ones[:], 1.0))

                def place_query(parity, g, sem_):
                    V.tensor_tensor(queries[:, parity, g, :, :],
                                    ps_p[:, 0:SEQ].unsqueeze(1).to_broadcast([P, HG, SEQ]),
                                    mask[:].unsqueeze(2).to_broadcast([P, HG, SEQ]), ALU.mult).then_inc(sem_, 1)

                def job(p, parity, turn, n, kind, arg):
                    first = isinstance(p, int) and p == 0
                    if kind == "turn":
                        for i in range(QT):
                            norm.apply(nc, x_sb, QT * p + i, xn[:, i, :]).then_inc(s_xn, 1)
                    dve.wait_ge(s_job, NJ * p + n + 1)
                    done = None
                    if kind == "turn":
                        done = V.tensor_copy(xt[:].rearrange("p i t -> p (i t)"), ps_p[:, 0:SEQ])
                    elif kind == "query":
                        chain.step(V.tensor_scalar(q_t[:], ps_p[:, 0:SEQ], bqk[:, 0:1], None, ALU.add))
                        chain.mark(V.tensor_copy(q_hi[:], q_t[:]))
                        chain.step(V.scalar_tensor_tensor(q_bound[:], q_t[:], -1.0, q_t[:], ALU.mult, ALU.max))
                        done = V.tensor_tensor(q_lo[:], q_t[:], q_hi[:].bitcast(F32), ALU.subtract)
                    elif kind == "key":
                        at, width = KCH[arg]
                        evac = V.tensor_scalar(k_t[:, at:at + width], ps_p[:, 0:width], bqk[:, 1:2], None, ALU.add)
                        done = evac
                        if arg == len(KCH) - 1:
                            done = None
                            evac.then_inc(s_job_done, 1)
                            dve.wait_ge(s_job_done, NJ * p + n + 1)
                            k = k_t[:, 0:CTX]
                            chain.mark(V.tensor_reduce(ends[:, 0:1], k, AX, ALU.max))
                            chain.step(V.tensor_reduce(ends[:, 1:2], k, AX, ALU.min))
                            chain.mark(V.tensor_tensor(ends[:, 2:3], ends[:, 0:1], ends[:, 1:2], ALU.add))
                            chain.step(V.tensor_tensor(ends[:, 3:4], ends[:, 0:1], ends[:, 1:2], ALU.subtract))
                            chain.step(V.tensor_scalar(ends[:, 2:4], ends[:, 2:4], 0.5, None, ALU.mult))
                            chain.step(V.tensor_scalar(k, k, ends[:, 2:3], None, ALU.subtract))
                            if not first:
                                placed(dve, 1 - parity, turn - 1 + parity)
                            chain.step(V.tensor_copy(k_hi[:, 0:CTX], k))
                            V.tensor_tensor(k_lo[:, 0:CTX], k, k_hi[:, 0:CTX].bitcast(F32),
                                            ALU.subtract).then_inc(s_split, 1)
                    elif kind == "value":
                        n_kt = min(arg + 4, KT) - arg
                        r = P if n_kt == 4 else rows
                        done = V.tensor_tensor(
                            values[0:r, parity, arg:arg + n_kt, :, 0:DK],
                            ps_p[0:r, 0:n_kt * D].rearrange("p (k h d) -> p k h d", k=n_kt, h=HEADS),
                            bv[0:r, :].rearrange("p (h d) -> p h d", h=HEADS).unsqueeze(1).to_broadcast([r, n_kt, HEADS, DK]),
                            ALU.add)
                    elif kind == "place_query":
                        if arg == 0:
                            chain.mark(V.tensor_scalar(q_bound[:], q_bound[:], ends[:, 3:4], None, ALU.mult))
                        place_query(parity, arg, s_job_done)
                    elif kind == "bound":
                        chain.step(V.tensor_reduce(over[0:HEADS, 0:1], ps_p[0:HEADS, 0:SEQ], AX, ALU.max))
                        done = V.tensor_scalar(over[0:HEADS, 1:2], over[0:HEADS, 0:1], EXP_LIMIT / SCORE_SCALE1, None, ALU.is_gt)
                    else:
                        done = V.tensor_copy(flag[0:1, parity:parity + 1], ps_p[0:1, 0:1])
                    if done is not None:
                        done.then_inc(s_job_done, 1)
                JOB_STEPS = 3 + 8 + 1

                def prepare(p, parity, turn, n):
                    if n == 0:
                        chain.at(setup + JOB_STEPS * p)
                    job(p, parity, turn, n, *JOBS[n])
                    if n == NJ - 1:
                        assert chain.n == JOB_STEPS, chain.n

                def maxima(p, parity):
                    dve.wait_ge(s_job_done, NJ * (p + 1))
                    dve.sem_inc(s_seen_dve, 1)
                    wide = dve.value_load(flag[0:1, parity:parity + 1], min_val=0, max_val=HEADS)
                    with dve.If(wide > 0):
                        for n, h, qt, i, at, width in top_rounds():
                            dve.wait_ge(s_top, TOP_FILLS * p + n + 1)
                            V.tensor_reduce(top_part[:, qt, h, i:i + 1], ps_p[:, 0:width], AX,
                                            ALU.max).then_inc(s_top_read, 1)
                        dve.wait_ge(s_top_read, TOP_READS * p + TOPS)
                        V.tensor_reduce(top_m[:], top_part[:], AX, ALU.max, negate=True).then_inc(s_top_read, 1)
                        dve.wait_ge(s_top, TOP_FILLS * p + TOPS + 1)
                        V.tensor_copy(minus_m[:], ps_p[0:HEADS, 0:SEQ]).then_inc(s_top_read, 1)
                        for g in range(GROUPS):
                            dve.wait_ge(s_top, TOP_FILLS * p + TOPS + 2 + g)
                            place_query(parity, g, s_top_read)
                    with dve.Else():
                        dve.sem_inc(s_top_read, TOP_READS)

                def take_o(b, g):
                    dve.wait_ge(s_av, UNITS * b + KT * (g + 1))
                    if g == 0:
                        wait(dve, s_fin, b)
                    V.tensor_copy(o_t[:, g, :], ps_o[g % 2][:]).then_inc(s_o_read, 1)

                def finish(b, step):
                    if step < 2:
                        dve.wait_ge(s_den, 16 * HG * (b + 1))
                        half = slice(2 * step, 2 * step + 2)
                        den = den_t[:, half, :].rearrange("p g q -> p (g q)")
                        fin.step(V.reciprocal(den, den))
                        V.tensor_tensor(o_t[:, half, :], o_t[:, half, :], den_t[:, half, :],
                                        ALU.mult).then_inc(s_fin_read, 1)
                    else:
                        dve.wait_ge(s_fin, b + 1)
                        to = x_sb[:, bass.ds(QT * b, QT), :]
                        fin.step(V.tensor_tensor(to, to, ps_f[:].rearrange("p (i d) -> p i d", i=BT)[:, 0:QT, :], ALU.add))
                        V.tensor_tensor(to, to, bo[:].unsqueeze(1).to_broadcast([P, QT, D]),
                                        ALU.add).then_inc(s_fin_read, 1)
                fin = Chain(dve, s_dve_fin)

                def attend(k, parity, last, turn):
                    first = isinstance(k, int) and k == 0
                    for n in range(UNITS):
                        if n in TAKE_AT:
                            g = TAKE_AT[n]
                            if g < GROUPS - 1:
                                take_o(k, g)
                            elif not first:
                                take_o(k - 1, g)
                        if n in FIN_AT and not first:
                            fin.at(3 * (k - 1) + FIN_AT[n])
                            finish(k - 1, FIN_AT[n])
                        if n in JOB_AT and not last:
                            prepare(k + 1, 1 - parity, turn + parity, JOB_AT[n])
                        if n == MAXIMA_AT and not last:
                            maxima(k + 1, 1 - parity)

                dve.wait_ge(s_wk, 32)
                for n in range(len(KCH)):
                    job(0, 0, 0, n, *FIRST_JOBS[n])
                norm.statistics(nc, dve, chain, x_sb)
                dve.wait_ge(s_w, W_ALL)
                chain.mark(V.tensor_copy(place_m_r[:], place_m[:]))
                chain.step(V.tensor_copy(place_r[:].rearrange("p a g r -> p (a g r)"),
                                         probs[:, 0, :, :].rearrange("p h q -> p (h q)")))
                V.memset(over[:], 0.0).then_inc(s_const, 1)
                dve.wait_ge(s_const, 2)
                for n in range(len(KCH), NJ):
                    job(0, 0, 0, n, *FIRST_JOBS[n])
                setup = chain.n - JOB_STEPS
                maxima(0, 0)
                rounds(dve, BATCH, attend)
                take_o(BATCH - 1, GROUPS - 1)
                for step in range(3):
                    fin.at(3 * (BATCH - 1) + step)
                    finish(BATCH - 1, step)
                dve.wait_ge(s_fin_read, 3 * BATCH)


def head_experts(nc, io, x_sb, ident, out_rows):
    with ExitStack() as ctx:
        def sb(name, shape, dt=F32):
            return ctx.enter_context(nc.sbuf_tensor("D_" + name, shape, dt))

        def ps(name, shape):
            return ctx.enter_context(nc.psum_tensor("D_" + name, shape, F32))

        def sem(name):
            return ctx.enter_context(nc.semaphore("D_" + name))

        HG1 = H1 // 2
        EG = 2
        QUADS = HP * EG
        UNITS = QUADS * 4
        RING = 8
        CHOICES = [P, BT * H1, E1]

        wm = sb("wm", [P, D])
        bm = sb("bm", [P, 1])
        emb = sb("emb", [P, P])
        w_up = sb("w_up", [P, 2, PAIRS, P])
        w_up_r = sb("w_up_r", [P, 2, PAIRS, P], F32R)
        part = sb("part", [P, 1])
        b_up = sb("b_up", [P, PAIRS])
        w_down = sb("w_down", [P, PAIRS, 32])
        b_down = sb("b_down", [P, EG])
        wo = sb("wo", [P, H1, D])
        bo = sb("bo", [P, D])
        order = sb("order", [P, E1])
        place_t = sb("place_t", [P, 2, HP, P], F32R)
        place_g = sb("place_g", [P, HG1, EG, P], F32R)
        norm = Norm(ctx, nc, "D")
        xn = sb("xn", [P, BT, D])
        xt = sb("xt", [P, BLOCK])
        h_t = sb("h_t", [P, BLOCK])
        h_hi = sb("h_hi", [P, BLOCK], F32R)
        h_lo = sb("h_lo", [P, BLOCK], F32R)
        up_in = sb("up_in", [P, 2, HP, BLOCK], F32R)
        weight = sb("weight", CHOICES)
        left = sb("left", CHOICES)
        hit = sb("hit", CHOICES)
        chosen = sb("chosen", [P, 2] + CHOICES[1:])
        top = sb("top", CHOICES[:2])
        best = sb("best", CHOICES[:2])
        total = sb("total", CHOICES[:2])
        parts = sb("parts", [P, BT, 2, 2, HG1 * E1], F32R)
        gate_t = sb("gate_t", [P, 2, 2, BLOCK], F32R)
        gate = sb("gate", [P, 2, 2, BLOCK])
        hidden = sb("hidden", [P, RING, 2, BLOCK])
        gated = sb("gated", [P, 2, 2, BLOCK])
        gated1 = sb("gated1", [P, 2, BLOCK])

        ps_p = ps("ps_p", [P, BLOCK])
        ps_u = [ps(f"ps_u{i}", [P, 2, BLOCK]) for i in range(2)]
        ps_e = ps("ps_e", [P, 2, BLOCK])
        ps_o = ps("ps_o", [P, BT, D])

        s_w = sem("s_w")
        s_const = sem("s_const")
        s_xn = sem("s_xn")
        s_job = sem("s_job")
        s_job_done = sem("s_job_done")
        s_shifted = sem("s_shifted")
        s_exp = sem("s_exp")
        s_up = sem("s_up")
        s_hid = sem("s_hid")
        s_down = sem("s_down")
        s_read = sem("s_read")
        s_gated = sem("s_gated")
        s_parts = sem("s_parts")
        s_place = sem("s_place")
        s_heads = sem("s_heads")
        s_wo = sem("s_wo")
        s_x4 = sem("s_x4")
        s_dve = sem("s_dve")
        s_dve_x = sem("s_dve_x")
        s_out = sem("s_out")

        PREPARE = {1: ("turn", 0), 2: ("project", 0), 5: ("logit", 0), 6: ("place_up", 0), 9: ("place_up", 1),
                   10: ("place_up", 2), 13: ("place_up", 3), 29: ("turn_gate", 0), 30: ("turn_gate", 1)}
        NPREP = len(PREPARE)
        GATES = {4 * v + 3 * s: ("place_gate", (v, s)) for v in range(QUADS) for s in range(2)}
        NGATE = len(GATES)
        EXP_AT, SPLIT_AT = 7, 27
        CHOOSE_AT = {9: (0,), 11: (1,), 12: (2,), 13: (3,), 15: (4,), 16: (5,), 17: (6, 7), 19: (8,), 20: (9,),
                     21: (10, 11), 23: (12,), 24: (13,), 25: (14, 15)}

        def timetable(entries):
            return {u % UNITS: (what, u >= UNITS) for u, what in entries}

        DOWN_AT = timetable((4 * v + 5 + s, (v, s)) for v in range(QUADS) for s in range(2))
        GATING_AT = timetable((4 * v + 6, v) for v in range(QUADS))
        OUT_AT = timetable((8 * hp + 15 + (0, 1, 4, 5)[n], (hp, n)) for hp in range(HP) for n in range(4))
        X_AT = 13
        HEADS_AT = 4

        def jobs(last):
            at = {**GATES, **({} if last else PREPARE)}
            return {u: (n, at[u]) for n, u in enumerate(sorted(at))}

        def jobs_before(k):
            return NPREP + (NPREP + NGATE) * k

        with nc.Block() as block:
            @block.sync
            def _(sp):
                for to, name in ((wm, "Wm"), (bm, "bm"), (emb, "emb"), (w_up, "w_up"), (b_up, "b_up"), (part, "part"),
                                 (w_down, "w_down"), (b_down, "b_down"), (wo, "wo")):
                    sp.dma_start(to[:], io["L1_ffn_" + name]).then_inc(s_w, 16)
                sp.dma_start(bo[:], io["L1_ffn_bo"].partition_broadcast(P)).then_inc(s_w, 16)
                sp.dma_start(order[:], io["order1"].partition_broadcast(P)).then_inc(s_w, 16)
                sp.dma_start(hidden[:, 0, :, :].rearrange("p a b -> p (a b)"),
                             io["place_t"].rearrange("p a b c -> p (a b c)")).then_inc(s_w, 16)
                sp.dma_start(hidden[:, 1, :, :].rearrange("p a b -> p (a b)"),
                             io["place_g"].rearrange("p a b c -> p (a b c)")).then_inc(s_w, 16)
                with sp.Fori(0, BLOCKS) as k:
                    sp.wait_ge(s_x4, k + 1)
                    sp.dma_start(out_rows[:, bass.ds(k * BT, BT), :],
                                 x_sb[:, bass.ds(k * BT, BT), :]).then_inc(s_out, 16)
                sp.wait_ge(s_out, 16 * BLOCKS)
            W_ALL = 16 * 13

            @block.tensor
            def _(pe):
                T = nc.tensor

                def job(p, parity, n, kind, arg):
                    wait(pe, s_job_done, n)
                    if kind == "turn":
                        pe.wait_ge(s_xn, BT * (p + 1))
                        for i in range(BT):
                            m = T.transpose(ps_p[:, i * P:(i + 1) * P], xn[:, i, :], ident[:])
                    elif kind == "project":
                        m = T.matmul(ps_p[:], wm[:], xt[:], start=True, stop=True)
                    elif kind == "place_up":
                        pe.wait_ge(s_heads, p + 1)
                        T.matmul(ps_p[:], place_t[:, 0, arg, :], h_hi[:], start=True, stop=False)
                        m = T.matmul(ps_p[:], place_t[:, 1, arg, :], h_lo[:], start=False, stop=True)
                    elif kind == "logit":
                        for i in range(BT):
                            m = T.matmul(ps_p[:, i * P:(i + 1) * P], h_t[:, i * P:(i + 1) * P], emb[:],
                                         start=True, stop=True)
                    elif kind == "turn_gate":
                        pe.wait_ge(s_parts, p + 1)
                        for i in range(BT):
                            m = T.transpose(ps_p[:, i * P:(i + 1) * P],
                                            parts[:, i, arg].rearrange("p a e -> p (a e)").bitcast(F32), ident[:])
                    else:
                        v, s = arg
                        half, h = divmod(v // EG * 2 + s, HG1)
                        m = T.matmul(ps_p[:], place_g[:, h, v % EG, :], gate_t[:, parity, half, :],
                                     start=True, stop=True)
                    m.then_inc(s_job, 1)

                def up(k, parity, u):
                    hp, pair = divmod(u, PAIRS)
                    wait(pe, s_hid, UNITS * k + u - 1)
                    for s in range(2):
                        m = T.matmul(ps_u[u % 2][:, s, :], w_up_r[:, s, pair, :], up_in[:, parity, hp, :],
                                     start=True, stop=True)
                    m.then_inc(s_up, 1)

                def down(k, v, s):
                    if s == 0:
                        pe.wait_ge(s_hid, UNITS * k + 4 * v + 4)
                        wait(pe, s_read, QUADS * k + v)
                    for i in range(4):
                        m = T.matmul(ps_e[32 * i:32 * i + 32, s, :], w_down[:, v % EG * 4 + i, :],
                                     hidden[:, (4 * v + i) % RING, s, :], start=True, stop=True)
                    if s == 1:
                        m.then_inc(s_down, 1)

                def out(k, hp, n):
                    if n == 0:
                        pe.wait_ge(s_gated, HP * k + hp + 1)
                        if hp == 0:
                            wait(pe, s_dve_x, k)
                    s, second = divmod(n, 2)
                    for i in (2 * second, 2 * second + 1):
                        m = T.matmul(ps_o[:, i, :], gated[:, hp % 2, s, i * P:(i + 1) * P], wo[:, hp * 2 + s, :],
                                     start=(hp == 0 and s == 0 and i == 0), stop=(hp == HP - 1 and s == 1),
                                     skip_group_check=True)
                    if n == 3:
                        m.then_inc(s_wo, 1)

                def experts(k, parity, last, turn):
                    first = isinstance(k, int) and k == 0
                    at = jobs(last)
                    pe.wait_ge(s_job_done, jobs_before(k))
                    for u in range(UNITS):
                        up(k, parity, u)
                        if u in at:
                            n, (kind, arg) = at[u]
                            if kind == "place_gate":
                                job(k, parity, jobs_before(k) + n, kind, arg)
                            else:
                                job(k + 1, 1 - parity, jobs_before(k) + n, kind, arg)
                        for table, visit in ((DOWN_AT, down), (OUT_AT, out)):
                            if u in table:
                                what, of_before = table[u]
                                if not of_before:
                                    visit(k, *what)
                                elif not first:
                                    visit(k - 1, *what)

                pe.wait_ge(s_w, W_ALL)
                pe.wait_ge(s_place, 2)
                for n, u in enumerate(sorted(PREPARE)):
                    job(0, 0, n, *PREPARE[u])
                pe.wait_ge(s_const, 2)
                rounds(pe, BLOCKS, experts)
                pe.wait_ge(s_job_done, jobs_before(BLOCKS - 1) + NGATE)
                for s in range(2):
                    down(BLOCKS - 1, QUADS - 1, s)
                for hp, n in (what for what, of_before in OUT_AT.values() if of_before):
                    out(BLOCKS - 1, hp, n)

            @block.scalar
            def _(act):
                norm.root(nc, act)
                act.wait_ge(s_w, W_ALL)
                for to, at in ((place_t[:].rearrange("p a b c -> p (a b c)"), 0),
                               (place_g[:].rearrange("p a b c -> p (a b c)"), 1)):
                    nc.scalar.copy(to, hidden[:, at, :, :].rearrange("p a b -> p (a b)")).then_inc(s_place, 1)
                act.wait_ge(s_place, 2)

                def exponent(p):
                    act.wait_ge(s_shifted, p + 1)
                    nc.scalar.activation(weight[:], weight[:], ACT.Exp).then_inc(s_exp, 1)

                def gelus(k, parity, last, turn):
                    for u in range(UNITS):
                        act.wait_ge(s_up, UNITS * k + u + 1)
                        wait(act, s_down, QUADS * k + u // 4 - 1)
                        nc.scalar.activation(hidden[:, u % RING, :, :], ps_u[u % 2][:], ACT.Gelu,
                                             bias=b_up[:, u % PAIRS:u % PAIRS + 1]).then_inc(s_hid, 1)
                        if u == EXP_AT and not last:
                            exponent(k + 1)

                exponent(0)
                rounds(act, BLOCKS, gelus)

            @block.gpsimd
            def _(pool):
                G = nc.gpsimd
                pool.wait_ge(s_w, W_ALL)

                def add_groups(k, hp):
                    pool.wait_ge(s_read, QUADS * k + EG * (hp + 1))
                    to = gated[:, hp % 2]
                    G.tensor_tensor(to, to, gated1[:], ALU.add).then_inc(s_gated, 1)

                def add_bias(k):
                    pool.wait_ge(s_dve_x, k + 1)
                    to = x_sb[:, bass.ds(BT * k, BT), :]
                    G.tensor_tensor(to, to, bo[:].unsqueeze(1).to_broadcast([P, BT, D]), ALU.add).then_inc(s_x4, 1)

                add_groups(0, 0)
                add_groups(0, 1)
                add_groups(0, 2)
                with pool.Fori(1, BLOCKS) as k:
                    add_groups(k - 1, HP - 1)
                    add_groups(k, 0)
                    add_bias(k - 1)
                    for hp in range(1, HP - 1):
                        add_groups(k, hp)
                add_groups(BLOCKS - 1, HP - 1)
                add_bias(BLOCKS - 1)

            @block.vector
            def _(dve):
                chain = Chain(dve, s_dve)
                V = nc.vector
                norm.statistics(nc, dve, chain, x_sb)
                setup = chain.n
                dve.wait_ge(s_w, W_ALL)

                def job(p, parity, n, kind, arg):
                    dve.wait_ge(s_job, n + 1)
                    if kind == "turn":
                        done = V.tensor_copy(xt[:], ps_p[:])
                    elif kind == "project":
                        done = V.tensor_scalar(h_t[:], ps_p[:], bm[:], None, ALU.add)
                    elif kind == "place_up":
                        done = V.tensor_copy(up_in[:, parity, arg, :], ps_p[:])
                    elif kind == "logit":
                        logits = ps_p[:].rearrange("p (a e) -> p a e", e=E1)
                        chain.step(V.tensor_reduce(top[:], logits, AX, ALU.max))
                        wait(dve, s_parts, p)
                        V.tensor_tensor(weight[:], logits, top[:].unsqueeze(2).to_broadcast(CHOICES),
                                        ALU.subtract).then_inc(s_shifted, 1)
                        dve.wait_ge(s_shifted, p + 1)
                        done = V.tensor_copy(top[:, 0:1], top[:, 0:1])
                    elif kind == "turn_gate":
                        done = V.tensor_copy(gate_t[:, parity, arg, :], ps_p[:])
                    else:
                        v, s = arg
                        done = V.tensor_copy(gate[:, v % 2, s, :], ps_p[:])
                    done.then_inc(s_job_done, 1)

                def normalize(p):
                    for i in range(BT):
                        norm.apply(nc, x_sb, BT * p + i, xn[:, i, :]).then_inc(s_xn, 1)

                def split_heads(p, n):
                    dve.wait_ge(s_job_done, n + 1)
                    chain.step(V.tensor_copy(h_hi[:], h_t[:]))
                    V.tensor_tensor(h_lo[:], h_t[:], h_hi[:].bitcast(F32), ALU.subtract).then_inc(s_heads, 1)

                def split_gates(p, n):
                    wait(dve, s_job, n)
                    chain.settle()
                    w = weight[:].rearrange("p (t q h) e -> p t q (h e)", t=BT, q=2)
                    chain.step(V.tensor_copy(parts[:, :, :, 0, :], w))
                    V.tensor_tensor(parts[:, :, :, 1, :], w, parts[:, :, :, 0, :].bitcast(F32),
                                    ALU.subtract).then_inc(s_parts, 1)

                def bc(small):
                    return small.unsqueeze(2).to_broadcast(CHOICES)

                def choose(p, step):
                    if step == 0:
                        dve.wait_ge(s_exp, p + 1)
                        chain.mark(V.tensor_reduce(total[:], weight[:], AX, ALU.add))
                        return
                    chain.settle()
                    r, kind = divmod(step - 3, 6)
                    if step == 1:
                        ins = V.reciprocal(total[:], total[:])
                    elif step == 2:
                        ins = V.tensor_tensor(weight[:], weight[:], bc(total[:]), ALU.mult)
                    elif step == 14:
                        ins = V.tensor_tensor(chosen[:, 0], chosen[:, 0], chosen[:, 1], ALU.add)
                    elif step == 15:
                        ins = V.tensor_tensor(weight[:], weight[:], chosen[:, 0], ALU.mult)
                    elif kind == 0:
                        ins = V.tensor_reduce(best[:], (weight if r == 0 else left)[:], AX, ALU.max)
                    elif kind == 1:
                        ins = V.tensor_tensor(hit[:], (weight if r == 0 else left)[:], bc(best[:]), ALU.is_equal)
                    elif kind == 2:
                        ins = V.tensor_tensor(hit[:], hit[:], order[:].unsqueeze(1).to_broadcast(CHOICES), ALU.mult)
                    elif kind == 3:
                        ins = V.tensor_reduce(best[:], hit[:], AX, ALU.max)
                    elif kind == 4:
                        ins = V.tensor_tensor(chosen[:, r], hit[:], bc(best[:]), ALU.is_equal)
                    else:
                        ins = V.scalar_tensor_tensor(left[:], chosen[:, 0], -2.0, weight[:], ALU.mult, ALU.add)
                    chain.mark(ins)
                CHOICE_STEPS = 16
                STEPS = 1 + 1 + 1 + CHOICE_STEPS

                def gating(k, parity, v):
                    dve.wait_ge(s_down, QUADS * k + v + 1)
                    if v % EG == 0:
                        wait(dve, s_wo, HP * k + v // EG - 1)
                        to = gated[:, v // EG % 2]
                    else:
                        wait(dve, s_gated, HP * k + v // EG)
                        to = gated1[:]
                    V.scalar_tensor_tensor(to, ps_e[:], b_down[:, v % EG:v % EG + 1], gate[:, v % 2],
                                           ALU.add, ALU.mult).then_inc(s_read, 1)

                def add_to_stream(k):
                    dve.wait_ge(s_wo, HP * (k + 1))
                    to = x_sb[:, bass.ds(BT * k, BT), :]
                    V.tensor_tensor(to, to, ps_o[:], ALU.add).then_inc(s_dve_x, 1)

                def experts(k, parity, last, turn):
                    first = isinstance(k, int) and k == 0
                    at = jobs(last)
                    chain.at(setup + STEPS * (k + 1))
                    for u in range(UNITS):
                        if u in at:
                            n, (kind, arg) = at[u]
                            if kind == "place_gate":
                                job(k, parity, jobs_before(k) + n, kind, arg)
                            else:
                                job(k + 1, 1 - parity, jobs_before(k) + n, kind, arg)
                        if u == 0 and not last:
                            normalize(k + 1)
                        if u == HEADS_AT and not last:
                            split_heads(k + 1, jobs_before(k) + at[2][0])
                        if u in GATING_AT:
                            v, of_before = GATING_AT[u]
                            if not of_before:
                                gating(k, parity, v)
                            elif not first:
                                gating(k - 1, 1 - parity, v)
                        if u in CHOOSE_AT and not last:
                            for step in CHOOSE_AT[u]:
                                choose(k + 1, step)
                        if u == SPLIT_AT and not last:
                            split_gates(k + 1, jobs_before(k))
                        if u == X_AT and not first:
                            add_to_stream(k - 1)
                    if not last:
                        assert chain.n == STEPS, chain.n

                chain.at(setup)
                for n, u in enumerate(sorted(PREPARE)):
                    if n == 0:
                        normalize(0)
                    if n == 2:
                        split_heads(0, 1)
                    if PREPARE[u] == ("turn_gate", 0):
                        for step in range(CHOICE_STEPS):
                            choose(0, step)
                        split_gates(0, 0)
                    job(0, 0, n, *PREPARE[u])
                    if n == 0:
                        flat = w_up[:].rearrange("p s e i -> p (s e i)")
                        both = w_up_r[:].rearrange("p s e i -> p (s e i)")
                        V.tensor_copy(both, flat).then_inc(s_const, 1)
                        dve.wait_ge(s_const, 1)
                        V.scalar_tensor_tensor(both, both.bitcast(F32), part[:], flat, ALU.mult,
                                               ALU.add).then_inc(s_const, 1)
                rounds(dve, BLOCKS, experts)
                gating(BLOCKS - 1, 1, QUADS - 1)
                add_to_stream(BLOCKS - 1)


_OUT = "out"


def kernel(**inputs):
    import concourse.bacc as bacc
    from concourse.bass_utils import run_bass_kernel_spmd

    arrays, shape = lay_out(inputs)
    nc = bacc.Bacc("TRN2", target_bir_lowering=False, num_devices=1)
    io = {n: nc.dram_tensor(n + "_dram", a.shape, mybir.dt.from_np(a.dtype), kind="ExternalInput").ap()
          for n, a in arrays.items()}
    io[_OUT] = nc.dram_tensor("out_dram", (TOKENS, D), F32, kind="ExternalOutput").ap()
    program(nc, io)
    r = run_bass_kernel_spmd(nc, [{n + "_dram": a for n, a in arrays.items()}], core_ids=[0])
    return r.results[0]["out_dram"].reshape(shape)


def lay_out(inputs):
    c = np.ascontiguousarray
    x = np.asarray(inputs["x"])
    a = {"x": c(x.reshape(TOKENS, D))}
    ctx = np.asarray(inputs["ctx_1024"])
    a["ctx"] = c(ctx.reshape(BATCH * CTX, D))
    a["pointers"] = c(np.asarray(inputs["itok_BxS_0_4092"]).reshape(TILES, P).T)
    a["ids"] = c(np.asarray(inputs["itok_BxS_0_7"]).reshape(TOKENS))
    a["positions"] = np.arange(IDS, dtype=np.float32)
    a["identity"] = np.eye(P, dtype=np.float32)
    for n in ("Wqj", "Wkj", "Wvj", "Wqi", "Wki", "Wvi"):
        a["L0_xattn_" + n] = c(np.asarray(inputs["L0_xattn_" + n]))
    a["L0_xattn_WoutT"] = c(np.asarray(inputs["L0_xattn_Wout"]).T)
    a["L0_xattn_gain"] = c(np.asarray(inputs["L0_xattn_gain"]).reshape(1))
    a["L0_xattn_council_weights"] = c(np.asarray(inputs["L0_xattn_council_weights"]))

    def get(name):
        return np.asarray(inputs[name])

    a["L0_ffn_w_up"] = c(np.concatenate([get("L0_ffn_W1"), get("L0_ffn_Ws1")[None]]).transpose(2, 0, 1))
    down = np.concatenate([get("L0_ffn_W2"), get("L0_ffn_Ws2")[None]])
    a["L0_ffn_w_down"] = c(down.reshape(GROUPS0, D, CH, P).transpose(3, 0, 2, 1))
    a["L0_ffn_b_up"] = c(np.concatenate([get("L0_ffn_b1"), get("L0_ffn_bs1")[None]]).reshape(GROUPS0 * CH, P).T)
    a["L0_ffn_b_down"] = c(np.concatenate([get("L0_ffn_b2"), get("L0_ffn_bs2")[None]]))
    a["L0_ffn_WgT"] = c(get("L0_ffn_Wg").T)
    a["L0_ffn_bg"], a["L0_ffn_bias"] = c(get("L0_ffn_bg")), c(get("L0_ffn_bias"))
    a["order0"] = np.arange(EXPERTS0, 0, -1, dtype=np.float32)

    ctx = ctx.reshape(BATCH, CTX, D)
    a["ctx_t"] = c(ctx.transpose(0, 2, 1))
    for n in ("Wq", "Wk", "Wv"):
        a["L1_xattn_" + n] = c(get("L1_xattn_" + n))
    a["L1_xattn_bqk"] = c(np.stack([get("L1_xattn_bq"), get("L1_xattn_bk")], axis=1))
    a["L1_xattn_bv"], a["L1_xattn_bo"] = c(get("L1_xattn_bv")), c(get("L1_xattn_bo"))
    strips = np.zeros((HG, 32, GROUPS, D), np.float32)
    strips[:, 0:DK] = get("L1_xattn_Wo").reshape(GROUPS, HG, DK, D).transpose(1, 2, 0, 3)
    a["L1_xattn_Wo_strips"] = strips.reshape(P, GROUPS, D)
    mask = np.zeros((P, HG), np.float32)
    place = np.zeros((P, 2, GROUPS, P), np.float32)
    place_m = np.zeros((HEADS, GROUPS, P), np.float32)
    for h in range(HEADS):
        g, j = divmod(h, HG)
        place_m[h, g, SHIFT_ROW + j] = 1
        mask[SHIFT_ROW + j, j] = 1
        for d in range(DK):
            for product, part in enumerate((0, 1, 0)):
                row = 32 * product + DK * j + d
                place[h * DK + d, part, g, row] = 1
                mask[row, j] = 1
    a["head_mask"] = mask
    a["place"], a["place_m"] = place, place_m
    a["head_sum"] = np.repeat(np.eye(HEADS, dtype=np.float32), DK, axis=0)

    blank = np.zeros
    f = np.float32
    a["L1_ffn_Wm"], a["L1_ffn_bm"] = c(get("L1_ffn_Wm")), c(get("L1_ffn_bm")[:, None])
    emb, emb_bd = get("L1_ffn_expert_emb"), blank((H1, HD1, H1, E1), f)
    w1, w_up = get("L1_ffn_W1").reshape(PAIRS, 2, HD1, I1), blank((2, 4, HD1, 2, PAIRS, 2, I1), f)
    w2, w_down = get("L1_ffn_W2").reshape(PAIRS, 2, I1, HD1), blank((2, I1, PAIRS, 2, HD1), f)
    place_t, place_g = blank((H1, HD1, 2, HP, 2, 4, HD1), f), blank((2, H1 // 2, E1, H1 // 2, 2, E1 // 2, HD1), f)
    for h in range(H1):
        emb_bd[h, :, h] = emb
        for d in range(HD1):
            for product in range(4):
                place_t[h, d, product % 2, h // 2, h % 2, product, d] = 1
        for e in range(E1):
            place_g[:, h % (H1 // 2), e, h % (H1 // 2), e // 8, e % 8, :] = 1
    for s in range(2):
        for product in range(4):
            w_up[s, product, :, s] = w1.transpose(2, 0, 1, 3)
        w_down[s, :, :, s] = w2[:, s].transpose(1, 0, 2)
    a["L1_ffn_emb"] = emb_bd.reshape(P, P)
    a["L1_ffn_w_up"] = w_up.reshape(P, 2, PAIRS, P)
    a["L1_ffn_w_down"] = w_down.reshape(P, PAIRS, 32)
    a["place_t"], a["place_g"] = place_t.reshape(P, 2, HP, P), place_g.reshape(P, H1 // 2, 2, P)
    low = np.tile(np.repeat(np.array([0, 0, 1, 1], f), HD1), 2)
    a["L1_ffn_part"] = -low[:, None]
    a["L1_ffn_b_up"] = c(get("L1_ffn_b1").reshape(PAIRS, P).T)
    a["L1_ffn_b_down"] = c(get("L1_ffn_b2").reshape(2, P).T)
    a["L1_ffn_wo"] = c(np.tile(get("L1_ffn_Wo").reshape(H1, HD1, D).transpose(1, 0, 2), (8, 1, 1)))
    a["L1_ffn_bo"] = c(get("L1_ffn_bo"))
    a["order1"] = np.arange(E1, 0, -1, dtype=np.float32)
    return a, x.shape
```

```python
from contextlib import ExitStack

import numpy as np
import concourse.bass as bass
from concourse import mybir

F32 = mybir.dt.float32
F32R = mybir.dt.float32r
I32 = mybir.dt.int32
ALU = mybir.AluOpType
ACT = mybir.ActivationFunctionType
AX = mybir.AxisListType.X

P = 128
BATCH, SEQ, D = 16, 256, 128
CTX = 1601
TOKENS = BATCH * SEQ
TILES = TOKENS // P
BT = 4
BLOCK = BT * P
BLOCKS = TILES // BT
EPS = 1e-5

WIN = 3
IDS = 256
SCORE_SCALE0 = 1.0 / float(np.sqrt(float(D)))

EXPERTS0, HID0 = 8, 4 * D
GROUPS0 = EXPERTS0 + 1
CH = HID0 // P

HEADS, DK = 16, 8
HG = 4
GROUPS = HEADS // HG
KT = -(-CTX // P)
CTXP = KT * P
QT = SEQ // P
SCORE_SCALE1 = 1.0 / float(np.sqrt(DK))
SHIFT_ROW = 96
KCH = [(i, min(512, CTX - i)) for i in range(0, CTX, 512)]

H1, E1, HD1, I1 = 8, 16, 16, 64
PAIRS = E1 // 2
HP = H1 // 2


class Chain:

    def __init__(self, eng, sem):
        self.eng, self.sem, self.base, self.n = eng, sem, 0, 0

    def mark(self, ins):
        ins.then_inc(self.sem, 1)
        self.n += 1
        return ins

    def settle(self):
        self.eng.wait_ge(self.sem, self.base + self.n)

    def step(self, ins):
        self.mark(ins)
        self.settle()
        return ins

    def at(self, base):
        self.base, self.n = base, 0


def wait(eng, sem, value):
    if isinstance(value, int) and value <= 0:
        return
    eng.wait_ge(sem, value)


def rounds(eng, count, body):
    body(0, 0, False, 0)
    with eng.Fori(0, (count - 2) // 2) as i:
        body(2 * i + 1, 1, False, i)
        body(2 * i + 2, 0, False, i + 1)
    body(count - 1, 1, True, (count - 2) // 2)


def program(nc, io):
    with ExitStack() as top:
        x_sb = top.enter_context(nc.sbuf_tensor("x_sb", [P, TILES, D], F32))
        ident = top.enter_context(nc.sbuf_tensor("ident", [P, P], F32))
        norm_b, norm_c, norm_d = (Norm(top, nc, tag) for tag in "BCD")
        with ExitStack() as c_room:
            c_loads = HeadAttentionLoads(c_room, nc, io)
            with ExitStack() as b_room:
                b_loads = ExpertLoads(b_room, nc, io)
                gather_attention(nc, io, x_sb, ident, norm_b, b_loads)
                expert_layer(nc, io, x_sb, ident, norm_b, norm_c, b_loads, c_loads)
            head_attention(nc, io, x_sb, ident, norm_c, norm_d, c_loads)
        head_experts(nc, io, x_sb, ident, norm_d)


class Norm:

    def __init__(self, ctx, nc, tag):
        def sb(name, shape):
            return ctx.enter_context(nc.sbuf_tensor(f"{tag}_{name}", shape, F32))
        self.stats = sb("stats", [P, TILES, 6])
        self.mean = sb("mean", [P, TILES])
        self.var = sb("var", [P, TILES])
        self.std = sb("std", [P, TILES])
        self.tmp = sb("tmp", [P, TILES])
        self.rstd = sb("rstd", [P, TILES])
        self.taken = ctx.enter_context(nc.semaphore(f"{tag}_taken"))
        self.var_ready = ctx.enter_context(nc.semaphore(f"{tag}_var_ready"))
        self.std_ready = ctx.enter_context(nc.semaphore(f"{tag}_std_ready"))

    def take(self, nc, x_sb, t):
        nc.vector.bn_stats(self.stats[:, bass.ds(t, 1), :].rearrange("p a s -> p (a s)"),
                           x_sb[:, bass.ds(t, 1), :].rearrange("p a d -> p (a d)")).then_inc(self.taken, 1)

    def statistics(self, nc, dve, chain):
        dve.wait_ge(self.taken, TILES)
        st = self.stats
        chain.mark(nc.vector.tensor_tensor(self.mean[:], st[:, :, 1], st[:, :, 4], ALU.add))
        chain.mark(nc.vector.tensor_tensor(self.tmp[:], st[:, :, 1], st[:, :, 4], ALU.subtract))
        chain.step(nc.vector.tensor_tensor(self.var[:], st[:, :, 2], st[:, :, 5], ALU.add))
        chain.mark(nc.vector.tensor_scalar(self.mean[:], self.mean[:], 0.5, None, ALU.mult))
        chain.mark(nc.vector.tensor_scalar(self.var[:], self.var[:], 1.0 / D, EPS, ALU.mult, ALU.add))
        chain.step(nc.vector.scalar_tensor_tensor(self.tmp[:], self.tmp[:], 0.25, self.tmp[:], ALU.mult, ALU.mult))
        chain.step(nc.vector.tensor_tensor(self.var[:], self.var[:], self.tmp[:], ALU.add))
        nc.vector.tensor_scalar(self.tmp[:], self.var[:], -0.5, None, ALU.mult).then_inc(self.var_ready, 1)
        dve.wait_ge(self.std_ready, 1)
        dve.wait_ge(self.var_ready, 1)
        chain.step(nc.vector.reciprocal(self.rstd[:], self.std[:]))
        chain.step(nc.vector.tensor_tensor(self.std[:], self.rstd[:], self.rstd[:], ALU.mult))
        chain.step(nc.vector.tensor_tensor(self.std[:], self.std[:], self.tmp[:], ALU.mult))
        chain.step(nc.vector.scalar_tensor_tensor(self.rstd[:], self.std[:], 1.5, self.rstd[:], ALU.add, ALU.mult))

    def root(self, nc, act):
        act.wait_ge(self.var_ready, 1)
        nc.scalar.activation(self.std[:], self.var[:], ACT.Sqrt).then_inc(self.std_ready, 1)

    def apply(self, nc, x_sb, t, out):
        return nc.vector.tensor_scalar(out, x_sb[:, bass.ds(t, 1), :].rearrange("p a d -> p (a d)"),
                                       self.mean[:, bass.ds(t, 1)], self.rstd[:, bass.ds(t, 1)],
                                       ALU.subtract, ALU.mult)


def gather_attention(nc, io, x_sb, ident, norm_after, loads_after):
    with ExitStack() as ctx:
        def sb(name, shape, dt=F32):
            return ctx.enter_context(nc.sbuf_tensor("A_" + name, shape, dt))

        def ps(name, shape):
            return ctx.enter_context(nc.psum_tensor("A_" + name, shape, F32))

        def sem(name):
            return ctx.enter_context(nc.semaphore("A_" + name))

        DOTS = BT * 2 * WIN
        wq = sb("wq", [P, 2, D])
        wk = sb("wk", [P, 2, D])
        wv = sb("wv", [P, 2, D])
        wout = sb("wout", [P, D])
        gain = sb("gain", [P, 1])
        council = sb("council", [P, 2])
        ptr = sb("ptr", [P, TILES], I32)
        ids = sb("ids", [P, BATCH, IDS], I32)
        position = sb("position", [P, IDS])
        base = sb("base", [P, BATCH, QT], I32)
        index = sb("index", [P, TILES, WIN], I32)
        id_index = sb("id_index", [P, TILES])
        picked = sb("picked", [P, IDS])
        rel = sb("rel", [P, TILES])
        window = sb("window", [P, TILES, WIN, D])
        g_sb = sb("g", [P, 2, D])
        m_sb = sb("m", [P, 2, D])
        cw = sb("cw", [P, 8])
        xn = sb("xn", [P, 2, BT, D])
        xt = sb("xt", [P, 2, BT, P])
        junk = sb("junk", [P, DOTS, D])
        raw = sb("raw", [P, 2, WIN, TILES])
        logic = sb("logic", [P, 12, TILES])
        probs = sb("probs", [P, 2, WIN, TILES])
        soft = sb("soft", [P, 3, 2, TILES])
        z = sb("z", [P, 2, BT, 2, D])
        zt = sb("zt", [P, 2, BT, 2, P])
        norm = Norm(ctx, nc, "A")

        ps_t = [ps(f"ps_t{i}", [P, BT, P]) for i in range(2)]
        ps_u = [ps(f"ps_u{i}", [P, 2, 2, D]) for i in range(4)]
        ps_o = [ps(f"ps_o{i}", [P, BT, D]) for i in range(2)]

        s_ptr = sem("s_ptr")
        s_x = sem("s_x")
        s_w = sem("s_w")
        s_base = sem("s_base")
        s_index = sem("s_index")
        s_window = [sem(f"s_window{k}") for k in range(BLOCKS)]
        s_gm = sem("s_gm")
        s_gm_used = sem("s_gm_used")
        s_cexp_in = sem("s_cexp_in")
        s_cexp = sem("s_cexp")
        s_xn = sem("s_xn")
        s_tr = sem("s_tr")
        s_xt = sem("s_xt")
        s_u = sem("s_u")
        s_dots = sem("s_dots")
        s_shifted = sem("s_shifted")
        s_exp = sem("s_exp")
        s_z = sem("s_z")
        s_ztr = sem("s_ztr")
        s_zt = sem("s_zt")
        s_o = sem("s_o")
        s_x1 = sem("s_x1")
        s_dve = sem("s_dve")

        ctx_rows = io["ctx"]
        HALF = BLOCKS // 2
        ORDER = [("queries", k) for k in range(HALF + 1)]
        for k in range(HALF):
            ORDER += [("output", k)] + ([("queries", HALF + 1 + k)] if k < HALF - 1 else [])
        ORDER += [("output", k) for k in range(HALF, BLOCKS)]
        with nc.Block() as block:
            @block.sync
            def _(sp):
                x_rows = io["x"].rearrange("(t p) d -> p t d", p=P)
                sp.dma_start(ptr[:], io["pointers"]).then_inc(s_ptr, 16)
                for h in range(2):
                    half = slice(h * TILES // 2, (h + 1) * TILES // 2)
                    sp.dma_start(x_sb[:, half, :], x_rows[:, half, :]).then_inc(s_x, 16)
                sp.dma_start(ident[:], io["identity"]).then_inc(s_w, 16)
                for i, n in enumerate("ji"):
                    sp.dma_start(wq[:, i, :], io["L0_xattn_Wq" + n]).then_inc(s_w, 16)
                    sp.dma_start(wk[:, i, :], io["L0_xattn_Wk" + n]).then_inc(s_w, 16)
                    sp.dma_start(wv[:, i, :], io["L0_xattn_Wv" + n]).then_inc(s_w, 16)
                sp.dma_start(wout[:], io["L0_xattn_WoutT"]).then_inc(s_w, 16)
                sp.dma_start(gain[:], io["L0_xattn_gain"].partition_broadcast(P)).then_inc(s_w, 16)
                sp.dma_start(council[:], io["L0_xattn_council_weights"].partition_broadcast(P)).then_inc(s_w, 16)
                sp.dma_start(position[:], io["positions"].partition_broadcast(P)).then_inc(s_w, 16)
                sp.dma_start(ids[:].rearrange("p b i -> p (b i)"),
                             io["ids"].partition_broadcast(P)).then_inc(s_w, 16)
                loads_after.start(sp)
            W_ALL = 16 * 12

            @block.gpsimd
            def _(pool):
                nc.gpsimd.iota(base[:], [[CTX, BATCH], [0, QT]], base=0, channel_multiplier=0).then_inc(s_base, 1)
                pool.wait_ge(s_index, WIN)
                for t in range(TILES):
                    for w in range(WIN):
                        nc.gpsimd.indirect_dma_start(
                            window[:, t, w, :], None, ctx_rows,
                            bass.IndirectOffsetOnAxis(index[:, t, w:w + 1], axis=0)).then_inc(
                                s_window[t // BT], 16)

            @block.vector
            def _(dve):
                chain = Chain(dve, s_dve)
                dve.wait_ge(s_ptr, 16)
                dve.wait_ge(s_base, 1)
                for w in range(WIN):
                    chain.mark(nc.vector.tensor_scalar(index[:, :, w], ptr[:], float(w), 0.0, ALU.add, ALU.max))
                chain.mark(nc.vector.tensor_scalar(id_index[:], ptr[:], 0.0, float(IDS - 1), ALU.max, ALU.min))
                chain.settle()
                for w in range(WIN):
                    nc.vector.scalar_tensor_tensor(index[:, :, w], index[:, :, w], float(CTX - 1),
                                                   base[:].rearrange("p b q -> p (b q)"),
                                                   ALU.min, ALU.add).then_inc(s_index, 1)
                dve.wait_ge(s_x, 32)
                for t in range(TILES):
                    norm.take(nc, x_sb, t)
                norm.statistics(nc, dve, chain)
                dve.wait_ge(s_w, W_ALL)
                chain.step(nc.vector.tensor_tensor(cw[:, 0:1], council[:, 0:1], council[:, 1:2], ALU.max))
                nc.vector.tensor_scalar(cw[:, 1:3], council[:], cw[:, 0:1], None, ALU.subtract).then_inc(s_cexp_in, 1)
                dve.wait_ge(s_cexp, 1)
                chain.step(nc.vector.tensor_tensor(cw[:, 5:6], cw[:, 3:4], cw[:, 4:5], ALU.add))
                chain.step(nc.vector.reciprocal(cw[:, 6:7], cw[:, 5:6]))
                chain.step(nc.vector.tensor_tensor(cw[:, 6:7], cw[:, 6:7], gain[:], ALU.mult))
                chain.step(nc.vector.tensor_scalar(cw[:, 3:5], cw[:, 3:5], cw[:, 6:7], None, ALU.mult))
                dve.wait_ge(s_gm, 1)
                nc.vector.tensor_copy(g_sb[:], ps_o[0][:, 0:2, :]).then_inc(s_gm_used, 1)
                for i in range(2):
                    nc.vector.tensor_scalar(m_sb[:, i, :], ps_o[0][:, 2 + i, :], cw[:, 3 + i:4 + i], None,
                                            ALU.mult).then_inc(s_gm_used, 1)

                def normalize(k, parity):
                    wait(dve, s_tr, k - 1)
                    for i in range(BT):
                        norm.apply(nc, x_sb, k * BT + i, xn[:, parity, i, :]).then_inc(s_xn, 1)

                normalize(0, 0)

                def dots(k, parity):
                    if k < BLOCKS - 1:
                        normalize(k + 1, 1 - parity)
                    dve.wait_ge(s_window[k], 16 * WIN * BT)
                    wait(dve, s_dots, DOTS * k)
                    for i in range(BT):
                        t = k * BT + i
                        if i % 2 == 0:
                            dve.wait_ge(s_u, 2 * k + i // 2 + 1)
                        for q in range(2):
                            for w in range(WIN):
                                nc.vector.tensor_tensor_reduce(
                                    junk[:, (i * 2 + q) * WIN + w, :], window[:, t, w, :],
                                    ps_u[2 * parity + i // 2][:, i % 2, q, :], SCORE_SCALE0, 0.0, ALU.mult, ALU.add,
                                    raw[:, q, w, t:t + 1]).then_inc(s_dots, 1)

                def pick_ids(k):
                    for t in range(k * BT, (k + 1) * BT):
                        chain.step(nc.vector.scalar_tensor_tensor(
                            picked[:], position[:], id_index[:, t:t + 1], ids[:, t // QT, :],
                            ALU.is_equal, ALU.mult, accum_out=rel[:, t:t + 1]))

                V = nc.vector

                def weigh(half):
                    dve.wait_ge(s_dots, DOTS * HALF * (half + 1))
                    tiles = slice(half * TILES // 2, (half + 1) * TILES // 2)
                    rule, value = [logic[:, i, tiles] for i in range(5)], [logic[:, 5 + i, tiles] for i in range(5)]
                    any_rule, keep = logic[:, 10, tiles], logic[:, 11, tiles]
                    l0, l1, l2 = (raw[:, 0, w, tiles] for w in range(WIN))
                    for c in range(5):
                        chain.mark(V.tensor_scalar(rule[c], rel[:, tiles], float(c), None, ALU.is_equal))
                    chain.mark(V.tensor_tensor(value[0], l1, l2, ALU.add))
                    chain.mark(V.tensor_tensor(value[1], l1, l2, ALU.max))
                    chain.mark(V.tensor_scalar(value[2], l1, -1.0, None, ALU.mult))
                    chain.mark(V.scalar_tensor_tensor(value[3], l1, -1.0, l2, ALU.mult, ALU.max))
                    chain.step(V.tensor_tensor(value[4], l1, l2, ALU.subtract))
                    chain.step(V.scalar_tensor_tensor(value[4], value[4], -1.0, value[4], ALU.mult, ALU.max))
                    chain.mark(V.tensor_tensor(any_rule, rule[0], rule[1], ALU.add))
                    for c in range(5):
                        chain.mark(V.tensor_tensor(value[c], rule[c], value[c], ALU.mult))
                    for c in range(2, 5):
                        chain.settle()
                        chain.mark(V.tensor_tensor(any_rule, any_rule, rule[c], ALU.add))
                    for c in range(1, 5):
                        chain.settle()
                        chain.mark(V.tensor_tensor(value[0], value[0], value[c], ALU.add))
                    chain.step(V.tensor_scalar(keep, any_rule, -1.0, 1.0, ALU.mult, ALU.add))
                    chain.step(V.tensor_tensor(l0, l0, keep, ALU.mult))
                    chain.step(V.tensor_tensor(value[0], value[0], any_rule, ALU.mult))
                    chain.step(V.tensor_tensor(l0, l0, value[0], ALU.add))
                    top_score, total, inverse = (soft[:, i, :, tiles] for i in range(3))
                    chain.step(V.tensor_tensor(top_score, raw[:, :, 0, tiles], raw[:, :, 1, tiles], ALU.max))
                    chain.step(V.tensor_tensor(top_score, top_score, raw[:, :, 2, tiles], ALU.max))
                    for w in range(WIN):
                        V.tensor_tensor(probs[:, :, w, tiles], raw[:, :, w, tiles], top_score, ALU.subtract).then_inc(s_shifted, 1)
                    dve.wait_ge(s_exp, half + 1)
                    chain.step(V.tensor_tensor(total, probs[:, :, 0, tiles], probs[:, :, 1, tiles], ALU.add))
                    chain.step(V.tensor_tensor(total, total, probs[:, :, 2, tiles], ALU.add))
                    chain.step(V.reciprocal(inverse, total))
                    for w in range(WIN):
                        chain.mark(V.tensor_tensor(probs[:, :, w, tiles], probs[:, :, w, tiles], inverse, ALU.mult))
                    chain.settle()

                def mixes(k, parity):
                    wait(dve, s_ztr, 2 * (k - 1))
                    for w in range(WIN):
                        for i in range(BT):
                            row = window[:, k * BT + i, w, :]
                            for q in range(2):
                                to, weight = z[:, parity, i, q, :], probs[:, q, w, k * BT + i:k * BT + i + 1]
                                if w == 0:
                                    chain.mark(V.tensor_scalar(to, row, weight, None, ALU.mult))
                                else:
                                    ins = V.scalar_tensor_tensor(to, row, weight, to, ALU.mult, ALU.add)
                                    chain.mark(ins) if w < WIN - 1 else ins.then_inc(s_z, 1)
                        if w < WIN - 1:
                            chain.settle()

                def add_to_stream(k, parity):
                    dve.wait_ge(s_o, k + 1)
                    to = x_sb[:, k * BT:(k + 1) * BT, :]
                    V.tensor_tensor(to, to, ps_o[parity][:], ALU.add).then_inc(s_x1, 1)
                    dve.wait_ge(s_x1, k + 1)
                    for t in range(k * BT, (k + 1) * BT):
                        norm_after.take(nc, x_sb, t)

                for k in range(BLOCKS):
                    if k >= HALF:
                        mixes(k - HALF, k % 2)
                        if k > HALF:
                            add_to_stream(k - HALF - 1, 1 - k % 2)
                    dots(k, k % 2)
                    pick_ids(k)
                    if k == HALF - 1:
                        weigh(0)
                weigh(1)
                for k in range(HALF, BLOCKS):
                    mixes(k, k % 2)
                    add_to_stream(k - 1, 1 - k % 2)
                add_to_stream(BLOCKS - 1, 1)

            @block.scalar
            def _(act):
                norm.root(nc, act)
                act.wait_ge(s_cexp_in, 1)
                nc.scalar.activation(cw[:, 3:5], cw[:, 1:3], ACT.Exp).then_inc(s_cexp, 1)

                def exponent(half):
                    act.wait_ge(s_shifted, WIN * (half + 1))
                    tiles = slice(half * TILES // 2, (half + 1) * TILES // 2)
                    nc.scalar.activation(probs[:, :, :, tiles], probs[:, :, :, tiles], ACT.Exp).then_inc(s_exp, 1)

                for kind, k in ORDER:
                    parity = k % 2
                    if kind == "queries":
                        act.wait_ge(s_tr, k + 1)
                        nc.scalar.copy(xt[:, parity, :, :], ps_t[parity][:]).then_inc(s_xt, 1)
                        continue
                    if k % HALF == 0:
                        exponent(k // HALF)
                    for half in range(2):
                        act.wait_ge(s_ztr, 2 * k + half + 1)
                        nc.scalar.copy(zt[:, parity, 2 * half:2 * half + 2, :, :].rearrange("p i q t -> p (i q) t"),
                                       ps_t[half][:]).then_inc(s_zt, 1)

            @block.tensor
            def _(pe):
                pe.wait_ge(s_w, W_ALL)
                for i in range(2):
                    nc.tensor.matmul(ps_o[0][:, i, :], wq[:, i, :], wk[:, i, :], start=True, stop=True)
                for i in range(2):
                    last_product = nc.tensor.matmul(ps_o[0][:, 2 + i, :], wv[:, i, :], wout[:], start=True, stop=True)
                last_product.then_inc(s_gm, 1)

                def queries(k, parity):
                    pe.wait_ge(s_xn, BT * (k + 1))
                    for i in range(BT):
                        tr = nc.tensor.transpose(ps_t[parity][:, i, :], xn[:, parity, i, :], ident[:])
                    tr.then_inc(s_tr, 1)
                    pe.wait_ge(s_xt, k + 1)
                    if k == 0:
                        pe.wait_ge(s_gm_used, 1)
                    wait(pe, s_dots, DOTS * (k - 1))
                    for half in range(2):
                        for i in range(2):
                            u = nc.tensor.matmul(ps_u[2 * parity + half][:, i, :, :], xt[:, parity, 2 * half + i, :],
                                                 g_sb[:], start=True, stop=True)
                        u.then_inc(s_u, 1)

                def output(k, parity):
                    for half in range(2):
                        pe.wait_ge(s_z, 2 * BT * k + 4 * half + 4)
                        for i in range(4):
                            tr = nc.tensor.transpose(ps_t[half][:, i, :], z[:, parity, 2 * half + i // 2, i % 2, :],
                                                     ident[:])
                        tr.then_inc(s_ztr, 1)
                    pe.wait_ge(s_zt, 2 * k + 2)
                    if k == 0:
                        pe.wait_ge(s_gm_used, 3)
                    for i in range(BT):
                        for q in range(2):
                            o = nc.tensor.matmul(ps_o[parity][:, i, :], zt[:, parity, i, q, :], m_sb[:, q, :],
                                                 start=(q == 0), stop=(q == 1))
                    o.then_inc(s_o, 1)

                for kind, k in ORDER:
                    (queries if kind == "queries" else output)(k, k % 2)


class ExpertLoads:

    def __init__(self, ctx, nc, io):
        def sb(name, shape):
            return ctx.enter_context(nc.sbuf_tensor("B_" + name, shape, F32))
        self.io = io
        self.w_up = sb("w_up", [P, GROUPS0, HID0])
        self.w_down = sb("w_down", [P, GROUPS0, CH, D])
        self.b_up = sb("b_up", [P, GROUPS0 * CH])
        self.b_down = sb("b_down", [GROUPS0, D])
        self.w_gate = sb("w_gate", [P, EXPERTS0])
        self.b_gate = sb("b_gate", [P, 2, EXPERTS0])
        self.order = sb("order", [P, EXPERTS0])
        self.s_w = ctx.enter_context(nc.semaphore("B_s_w"))
        self.s_w_down = ctx.enter_context(nc.semaphore("B_s_w_down"))
        self.all = 16 * 7

    def start(self, sp):
        io, s_w = self.io, self.s_w
        for to, name in ((self.w_gate[:], "WgT"), (self.b_up[:], "b_up"), (self.b_down[:], "b_down"),
                         (self.w_up[:], "w_up")):
            sp.dma_start(to, io["L0_ffn_" + name]).then_inc(s_w, 16)
        for i, name in enumerate(("bg", "bias")):
            sp.dma_start(self.b_gate[:, i, :], io["L0_ffn_" + name].partition_broadcast(P)).then_inc(s_w, 16)
        sp.dma_start(self.order[:], io["order0"].partition_broadcast(P)).then_inc(s_w, 16)
        sp.dma_start(self.w_down[:], io["L0_ffn_w_down"]).then_inc(self.s_w_down, 16)


def expert_layer(nc, io, x_sb, ident, norm, norm_after, loads, loads_after):
    with ExitStack() as ctx:
        def sb(name, shape, dt=F32):
            return ctx.enter_context(nc.sbuf_tensor("B_" + name, shape, dt))

        def ps(name, shape):
            return ctx.enter_context(nc.psum_tensor("B_" + name, shape, F32))

        def sem(name):
            return ctx.enter_context(nc.semaphore("B_" + name))

        w_up, w_down, b_up, b_down = loads.w_up, loads.w_down, loads.b_up, loads.b_down
        w_gate, b_gate, order = loads.w_gate, loads.b_gate, loads.order
        s_w, W_ALL, s_w_down = loads.s_w, loads.all, loads.s_w_down
        w_up_hi = sb("w_up_hi", [P, GROUPS0, HID0], F32R)
        w_up_lo = sb("w_up_lo", [P, GROUPS0, HID0], F32R)
        xn = sb("xn", [P, 2, BT, D])
        xt = sb("xt", [P, BT, P])
        xt_hi = sb("xt_hi", [P, 2, BT, P], F32R)
        xt_lo = sb("xt_lo", [P, 2, BT, P], F32R)
        score = sb("score", [P, BT, EXPERTS0])
        left = sb("left", [P, BT, EXPERTS0])
        best = sb("best", [P, BT])
        hit = sb("hit", [P, BT, EXPERTS0])
        chosen = sb("chosen", [P, 2, BT, EXPERTS0])
        gate = sb("gate", [P, 2, BT, GROUPS0])
        gate_t = sb("gate_t", [GROUPS0, 2, BLOCK])
        HB = 3
        hidden = sb("hidden", [P, HB, CH, BLOCK])
        acc = sb("acc", [P, BT, D])

        ps_t = ps("ps_t", [P, BT, P])
        ps_g = ps("ps_g", [P, BLOCK])
        ps_h = [ps(f"ps_h{i}", [P, BLOCK]) for i in range(CH)]
        ps_e = [ps(f"ps_e{i}", [P, BT, D]) for i in range(2)]

        s_xn = sem("s_xn")
        s_tr = sem("s_tr")
        s_xt = sem("s_xt")
        s_xt_hi = sem("s_xt_hi")
        s_parts = sem("s_parts")
        s_w_hi = sem("s_w_hi")
        s_w_lo = sem("s_w_lo")
        s_logit = sem("s_logit")
        s_z = sem("s_z")
        s_sig = sem("s_sig")
        s_gate = sem("s_gate")
        s_gtr = sem("s_gtr")
        s_gt = sem("s_gt")
        s_up = sem("s_up")
        s_hid = sem("s_hid")
        s_down = sem("s_down")
        s_acc = sem("s_acc")
        s_dve = sem("s_dve")
        s_x2 = sem("s_x2")

        UPS = GROUPS0 * CH
        with nc.Block() as block:
            @block.sync
            def _(sp):
                loads_after.start(sp)

            @block.tensor
            def _(pe):
                def turn_block(k, parity):
                    pe.wait_ge(s_xn, BT * (k + 1))
                    wait(pe, s_xt, k)
                    for i in range(BT):
                        tr = nc.tensor.transpose(ps_t[:, i, :], xn[:, parity, i, :], ident[:])
                    tr.then_inc(s_tr, 1)

                def logits(k, parity):
                    pe.wait_ge(s_xt, k + 1)
                    wait(pe, s_gt, k)
                    for i in range(BT):
                        lg = nc.tensor.matmul(ps_g[:, i * EXPERTS0:(i + 1) * EXPERTS0], xt[:, i, :],
                                              w_gate[:], start=True, stop=True)
                    lg.then_inc(s_logit, 1)

                def up(k, parity, e):
                    for c in range(CH):
                        u = e * CH + c
                        wait(pe, s_hid, UPS * k + u - CH + 1)
                        for n, (w, x) in enumerate(((w_up_hi, xt_hi), (w_up_hi, xt_lo), (w_up_lo, xt_hi))):
                            m = nc.tensor.matmul(ps_h[c][:], w[:, e, c * P:(c + 1) * P],
                                                 x[:, parity, :, :].rearrange("p i t -> p (i t)"),
                                                 start=(n == 0), stop=(n == 2))
                        m.then_inc(s_up, 1)

                def down(k, parity, e):
                    pe.wait_ge(s_hid, UPS * k + (e + 1) * CH)
                    if e == EXPERTS0:
                        pe.wait_ge(s_gt, k + 1)
                    wait(pe, s_acc, BT * (GROUPS0 * k + max(0, e - 1)))
                    for i in range(BT):
                        for c in range(CH):
                            dn = nc.tensor.matmul(ps_e[e % 2][:, i, :], hidden[:, e % HB, c, i * P:(i + 1) * P],
                                                  w_down[:, e, c, :], start=(c == 0),
                                                  stop=(c == CH - 1 and e < EXPERTS0))
                        if e == EXPERTS0:
                            dn = nc.tensor.matmul(ps_e[e % 2][:, i, :], gate_t[:, parity, i * P:(i + 1) * P],
                                                  b_down[:], start=False, stop=True)
                    dn.then_inc(s_down, 1)

                def experts(k, parity, last, turn):
                    first = isinstance(k, int) and k == 0
                    pe.wait_ge(s_parts, k + 1)
                    for e in range(GROUPS0):
                        if first:
                            pe.wait_ge(s_w_lo, e + 1)
                            if e == 1:
                                pe.wait_ge(s_w_down, 16)
                        up(k, parity, e)
                        if e > 0:
                            down(k, parity, e - 1)
                        elif not first:
                            down(k - 1, 1 - parity, GROUPS0 - 1)
                        if e == 3:
                            pe.wait_ge(s_gate, k + 1)
                            for i in range(BT):
                                tr = nc.tensor.transpose(ps_g[0:GROUPS0, i * P:(i + 1) * P],
                                                         gate[:, parity, i, :], ident[:])
                            tr.then_inc(s_gtr, 1)
                        if e == 5 and not last:
                            turn_block(k + 1, 1 - parity)
                        if e == 6 and not last:
                            logits(k + 1, 1 - parity)

                pe.wait_ge(s_w, W_ALL)
                turn_block(0, 0)
                logits(0, 0)
                rounds(pe, BLOCKS, experts)
                down(BLOCKS - 1, (BLOCKS - 1) % 2, GROUPS0 - 1)

            @block.scalar
            def _(act):
                norm.root(nc, act)

                def turned(k, parity):
                    act.wait_ge(s_tr, k + 1)
                    wait(act, s_logit, k)
                    wait(act, s_parts, k)
                    nc.scalar.copy(xt[:], ps_t[:]).then_inc(s_xt, 1)

                def sigmoid(k):
                    act.wait_ge(s_z, k + 1)
                    nc.scalar.activation(score[:], score[:], ACT.Sigmoid).then_inc(s_sig, 1)

                def gelus(k, parity, last, turn):
                    for e in range(GROUPS0):
                        wait(act, s_down, GROUPS0 * k + e - HB + 1)
                        for c in range(CH):
                            u = e * CH + c
                            act.wait_ge(s_up, UPS * k + u + 1)
                            nc.scalar.activation(hidden[:, e % HB, c, :], ps_h[c][:], ACT.Gelu,
                                                 bias=b_up[:, u:u + 1]).then_inc(s_hid, 1)
                        if e == 3:
                            act.wait_ge(s_gtr, k + 1)
                            nc.scalar.copy(gate_t[:, parity, :], ps_g[0:GROUPS0, :]).then_inc(s_gt, 1)
                        if e == 5 and not last:
                            turned(k + 1, 1 - parity)
                    if not last:
                        sigmoid(k + 1)

                turned(0, 0)
                sigmoid(0)
                rounds(act, BLOCKS, gelus)

            @block.gpsimd
            def _(pool):
                for e in range(GROUPS0):
                    pool.wait_ge(s_w_hi, e + 1)
                    nc.gpsimd.tensor_tensor(w_up_lo[:, e, :], w_up[:, e, :], w_up_hi[:, e, :].bitcast(F32),
                                            ALU.subtract).then_inc(s_w_lo, 1)

            @block.vector
            def _(dve):
                chain = Chain(dve, s_dve)
                V = nc.vector
                norm.statistics(nc, dve, chain)
                for parity in range(2):
                    chain.mark(V.memset(gate[:, parity, :, EXPERTS0:], 1.0))
                chain.settle()
                setup = chain.n
                dve.wait_ge(s_w, W_ALL)

                def normalize(k, parity):
                    wait(dve, s_tr, k - 1)
                    for i in range(BT):
                        norm.apply(nc, x_sb, k * BT + i, xn[:, parity, i, :]).then_inc(s_xn, 1)

                def scores(k):
                    dve.wait_ge(s_logit, k + 1)
                    chain.at(setup + STEPS * k)
                    for i in range(2):
                        src = ps_g[:, 0:BT * EXPERTS0].rearrange("p (i e) -> p i e", i=BT) if i == 0 else score[:]
                        ins = V.tensor_tensor(score[:], src, b_gate[:, i:i + 1, :].to_broadcast([P, BT, EXPERTS0]),
                                              ALU.add)
                        chain.step(ins) if i == 0 else ins.then_inc(s_z, 1)

                def gates(k, parity):
                    wide = [P, BT, EXPERTS0]
                    dve.wait_ge(s_sig, k + 1)
                    chain.at(setup + STEPS * k + 1)
                    for n in range(2):
                        src = score if n == 0 else left
                        chain.step(V.tensor_reduce(best[:], src[:], AX, ALU.max))
                        chain.step(V.tensor_tensor(hit[:], src[:], best[:].unsqueeze(2).to_broadcast(wide), ALU.is_equal))
                        chain.step(V.tensor_tensor(hit[:], hit[:], order[:].unsqueeze(1).to_broadcast(wide), ALU.mult))
                        chain.step(V.tensor_reduce(best[:], hit[:], AX, ALU.max))
                        chain.step(V.tensor_tensor(chosen[:, n], hit[:], best[:].unsqueeze(2).to_broadcast(wide), ALU.is_equal))
                        if n == 0:
                            chain.step(V.scalar_tensor_tensor(left[:], chosen[:, 0], -2.0, score[:], ALU.mult, ALU.add))
                    chain.step(V.tensor_tensor(chosen[:, 0], chosen[:, 0], chosen[:, 1], ALU.add))
                    V.tensor_tensor(gate[:, parity, :, 0:EXPERTS0], chosen[:, 0], score[:], ALU.mult).then_inc(s_gate, 1)
                    assert chain.n == STEPS - 1, chain.n
                    dve.wait_ge(s_gate, k + 1)
                STEPS = 1 + 5 * 2 + 1 + 1

                def split_inputs(k, parity):
                    dve.wait_ge(s_xt, k + 1)
                    V.tensor_copy(xt_hi[:, parity], xt[:]).then_inc(s_xt_hi, 1)
                    dve.wait_ge(s_xt_hi, k + 1)
                    V.tensor_tensor(xt_lo[:, parity], xt[:], xt_hi[:, parity].bitcast(F32),
                                    ALU.subtract).then_inc(s_parts, 1)

                def sums(k, parity, last, turn):
                    gates(k, parity)
                    for e in range(GROUPS0):
                        dve.wait_ge(s_down, GROUPS0 * k + e + 1)
                        if e > 0 or not (isinstance(k, int) and k == 0):
                            dve.wait_ge(s_acc, BT * (GROUPS0 * k + e))
                        if e == EXPERTS0:
                            V.tensor_tensor(acc[:], acc[:], ps_e[e % 2][:], ALU.add).then_inc(s_acc, BT)
                            dve.wait_ge(s_acc, BT * GROUPS0 * (k + 1))
                            to = x_sb[:, bass.ds(k * BT, BT), :]
                            V.tensor_tensor(to, to, acc[:], ALU.add).then_inc(s_x2, 1)
                            dve.wait_ge(s_x2, k + 1)
                            for i in range(BT):
                                norm_after.take(nc, x_sb, k * BT + i)
                            continue
                        for i in range(BT):
                            g = gate[:, parity, i, e:e + 1]
                            if e == 0:
                                ins = V.tensor_scalar(acc[:, i, :], ps_e[0][:, i, :], g, None, ALU.mult)
                            else:
                                ins = V.scalar_tensor_tensor(acc[:, i, :], ps_e[e % 2][:, i, :], g, acc[:, i, :],
                                                             ALU.mult, ALU.add)
                            ins.then_inc(s_acc, 1)
                        if e == 1 and not last:
                            normalize(k + 1, 1 - parity)
                        if e == 6 and not last:
                            split_inputs(k + 1, 1 - parity)
                        if e == 7 and not last:
                            scores(k + 1)

                normalize(0, 0)
                for e in range(GROUPS0):
                    V.tensor_copy(w_up_hi[:, e, :], w_up[:, e, :]).then_inc(s_w_hi, 1)
                split_inputs(0, 0)
                scores(0)
                rounds(dve, BLOCKS, sums)


class HeadAttentionLoads:

    def __init__(self, ctx, nc, io):
        def sb(name, shape):
            return ctx.enter_context(nc.sbuf_tensor("C_" + name, shape, F32))
        self.io = io
        self.weights = [sb(name, shape) for name, shape in (
            ("wq", [P, D]), ("wk", [P, D]), ("wv", [P, D]), ("wo", [P, GROUPS, D]), ("bqk", [P, 2]), ("bv", [P, D]),
            ("bo", [P, D]))]
        self.mask = sb("mask", [P, HG])
        self.head_sum = sb("head_sum", [P, HEADS])
        self.place_m = sb("place_m", [HEADS, GROUPS, P])
        self.ctx_t = sb("ctx_t", [P, 2, CTX])
        self.s_w = ctx.enter_context(nc.semaphore("C_s_w"))
        self.all = 16 * 10
        self.s_ctx = [ctx.enter_context(nc.semaphore(f"C_s_ctx{i}")) for i in range(2)]

    def start(self, sp):
        io, s_w = self.io, self.s_w
        wq, wk, wv, wo, bqk, bv, bo = self.weights
        for to, name in ((wq, "L1_xattn_Wq"), (wk, "L1_xattn_Wk"), (wv, "L1_xattn_Wv"), (wo, "L1_xattn_Wo_strips"),
                         (bqk, "L1_xattn_bqk"), (self.mask, "head_mask"), (self.head_sum, "head_sum"),
                         (self.place_m, "place_m")):
            sp.dma_start(to[:], io[name]).then_inc(s_w, 16)
        for to, name in ((bv, "bv"), (bo, "bo")):
            sp.dma_start(to[:], io["L1_xattn_" + name].partition_broadcast(P)).then_inc(s_w, 16)
        for p in range(2):
            sp.dma_start(self.ctx_t[:, p, :], io["ctx_t"][p]).then_inc(self.s_ctx[p], 16)


def head_attention(nc, io, x_sb, ident, norm, norm_after, loads):
    EXP_LIMIT = 60.0
    UNITS = GROUPS * KT
    PRING = 4
    LAG = 2
    with ExitStack() as ctx:
        def sb(name, shape, dt=F32):
            return ctx.enter_context(nc.sbuf_tensor("C_" + name, shape, dt))

        def ps(name, shape):
            return ctx.enter_context(nc.psum_tensor("C_" + name, shape, F32))

        def sem(name):
            return ctx.enter_context(nc.semaphore("C_" + name))

        wq, wk, wv, wo, bqk, bv, bo = loads.weights
        mask, head_sum, place_m, ctx_t = loads.mask, loads.head_sum, loads.place_m, loads.ctx_t
        s_w, W_ALL, s_ctx = loads.s_w, loads.all, loads.s_ctx
        ones = sb("ones", [P, 1])
        place_m_r = sb("place_m_r", [HEADS, GROUPS, P], F32R)
        place_r = sb("place_r", [P, 2, GROUPS, P], F32R)
        k_t = sb("k_t", [P, CTX])
        k_hi = sb("k_hi", [P, CTX], F32R)
        k_lo = sb("k_lo", [P, CTX], F32R)
        ends = sb("ends", [P, 4])
        keys = sb("keys", [P, 2, GROUPS, CTXP], F32R)
        values = sb("values", [P, 2, KT, HEADS, 2 * DK])
        xn = sb("xn", [P, QT, D])
        xt = sb("xt", [P, QT, P])
        q_t = sb("q_t", [P, SEQ])
        q_hi = sb("q_hi", [P, SEQ], F32R)
        q_lo = sb("q_lo", [P, SEQ], F32R)
        q_bound = sb("q_bound", [P, SEQ])
        queries = sb("queries", [P, 2, GROUPS, HG, SEQ], F32R)
        over = sb("over", [P, 2])
        flag = sb("flag", [1, 2], I32)
        top_part = sb("top_part", [P, QT, HEADS, len(KCH)])
        top_m = sb("top_m", [P, QT, HEADS])
        minus_m = sb("minus_m", [HEADS, SEQ], F32R)
        probs = sb("probs", [P, PRING, HG, SEQ])
        o_t = sb("o_t", [P, GROUPS, SEQ])
        den_t = sb("den_t", [P, GROUPS, SEQ])

        ps_s = [ps(f"ps_s{i}", [P, HG, SEQ]) for i in range(2)]
        ps_o = [ps(f"ps_o{i}", [P, SEQ]) for i in range(2)]
        ps_p = ps("ps_p", [P, 512])
        ps_f = ps("ps_f", [P, 512])

        s_place = sem("s_place")
        s_const = sem("s_const")
        s_split = sem("s_split")
        s_placed = [sem(f"s_placed{i}") for i in range(2)]
        s_xn = sem("s_xn")
        s_job = sem("s_job")
        s_job_done = sem("s_job_done")
        s_score = sem("s_score")
        s_exp = sem("s_exp")
        s_av = sem("s_av")
        s_o_read = sem("s_o_read")
        s_den = sem("s_den")
        s_fin = sem("s_fin")
        s_fin_read = sem("s_fin_read")
        s_top = sem("s_top")
        s_top_read = sem("s_top_read")
        s_dve = sem("s_dve")
        s_pool = sem("s_pool")
        s_dve_fin = sem("s_dve_fin")
        s_seen_pe = sem("s_seen_pe")
        s_seen_dve = sem("s_seen_dve")

        JOBS = ([("turn", 0), ("query", 0)] + [("key", i) for i in range(len(KCH))]
                + [("value", i) for i in range(0, KT, 4)] + [("place_query", g) for g in range(GROUPS)]
                + [("bound", 0), ("count", 0)])
        FIRST_JOBS = sorted(JOBS, key=lambda job: (job[0] != "key") + (job[0] == "value"))
        BEFORE_SCORES = [kind for kind, _ in FIRST_JOBS].index("value")
        NJ = len(JOBS)
        JOB_AT = dict(zip((4, 5, 14, 18, 20, 22, 24, 33, 35, 37, 39, 41, 43, 45, 47, 49), range(NJ)))
        assert len(JOB_AT) == NJ
        FIN_AT = {6: 0, 7: 1, 16: 2}
        TAKE_AT = {19: 0, 15 + KT: 1, 15 + 2 * KT: 2, 2: 3}
        MAXIMA_AT = max(JOB_AT) + 1
        assert MAXIMA_AT < UNITS
        TOPS = HEADS * QT * len(KCH)
        TOP_FILLS = TOPS + 1 + GROUPS
        TOP_READS = TOPS + 2 + GROUPS

        def top_rounds():
            n = 0
            for h in range(HEADS):
                for qt in range(QT):
                    for i, (at, width) in enumerate(KCH):
                        yield n, h, qt, i, at, width
                        n += 1

        with nc.Block() as block:
            @block.sync
            def _(sp):
                sp.dma_start(probs[:, 0, :, :].rearrange("p h q -> p (h q)"),
                             io["place"].rearrange("p a g r -> p (a g r)")).then_inc(s_place, 16)

                def move_sums(b):
                    sp.wait_ge(s_o_read, GROUPS * (b + 1))
                    for j in range(HG):
                        sp.dma_start(den_t[32 * j:32 * j + DK, :, :],
                                     o_t[32 * j + DK:32 * j + 2 * DK, :, :]).then_inc(s_den, 16)

                def place(p, parity, load, sums=True):
                    if sums:
                        move_sums(p - 2)
                    sp.wait_ge(s_split, p + 1)
                    for g in range(GROUPS):
                        for product, part in enumerate((k_hi, k_hi, k_lo)):
                            sp.dma_start(keys[32 * product:32 * product + 32, parity, g, 0:CTX].bitcast(F32),
                                         part[32 * g:32 * g + 32, 0:CTX].bitcast(F32)).then_inc(s_placed[parity], 16)
                    if load:
                        sp.wait_ge(s_job_done, NJ * (p + 1))
                        sp.dma_start(ctx_t[:, parity, :], io["ctx_t"][bass.ds(p + 2, 1)].rearrange(
                            "b p c -> p (b c)")).then_inc(s_ctx[parity], 16)

                place(0, 0, True, False)
                place(1, 1, True, False)
                with sp.Fori(1, BATCH // 2 - 1) as i:
                    place(2 * i, 0, True)
                    place(2 * i + 1, 1, True)
                place(BATCH - 2, 0, False)
                place(BATCH - 1, 1, False)
                move_sums(BATCH - 2)
                move_sums(BATCH - 1)

            def loaded(eng, parity, turn):
                eng.wait_ge(s_ctx[parity], 16 * (turn + 1))

            def placed(eng, parity, turn):
                eng.wait_ge(s_placed[parity], 16 * 3 * GROUPS * (turn + 1))

            @block.tensor
            def _(pe):
                T = nc.tensor

                def place_query(parity, g, shifted=False):
                    T.matmul(ps_p[:, 0:SEQ], place_r[:, 0, g, :], q_hi[:], start=True, stop=False)
                    m = T.matmul(ps_p[:, 0:SEQ], place_r[:, 1, g, :], q_lo[:], start=False, stop=not shifted)
                    if shifted:
                        m = T.matmul(ps_p[:, 0:SEQ], place_m_r[:, g, :], minus_m[:], start=False, stop=True)
                    return m

                def job(p, parity, turn, n, kind, arg):
                    wait(pe, s_job_done, NJ * p + n)
                    if kind == "turn":
                        pe.wait_ge(s_xn, QT * (p + 1))
                        for i in range(QT):
                            m = T.transpose(ps_p[:, i * P:(i + 1) * P], xn[:, i, :], ident[:])
                    elif kind == "query":
                        m = T.matmul(ps_p[:, 0:SEQ], wq[:], xt[:].rearrange("p i t -> p (i t)"), start=True, stop=True)
                    elif kind == "key":
                        if arg == 0:
                            loaded(pe, parity, turn)
                        at, width = KCH[arg]
                        m = T.matmul(ps_p[:, 0:width], wk[:], ctx_t[:, parity, at:at + width], start=True, stop=True)
                    elif kind == "value":
                        for kt in range(arg, min(arg + 4, KT)):
                            rows = min(P, CTX - kt * P)
                            m = T.matmul(ps_p[0:rows, (kt - arg) * D:(kt - arg + 1) * D],
                                         ctx_t[:, parity, kt * P:kt * P + rows], wv[:], start=True, stop=True)
                    elif kind == "place_query":
                        m = place_query(parity, arg)
                    elif kind == "bound":
                        m = T.matmul(ps_p[0:HEADS, 0:SEQ], head_sum[:], q_bound[:], start=True, stop=True)
                    else:
                        m = T.matmul(ps_p[0:1, 0:1], over[:, 1:2], ones[:], start=True, stop=True)
                    m.then_inc(s_job, 1)

                def maxima(p, parity, turn, prepared=NJ):
                    pe.wait_ge(s_job_done, NJ * p + prepared)
                    pe.sem_inc(s_seen_pe, 1)
                    wide = pe.value_load(flag[0:1, parity:parity + 1], min_val=0, max_val=HEADS)
                    with pe.If(wide > 0):
                        placed(pe, parity, turn)
                        for n, h, qt, i, at, width in top_rounds():
                            wait(pe, s_top_read, TOP_READS * p + n)
                            T.matmul(ps_p[:, 0:width + width % 2],
                                     queries[:, parity, h // HG, h % HG, qt * P:(qt + 1) * P],
                                     keys[:, parity, h // HG, at:at + width + width % 2],
                                     start=True, stop=True).then_inc(s_top, 1)
                        pe.wait_ge(s_top_read, TOP_READS * p + TOPS + 1)
                        for qt in range(QT):
                            m = T.transpose(ps_p[0:HEADS, qt * P:(qt + 1) * P], top_m[:, qt, :], ident[:])
                        m.then_inc(s_top, 1)
                        for g in range(GROUPS):
                            pe.wait_ge(s_top_read, TOP_READS * p + TOPS + 2 + g)
                            place_query(parity, g, True).then_inc(s_top, 1)
                    with pe.Else():
                        pe.sem_inc(s_top, TOP_FILLS)

                def scores(k, parity, n):
                    g, kt = divmod(n, KT)
                    wait(pe, s_exp, UNITS * k + n - 1)
                    for j in range(HG):
                        m = T.matmul(ps_s[n % 2][:, j, :], keys[:, parity, g, kt * P:(kt + 1) * P],
                                     queries[:, parity, g, j, :], start=True, stop=True)
                    m.then_inc(s_score, 1)

                def weigh(k, parity, n):
                    g, kt = divmod(n, KT)
                    pe.wait_ge(s_exp, UNITS * k + n + 1)
                    if kt == 0:
                        wait(pe, s_o_read, GROUPS * k + g - 1)
                    for j in range(HG):
                        m = T.matmul(ps_o[g % 2][32 * j:32 * j + 2 * DK, :], values[:, parity, kt, g * HG + j, :],
                                     probs[:, n % PRING, j, :], start=(kt == 0), stop=(kt == KT - 1))
                    m.then_inc(s_av, 1)
                    return m

                def finish(b):
                    pe.wait_ge(s_fin_read, 3 * b + 2)
                    for qt in range(QT):
                        for g in range(GROUPS):
                            m = T.matmul(ps_f[:, qt * D:(qt + 1) * D], o_t[:, g, qt * P:(qt + 1) * P], wo[:, g, :],
                                         start=(g == 0), stop=(g == GROUPS - 1))
                    m.then_inc(s_fin, 1)

                def attend(k, parity, last, turn):
                    first = isinstance(k, int) and k == 0
                    for n in range(UNITS):
                        if n == 0:
                            pe.wait_ge(s_job_done, BEFORE_SCORES if first else NJ * (k + 1))
                            pe.wait_ge(s_top_read, TOP_READS * (k + 1))
                            placed(pe, parity, turn)
                        scores(k, parity, n)
                        if first and n == LAG - 1:
                            for v in range(BEFORE_SCORES, NJ):
                                job(0, 0, 0, v, *FIRST_JOBS[v])
                            pe.wait_ge(s_job_done, NJ)
                        if n >= LAG:
                            weigh(k, parity, n - LAG)
                        elif not first:
                            weigh(k - 1, 1 - parity, UNITS - LAG + n)
                        if FIN_AT.get(n) == 2 and not first:
                            finish(k - 1)
                        if n in JOB_AT and not last:
                            job(k + 1, 1 - parity, turn + parity, JOB_AT[n], *JOBS[JOB_AT[n]])
                        if n == MAXIMA_AT and not last:
                            maxima(k + 1, 1 - parity, turn + parity)

                pe.wait_ge(s_w, W_ALL)
                for n, (kind, arg) in enumerate(FIRST_JOBS[:BEFORE_SCORES]):
                    if kind == "turn":
                        pe.wait_ge(s_const, 2)
                    job(0, 0, 0, n, kind, arg)
                maxima(0, 0, 0, BEFORE_SCORES)
                rounds(pe, BATCH, attend)
                for n in range(UNITS - LAG, UNITS):
                    weigh(BATCH - 1, 1, n)
                finish(BATCH - 1)

            @block.scalar
            def _(act):
                norm.root(nc, act)

                def exps(k, parity, last, turn):
                    for n in range(UNITS):
                        act.wait_ge(s_score, UNITS * k + n + 1)
                        wait(act, s_av, UNITS * k + n - PRING + 1)
                        nc.scalar.activation(probs[:, n % PRING, :, :], ps_s[n % 2][:], ACT.Exp,
                                             scale=SCORE_SCALE1).then_inc(s_exp, 1)

                rounds(act, BATCH, exps)

            @block.gpsimd
            def _(pool):
                G = nc.gpsimd
                chain = Chain(pool, s_pool)
                chain.step(G.memset(keys[:, :, :, CTX:].bitcast(F32), 0.0))
                chain.step(G.memset(keys[SHIFT_ROW:, :, :, 0:CTX].bitcast(F32), 1.0))
                chain.step(G.memset(values[:, :, 0:KT - 1].rearrange("p a k h v -> p a (k h v)"), 1.0))
                chain.step(G.memset(values[:, :, KT - 1].rearrange("p a h v -> p a (h v)"), 0.0))
                for parity in range(2):
                    chain.step(G.memset(values[0:CTX - (KT - 1) * P, parity, KT - 1, :, DK:], 1.0))
                pool.sem_inc(s_const, 1)

            @block.vector
            def _(dve):
                chain = Chain(dve, s_dve)
                V = nc.vector
                rows = CTX - (KT - 1) * P
                for bank in ps_o:
                    chain.mark(V.memset(bank[:], 0.0))
                chain.mark(V.memset(den_t[:], 1.0))
                chain.mark(V.memset(ones[:], 1.0))

                def place_query(parity, g, sem_):
                    V.tensor_tensor(queries[:, parity, g, :, :],
                                    ps_p[:, 0:SEQ].unsqueeze(1).to_broadcast([P, HG, SEQ]),
                                    mask[:].unsqueeze(2).to_broadcast([P, HG, SEQ]), ALU.mult).then_inc(sem_, 1)

                def job(p, parity, turn, n, kind, arg):
                    first = isinstance(p, int) and p == 0
                    if kind == "turn":
                        for i in range(QT):
                            norm.apply(nc, x_sb, QT * p + i, xn[:, i, :]).then_inc(s_xn, 1)
                    dve.wait_ge(s_job, NJ * p + n + 1)
                    done = None
                    if kind == "turn":
                        done = V.tensor_copy(xt[:].rearrange("p i t -> p (i t)"), ps_p[:, 0:SEQ])
                    elif kind == "query":
                        chain.step(V.tensor_scalar(q_t[:], ps_p[:, 0:SEQ], bqk[:, 0:1], None, ALU.add))
                        chain.mark(V.tensor_copy(q_hi[:], q_t[:]))
                        chain.step(V.scalar_tensor_tensor(q_bound[:], q_t[:], -1.0, q_t[:], ALU.mult, ALU.max))
                        done = V.tensor_tensor(q_lo[:], q_t[:], q_hi[:].bitcast(F32), ALU.subtract)
                    elif kind == "key":
                        at, width = KCH[arg]
                        evac = V.tensor_scalar(k_t[:, at:at + width], ps_p[:, 0:width], bqk[:, 1:2], None, ALU.add)
                        done = evac
                        if arg == len(KCH) - 1:
                            done = None
                            evac.then_inc(s_job_done, 1)
                            dve.wait_ge(s_job_done, NJ * p + n + 1)
                            k = k_t[:, 0:CTX]
                            chain.mark(V.tensor_reduce(ends[:, 0:1], k, AX, ALU.max))
                            chain.step(V.tensor_reduce(ends[:, 1:2], k, AX, ALU.min))
                            chain.mark(V.tensor_tensor(ends[:, 2:3], ends[:, 0:1], ends[:, 1:2], ALU.add))
                            chain.step(V.tensor_tensor(ends[:, 3:4], ends[:, 0:1], ends[:, 1:2], ALU.subtract))
                            chain.step(V.tensor_scalar(ends[:, 2:4], ends[:, 2:4], 0.5, None, ALU.mult))
                            chain.step(V.tensor_scalar(k, k, ends[:, 2:3], None, ALU.subtract))
                            if not first:
                                placed(dve, 1 - parity, turn - 1 + parity)
                            chain.step(V.tensor_copy(k_hi[:, 0:CTX], k))
                            V.tensor_tensor(k_lo[:, 0:CTX], k, k_hi[:, 0:CTX].bitcast(F32),
                                            ALU.subtract).then_inc(s_split, 1)
                    elif kind == "value":
                        n_kt = min(arg + 4, KT) - arg
                        r = P if n_kt == 4 else rows
                        done = V.tensor_tensor(
                            values[0:r, parity, arg:arg + n_kt, :, 0:DK],
                            ps_p[0:r, 0:n_kt * D].rearrange("p (k h d) -> p k h d", k=n_kt, h=HEADS),
                            bv[0:r, :].rearrange("p (h d) -> p h d", h=HEADS).unsqueeze(1).to_broadcast([r, n_kt, HEADS, DK]),
                            ALU.add)
                    elif kind == "place_query":
                        if arg == 0:
                            chain.mark(V.tensor_scalar(q_bound[:], q_bound[:], ends[:, 3:4], None, ALU.mult))
                        place_query(parity, arg, s_job_done)
                    elif kind == "bound":
                        chain.step(V.tensor_reduce(over[0:HEADS, 0:1], ps_p[0:HEADS, 0:SEQ], AX, ALU.max))
                        done = V.tensor_scalar(over[0:HEADS, 1:2], over[0:HEADS, 0:1], EXP_LIMIT / SCORE_SCALE1, None, ALU.is_gt)
                    else:
                        done = V.tensor_copy(flag[0:1, parity:parity + 1], ps_p[0:1, 0:1])
                    if done is not None:
                        done.then_inc(s_job_done, 1)
                JOB_STEPS = 3 + 8 + 1

                def prepare(p, parity, turn, n):
                    if n == 0:
                        chain.at(setup + JOB_STEPS * p)
                    job(p, parity, turn, n, *JOBS[n])
                    if n == NJ - 1:
                        assert chain.n == JOB_STEPS, chain.n

                def maxima(p, parity, prepared=NJ):
                    dve.wait_ge(s_job_done, NJ * p + prepared)
                    dve.sem_inc(s_seen_dve, 1)
                    wide = dve.value_load(flag[0:1, parity:parity + 1], min_val=0, max_val=HEADS)
                    with dve.If(wide > 0):
                        for n, h, qt, i, at, width in top_rounds():
                            dve.wait_ge(s_top, TOP_FILLS * p + n + 1)
                            V.tensor_reduce(top_part[:, qt, h, i:i + 1], ps_p[:, 0:width], AX,
                                            ALU.max).then_inc(s_top_read, 1)
                        dve.wait_ge(s_top_read, TOP_READS * p + TOPS)
                        V.tensor_reduce(top_m[:], top_part[:], AX, ALU.max, negate=True).then_inc(s_top_read, 1)
                        dve.wait_ge(s_top, TOP_FILLS * p + TOPS + 1)
                        V.tensor_copy(minus_m[:], ps_p[0:HEADS, 0:SEQ]).then_inc(s_top_read, 1)
                        for g in range(GROUPS):
                            dve.wait_ge(s_top, TOP_FILLS * p + TOPS + 2 + g)
                            place_query(parity, g, s_top_read)
                    with dve.Else():
                        dve.sem_inc(s_top_read, TOP_READS)

                def take_o(b, g):
                    dve.wait_ge(s_av, UNITS * b + KT * (g + 1))
                    if g == 0:
                        wait(dve, s_fin, b)
                    V.tensor_copy(o_t[:, g, :], ps_o[g % 2][:]).then_inc(s_o_read, 1)

                def finish(b, step):
                    if step < 2:
                        dve.wait_ge(s_den, 16 * HG * (b + 1))
                        half = slice(2 * step, 2 * step + 2)
                        den = den_t[:, half, :].rearrange("p g q -> p (g q)")
                        fin.step(V.reciprocal(den, den))
                        V.tensor_tensor(o_t[:, half, :], o_t[:, half, :], den_t[:, half, :],
                                        ALU.mult).then_inc(s_fin_read, 1)
                    else:
                        dve.wait_ge(s_fin, b + 1)
                        to = x_sb[:, bass.ds(QT * b, QT), :]
                        fin.step(V.tensor_tensor(to, to, ps_f[:].rearrange("p (i d) -> p i d", i=BT)[:, 0:QT, :], ALU.add))
                        V.tensor_tensor(to, to, bo[:].unsqueeze(1).to_broadcast([P, QT, D]),
                                        ALU.add).then_inc(s_fin_read, 1)
                        dve.wait_ge(s_fin_read, 3 * b + 3)
                        for i in range(QT):
                            norm_after.take(nc, x_sb, QT * b + i)
                fin = Chain(dve, s_dve_fin)

                def attend(k, parity, last, turn):
                    first = isinstance(k, int) and k == 0
                    for n in range(UNITS):
                        if n in TAKE_AT:
                            g = TAKE_AT[n]
                            if g < GROUPS - 1:
                                take_o(k, g)
                            elif not first:
                                take_o(k - 1, g)
                        if n in FIN_AT and not first:
                            fin.at(3 * (k - 1) + FIN_AT[n])
                            finish(k - 1, FIN_AT[n])
                        if n in JOB_AT and not last:
                            prepare(k + 1, 1 - parity, turn + parity, JOB_AT[n])
                        if n == MAXIMA_AT and not last:
                            maxima(k + 1, 1 - parity)

                dve.wait_ge(s_w, W_ALL)
                for n in range(len(KCH)):
                    job(0, 0, 0, n, *FIRST_JOBS[n])
                norm.statistics(nc, dve, chain)
                dve.wait_ge(s_place, 16)
                chain.mark(V.tensor_copy(place_m_r[:], place_m[:]))
                chain.step(V.tensor_copy(place_r[:].rearrange("p a g r -> p (a g r)"),
                                         probs[:, 0, :, :].rearrange("p h q -> p (h q)")))
                V.memset(over[:], 0.0).then_inc(s_const, 1)
                dve.wait_ge(s_const, 2)
                for n in range(len(KCH), BEFORE_SCORES):
                    job(0, 0, 0, n, *FIRST_JOBS[n])
                setup = chain.n - JOB_STEPS
                maxima(0, 0, BEFORE_SCORES)
                for n in range(BEFORE_SCORES, NJ):
                    job(0, 0, 0, n, *FIRST_JOBS[n])
                rounds(dve, BATCH, attend)
                take_o(BATCH - 1, GROUPS - 1)
                for step in range(3):
                    fin.at(3 * (BATCH - 1) + step)
                    finish(BATCH - 1, step)
                dve.wait_ge(s_fin_read, 3 * BATCH)


def head_experts(nc, io, x_sb, ident, norm):
    with ExitStack() as ctx:
        def sb(name, shape, dt=F32):
            return ctx.enter_context(nc.sbuf_tensor("D_" + name, shape, dt))

        def ps(name, shape):
            return ctx.enter_context(nc.psum_tensor("D_" + name, shape, F32))

        def sem(name):
            return ctx.enter_context(nc.semaphore("D_" + name))

        HG1 = H1 // 2
        EG = 2
        QUADS = HP * EG
        UNITS = QUADS * 4
        RING = 8
        CHOICES = [P, BT * H1, E1]

        wm = sb("wm", [P, D])
        bm = sb("bm", [P, 1])
        emb = sb("emb", [P, P])
        w_up = sb("w_up", [P, 2, PAIRS, P])
        w_up_r = sb("w_up_r", [P, 2, PAIRS, P], F32R)
        part = sb("part", [P, 1])
        b_up = sb("b_up", [P, PAIRS])
        w_down = sb("w_down", [P, PAIRS, 32])
        b_down = sb("b_down", [P, EG])
        wo = sb("wo", [P, H1, D])
        bo = sb("bo", [P, D])
        order = sb("order", [P, E1])
        place_t = sb("place_t", [P, 2, HP, P], F32R)
        place_g = sb("place_g", [P, HG1, EG, P], F32R)
        xn = sb("xn", [P, BT, D])
        xt = sb("xt", [P, BLOCK])
        h_t = sb("h_t", [P, BLOCK])
        h_hi = sb("h_hi", [P, BLOCK], F32R)
        h_lo = sb("h_lo", [P, BLOCK], F32R)
        up_in = sb("up_in", [P, 2, HP, BLOCK], F32R)
        weight = sb("weight", CHOICES)
        left = sb("left", CHOICES)
        hit = sb("hit", CHOICES)
        chosen = sb("chosen", [P, 2] + CHOICES[1:])
        top = sb("top", CHOICES[:2])
        best = sb("best", CHOICES[:2])
        total = sb("total", CHOICES[:2])
        parts = sb("parts", [P, BT, 2, 2, HG1 * E1], F32R)
        gate_t = sb("gate_t", [P, 2, 2, BLOCK], F32R)
        gate = sb("gate", [P, 2, 2, BLOCK])
        hidden = sb("hidden", [P, RING, 2, BLOCK])
        gated = sb("gated", [P, 2, 2, BLOCK])
        gated1 = sb("gated1", [P, 2, BLOCK])

        ps_p = ps("ps_p", [P, BLOCK])
        ps_u = [ps(f"ps_u{i}", [P, 2, BLOCK]) for i in range(2)]
        ps_e = ps("ps_e", [P, 2, BLOCK])
        ps_o = ps("ps_o", [P, BT, D])

        s_w_first = sem("s_w_first")
        s_w = sem("s_w")
        s_const = sem("s_const")
        s_xn = sem("s_xn")
        s_job = sem("s_job")
        s_job_done = sem("s_job_done")
        s_shifted = sem("s_shifted")
        s_exp = sem("s_exp")
        s_up = sem("s_up")
        s_hid = sem("s_hid")
        s_down = sem("s_down")
        s_read = sem("s_read")
        s_gated = sem("s_gated")
        s_parts = sem("s_parts")
        s_place = sem("s_place")
        s_heads = sem("s_heads")
        s_wo = sem("s_wo")
        s_x4 = sem("s_x4")
        s_dve = sem("s_dve")
        s_dve_x = sem("s_dve_x")
        s_out = sem("s_out")

        PREPARE = {2: ("turn", 0), 3: ("project", 0), 6: ("logit", 0), 7: ("place_up", 0), 10: ("place_up", 1),
                   14: ("place_up", 2), 18: ("place_up", 3), 26: ("turn_gate", 0), 30: ("turn_gate", 1)}
        NPREP = len(PREPARE)
        GATES = {4 * v + s: ("place_gate", (v, s)) for v in range(QUADS) for s in range(2)}
        NGATE = len(GATES)
        EXP_AT, SPLIT_AT = 6, 25
        CHOOSE_AT = {9: (0, 1, 2), 10: (3,), 13: (4,), 14: (5,), 17: (6, 7, 8), 18: (9,), 21: (10, 11, 12),
                     22: (13,), 23: (14,), 24: (15,)}

        def timetable(entries):
            return {u % UNITS: (what, u >= UNITS) for u, what in entries}

        DOWN_AT = timetable((4 * v + 5 + s, (v, s)) for v in range(QUADS) for s in range(2))
        GATING_AT = timetable((4 * v + 6, v) for v in range(QUADS))
        OUT_AT = timetable((8 * hp + 15 + (0, 1, 4, 5)[n], (hp, n)) for hp in range(HP) for n in range(4))
        X_AT = 13
        HEADS_AT = 4

        def jobs(last):
            at = {**GATES, **({} if last else PREPARE)}
            return {u: (n, at[u]) for n, u in enumerate(sorted(at))}

        def jobs_before(k):
            return NPREP + (NPREP + NGATE) * k

        with nc.Block() as block:
            @block.sync
            def _(sp):
                for to, name in ((wm, "Wm"), (bm, "bm"), (emb, "emb")):
                    sp.dma_start(to[:], io["L1_ffn_" + name]).then_inc(s_w_first, 16)
                sp.dma_start(hidden[:, 0, :, :].rearrange("p a b -> p (a b)"),
                             io["place_t"].rearrange("p a b c -> p (a b c)")).then_inc(s_w_first, 16)
                for to, name in ((w_up, "w_up"), (part, "part"), (b_up, "b_up"), (w_down, "w_down"), (b_down, "b_down"),
                                 (wo, "wo")):
                    sp.dma_start(to[:], io["L1_ffn_" + name]).then_inc(s_w, 16)
                sp.dma_start(bo[:], io["L1_ffn_bo"].partition_broadcast(P)).then_inc(s_w, 16)
                sp.dma_start(order[:], io["order1"].partition_broadcast(P)).then_inc(s_w, 16)
                sp.dma_start(hidden[:, 1, :, :].rearrange("p a b -> p (a b)"),
                             io["place_g"].rearrange("p a b c -> p (a b c)")).then_inc(s_w, 16)
                out_rows = io["out"].rearrange("(t p) d -> p t d", p=P)
                with sp.Fori(0, BLOCKS) as k:
                    sp.wait_ge(s_x4, k + 1)
                    sp.dma_start(out_rows[:, bass.ds(k * BT, BT), :],
                                 x_sb[:, bass.ds(k * BT, BT), :]).then_inc(s_out, 16)
                sp.wait_ge(s_out, 16 * BLOCKS)
            W_FIRST, W_ALL = 16 * 4, 16 * 9

            @block.tensor
            def _(pe):
                T = nc.tensor

                def job(p, parity, n, kind, arg):
                    wait(pe, s_job_done, n)
                    if kind == "turn":
                        pe.wait_ge(s_xn, BT * (p + 1))
                        for i in range(BT):
                            m = T.transpose(ps_p[:, i * P:(i + 1) * P], xn[:, i, :], ident[:])
                    elif kind == "project":
                        m = T.matmul(ps_p[:], wm[:], xt[:], start=True, stop=True)
                    elif kind == "place_up":
                        pe.wait_ge(s_heads, p + 1)
                        T.matmul(ps_p[:], place_t[:, 0, arg, :], h_hi[:], start=True, stop=False)
                        m = T.matmul(ps_p[:], place_t[:, 1, arg, :], h_lo[:], start=False, stop=True)
                    elif kind == "logit":
                        for i in range(BT):
                            m = T.matmul(ps_p[:, i * P:(i + 1) * P], h_t[:, i * P:(i + 1) * P], emb[:],
                                         start=True, stop=True)
                    elif kind == "turn_gate":
                        pe.wait_ge(s_parts, p + 1)
                        for i in range(BT):
                            m = T.transpose(ps_p[:, i * P:(i + 1) * P],
                                            parts[:, i, arg].rearrange("p a e -> p (a e)").bitcast(F32), ident[:])
                    else:
                        v, s = arg
                        half, h = divmod(v // EG * 2 + s, HG1)
                        m = T.matmul(ps_p[:], place_g[:, h, v % EG, :], gate_t[:, parity, half, :],
                                     start=True, stop=True)
                    m.then_inc(s_job, 1)

                def up(k, parity, u):
                    hp, pair = divmod(u, PAIRS)
                    wait(pe, s_hid, UNITS * k + u - 1)
                    for s in range(2):
                        m = T.matmul(ps_u[u % 2][:, s, :], w_up_r[:, s, pair, :], up_in[:, parity, hp, :],
                                     start=True, stop=True)
                    m.then_inc(s_up, 1)

                def down(k, v, s):
                    if s == 0:
                        pe.wait_ge(s_hid, UNITS * k + 4 * v + 4)
                        wait(pe, s_read, QUADS * k + v)
                    for i in range(4):
                        m = T.matmul(ps_e[32 * i:32 * i + 32, s, :], w_down[:, v % EG * 4 + i, :],
                                     hidden[:, (4 * v + i) % RING, s, :], start=True, stop=True)
                    if s == 1:
                        m.then_inc(s_down, 1)

                def out(k, hp, n):
                    if n == 0:
                        pe.wait_ge(s_gated, HP * k + hp + 1)
                        if hp == 0:
                            wait(pe, s_dve_x, k)
                    s, second = divmod(n, 2)
                    for i in (2 * second, 2 * second + 1):
                        m = T.matmul(ps_o[:, i, :], gated[:, hp % 2, s, i * P:(i + 1) * P], wo[:, hp * 2 + s, :],
                                     start=(hp == 0 and s == 0 and i == 0), stop=(hp == HP - 1 and s == 1),
                                     skip_group_check=True)
                    if n == 3:
                        m.then_inc(s_wo, 1)

                def experts(k, parity, last, turn):
                    first = isinstance(k, int) and k == 0
                    at = jobs(last)
                    pe.wait_ge(s_job_done, jobs_before(k))
                    for u in range(UNITS):
                        up(k, parity, u)
                        if u in at:
                            n, (kind, arg) = at[u]
                            if kind == "place_gate":
                                job(k, parity, jobs_before(k) + n, kind, arg)
                            else:
                                job(k + 1, 1 - parity, jobs_before(k) + n, kind, arg)
                        for table, visit in ((DOWN_AT, down), (OUT_AT, out)):
                            if u in table:
                                what, of_before = table[u]
                                if not of_before:
                                    visit(k, *what)
                                elif not first:
                                    visit(k - 1, *what)

                pe.wait_ge(s_w_first, W_FIRST)
                for n, u in enumerate(sorted(PREPARE)):
                    if PREPARE[u] == ("place_up", 0):
                        pe.wait_ge(s_place, 1)
                    job(0, 0, n, *PREPARE[u])
                pe.wait_ge(s_w, W_ALL)
                pe.wait_ge(s_const, 2)
                pe.wait_ge(s_place, 2)
                rounds(pe, BLOCKS, experts)
                pe.wait_ge(s_job_done, jobs_before(BLOCKS - 1) + NGATE)
                for s in range(2):
                    down(BLOCKS - 1, QUADS - 1, s)
                for hp, n in (what for what, of_before in OUT_AT.values() if of_before):
                    out(BLOCKS - 1, hp, n)

            @block.scalar
            def _(act):
                norm.root(nc, act)
                for to, at in ((place_t[:].rearrange("p a b c -> p (a b c)"), 0),
                               (place_g[:].rearrange("p a b c -> p (a b c)"), 1)):
                    if at == 0:
                        act.wait_ge(s_w_first, W_FIRST)
                    else:
                        act.wait_ge(s_w, W_ALL)
                    nc.scalar.copy(to, hidden[:, at, :, :].rearrange("p a b -> p (a b)")).then_inc(s_place, 1)
                act.wait_ge(s_place, 2)

                def exponent(p):
                    act.wait_ge(s_shifted, p + 1)
                    nc.scalar.activation(weight[:], weight[:], ACT.Exp).then_inc(s_exp, 1)

                def gelus(k, parity, last, turn):
                    for u in range(UNITS):
                        act.wait_ge(s_up, UNITS * k + u + 1)
                        wait(act, s_down, QUADS * k + u // 4 - 1)
                        nc.scalar.activation(hidden[:, u % RING, :, :], ps_u[u % 2][:], ACT.Gelu,
                                             bias=b_up[:, u % PAIRS:u % PAIRS + 1]).then_inc(s_hid, 1)
                        if u == EXP_AT and not last:
                            exponent(k + 1)

                exponent(0)
                rounds(act, BLOCKS, gelus)

            @block.gpsimd
            def _(pool):
                G = nc.gpsimd
                pool.wait_ge(s_w, W_ALL)

                def add_groups(k, hp):
                    pool.wait_ge(s_read, QUADS * k + EG * (hp + 1))
                    to = gated[:, hp % 2]
                    G.tensor_tensor(to, to, gated1[:], ALU.add).then_inc(s_gated, 1)

                def add_bias(k):
                    pool.wait_ge(s_dve_x, k + 1)
                    to = x_sb[:, bass.ds(BT * k, BT), :]
                    G.tensor_tensor(to, to, bo[:].unsqueeze(1).to_broadcast([P, BT, D]), ALU.add).then_inc(s_x4, 1)

                add_groups(0, 0)
                add_groups(0, 1)
                add_groups(0, 2)
                with pool.Fori(1, BLOCKS) as k:
                    add_groups(k - 1, HP - 1)
                    add_groups(k, 0)
                    add_bias(k - 1)
                    for hp in range(1, HP - 1):
                        add_groups(k, hp)
                add_groups(BLOCKS - 1, HP - 1)
                add_bias(BLOCKS - 1)

            @block.vector
            def _(dve):
                chain = Chain(dve, s_dve)
                V = nc.vector
                norm.statistics(nc, dve, chain)
                setup = chain.n
                dve.wait_ge(s_w_first, W_FIRST)

                def job(p, parity, n, kind, arg):
                    dve.wait_ge(s_job, n + 1)
                    if kind == "turn":
                        done = V.tensor_copy(xt[:], ps_p[:])
                    elif kind == "project":
                        done = V.tensor_scalar(h_t[:], ps_p[:], bm[:], None, ALU.add)
                    elif kind == "place_up":
                        done = V.tensor_copy(up_in[:, parity, arg, :], ps_p[:])
                    elif kind == "logit":
                        logits = ps_p[:].rearrange("p (a e) -> p a e", e=E1)
                        chain.step(V.tensor_reduce(top[:], logits, AX, ALU.max))
                        wait(dve, s_parts, p)
                        V.tensor_tensor(weight[:], logits, top[:].unsqueeze(2).to_broadcast(CHOICES),
                                        ALU.subtract).then_inc(s_shifted, 1)
                        dve.wait_ge(s_shifted, p + 1)
                        done = V.tensor_copy(top[:, 0:1], top[:, 0:1])
                    elif kind == "turn_gate":
                        done = V.tensor_copy(gate_t[:, parity, arg, :], ps_p[:])
                    else:
                        v, s = arg
                        wait(dve, s_read, QUADS * p + v - 1)
                        done = V.tensor_copy(gate[:, v % 2, s, :], ps_p[:])
                    done.then_inc(s_job_done, 1)

                def normalize(p):
                    for i in range(BT):
                        norm.apply(nc, x_sb, BT * p + i, xn[:, i, :]).then_inc(s_xn, 1)

                def split_heads(p, n):
                    dve.wait_ge(s_job_done, n + 1)
                    chain.step(V.tensor_copy(h_hi[:], h_t[:]))
                    V.tensor_tensor(h_lo[:], h_t[:], h_hi[:].bitcast(F32), ALU.subtract).then_inc(s_heads, 1)

                def split_gates(p, n):
                    wait(dve, s_job, n)
                    chain.settle()
                    w = weight[:].rearrange("p (t q h) e -> p t q (h e)", t=BT, q=2)
                    chain.step(V.tensor_copy(parts[:, :, :, 0, :], w))
                    V.tensor_tensor(parts[:, :, :, 1, :], w, parts[:, :, :, 0, :].bitcast(F32),
                                    ALU.subtract).then_inc(s_parts, 1)

                def bc(small):
                    return small.unsqueeze(2).to_broadcast(CHOICES)

                def choose(p, step):
                    if step == 0:
                        dve.wait_ge(s_exp, p + 1)
                        chain.mark(V.tensor_reduce(total[:], weight[:], AX, ALU.add))
                        return
                    chain.settle()
                    r, kind = divmod(step - 3, 6)
                    if step == 1:
                        ins = V.reciprocal(total[:], total[:])
                    elif step == 2:
                        ins = V.tensor_tensor(weight[:], weight[:], bc(total[:]), ALU.mult)
                    elif step == 14:
                        ins = V.tensor_tensor(chosen[:, 0], chosen[:, 0], chosen[:, 1], ALU.add)
                    elif step == 15:
                        ins = V.tensor_tensor(weight[:], weight[:], chosen[:, 0], ALU.mult)
                    elif kind == 0:
                        ins = V.tensor_reduce(best[:], (weight if r == 0 else left)[:], AX, ALU.max)
                    elif kind == 1:
                        ins = V.tensor_tensor(hit[:], (weight if r == 0 else left)[:], bc(best[:]), ALU.is_equal)
                    elif kind == 2:
                        ins = V.tensor_tensor(hit[:], hit[:], order[:].unsqueeze(1).to_broadcast(CHOICES), ALU.mult)
                    elif kind == 3:
                        ins = V.tensor_reduce(best[:], hit[:], AX, ALU.max)
                    elif kind == 4:
                        ins = V.tensor_tensor(chosen[:, r], hit[:], bc(best[:]), ALU.is_equal)
                    else:
                        ins = V.scalar_tensor_tensor(left[:], chosen[:, 0], -2.0, weight[:], ALU.mult, ALU.add)
                    chain.mark(ins)
                CHOICE_STEPS = 16
                STEPS = 1 + 1 + 1 + CHOICE_STEPS

                def gating(k, parity, v):
                    dve.wait_ge(s_down, QUADS * k + v + 1)
                    if v % EG == 0:
                        wait(dve, s_wo, HP * k + v // EG - 1)
                        to = gated[:, v // EG % 2]
                    else:
                        wait(dve, s_gated, HP * k + v // EG)
                        to = gated1[:]
                    V.scalar_tensor_tensor(to, ps_e[:], b_down[:, v % EG:v % EG + 1], gate[:, v % 2],
                                           ALU.add, ALU.mult).then_inc(s_read, 1)

                def add_to_stream(k):
                    dve.wait_ge(s_wo, HP * (k + 1))
                    to = x_sb[:, bass.ds(BT * k, BT), :]
                    V.tensor_tensor(to, to, ps_o[:], ALU.add).then_inc(s_dve_x, 1)

                def experts(k, parity, last, turn):
                    first = isinstance(k, int) and k == 0
                    at = jobs(last)
                    chain.at(setup + STEPS * (k + 1))
                    for u in range(UNITS):
                        if u in at:
                            n, (kind, arg) = at[u]
                            if kind == "place_gate":
                                job(k, parity, jobs_before(k) + n, kind, arg)
                            else:
                                job(k + 1, 1 - parity, jobs_before(k) + n, kind, arg)
                        if u == 0 and not last:
                            normalize(k + 1)
                        if u == HEADS_AT and not last:
                            split_heads(k + 1, jobs_before(k) + at[3][0])
                        if u in GATING_AT:
                            v, of_before = GATING_AT[u]
                            if not of_before:
                                gating(k, parity, v)
                            elif not first:
                                gating(k - 1, 1 - parity, v)
                        if u in CHOOSE_AT and not last:
                            for step in CHOOSE_AT[u]:
                                choose(k + 1, step)
                        if u == SPLIT_AT and not last:
                            split_gates(k + 1, jobs_before(k))
                        if u == X_AT and not first:
                            add_to_stream(k - 1)
                    if not last:
                        assert chain.n == STEPS, chain.n

                chain.at(setup)
                for n, u in enumerate(sorted(PREPARE)):
                    if n == 0:
                        normalize(0)
                    if n == 2:
                        split_heads(0, 1)
                    if PREPARE[u] == ("turn_gate", 0):
                        for step in range(CHOICE_STEPS):
                            choose(0, step)
                        split_gates(0, 0)
                    job(0, 0, n, *PREPARE[u])
                    if n == 2:
                        dve.wait_ge(s_w, W_ALL)
                        flat = w_up[:].rearrange("p s e i -> p (s e i)")
                        both = w_up_r[:].rearrange("p s e i -> p (s e i)")
                        V.tensor_copy(both, flat).then_inc(s_const, 1)
                        dve.wait_ge(s_const, 1)
                        V.scalar_tensor_tensor(both, both.bitcast(F32), part[:], flat, ALU.mult,
                                               ALU.add).then_inc(s_const, 1)
                rounds(dve, BLOCKS, experts)
                gating(BLOCKS - 1, 1, QUADS - 1)
                add_to_stream(BLOCKS - 1)


def kernel(**inputs):
    import concourse.bacc as bacc
    from concourse.bass_utils import run_bass_kernel_spmd

    arrays, shape = lay_out(inputs)
    nc = bacc.Bacc("TRN2", target_bir_lowering=False, num_devices=1)
    io = {n: nc.dram_tensor(n + "_dram", a.shape, mybir.dt.from_np(a.dtype), kind="ExternalInput").ap()
          for n, a in arrays.items()}
    io["out"] = nc.dram_tensor("out_dram", (TOKENS, D), F32, kind="ExternalOutput").ap()
    program(nc, io)
    r = run_bass_kernel_spmd(nc, [{n + "_dram": a for n, a in arrays.items()}], core_ids=[0])
    return r.results[0]["out_dram"].reshape(shape)


def lay_out(inputs):
    c = np.ascontiguousarray
    x = np.asarray(inputs["x"])
    a = {"x": c(x.reshape(TOKENS, D))}
    ctx = np.asarray(inputs["ctx_1024"])
    a["ctx"] = c(ctx.reshape(BATCH * CTX, D))
    a["pointers"] = c(np.asarray(inputs["itok_BxS_0_4092"]).reshape(TILES, P).T)
    a["ids"] = c(np.asarray(inputs["itok_BxS_0_7"]).reshape(TOKENS))
    a["positions"] = np.arange(IDS, dtype=np.float32)
    a["identity"] = np.eye(P, dtype=np.float32)
    for n in ("Wqj", "Wkj", "Wvj", "Wqi", "Wki", "Wvi"):
        a["L0_xattn_" + n] = c(np.asarray(inputs["L0_xattn_" + n]))
    a["L0_xattn_WoutT"] = c(np.asarray(inputs["L0_xattn_Wout"]).T)
    a["L0_xattn_gain"] = c(np.asarray(inputs["L0_xattn_gain"]).reshape(1))
    a["L0_xattn_council_weights"] = c(np.asarray(inputs["L0_xattn_council_weights"]))

    def get(name):
        return np.asarray(inputs[name])

    a["L0_ffn_w_up"] = c(np.concatenate([get("L0_ffn_W1"), get("L0_ffn_Ws1")[None]]).transpose(2, 0, 1))
    down = np.concatenate([get("L0_ffn_W2"), get("L0_ffn_Ws2")[None]])
    a["L0_ffn_w_down"] = c(down.reshape(GROUPS0, D, CH, P).transpose(3, 0, 2, 1))
    a["L0_ffn_b_up"] = c(np.concatenate([get("L0_ffn_b1"), get("L0_ffn_bs1")[None]]).reshape(GROUPS0 * CH, P).T)
    a["L0_ffn_b_down"] = c(np.concatenate([get("L0_ffn_b2"), get("L0_ffn_bs2")[None]]))
    a["L0_ffn_WgT"] = c(get("L0_ffn_Wg").T)
    a["L0_ffn_bg"], a["L0_ffn_bias"] = c(get("L0_ffn_bg")), c(get("L0_ffn_bias"))
    a["order0"] = np.arange(EXPERTS0, 0, -1, dtype=np.float32)

    ctx = ctx.reshape(BATCH, CTX, D)
    a["ctx_t"] = c(ctx.transpose(0, 2, 1))
    for n in ("Wq", "Wk", "Wv"):
        a["L1_xattn_" + n] = c(get("L1_xattn_" + n))
    a["L1_xattn_bqk"] = c(np.stack([get("L1_xattn_bq"), get("L1_xattn_bk")], axis=1))
    a["L1_xattn_bv"], a["L1_xattn_bo"] = c(get("L1_xattn_bv")), c(get("L1_xattn_bo"))
    strips = np.zeros((HG, 32, GROUPS, D), np.float32)
    strips[:, 0:DK] = get("L1_xattn_Wo").reshape(GROUPS, HG, DK, D).transpose(1, 2, 0, 3)
    a["L1_xattn_Wo_strips"] = strips.reshape(P, GROUPS, D)
    mask = np.zeros((P, HG), np.float32)
    place = np.zeros((P, 2, GROUPS, P), np.float32)
    place_m = np.zeros((HEADS, GROUPS, P), np.float32)
    for h in range(HEADS):
        g, j = divmod(h, HG)
        place_m[h, g, SHIFT_ROW + j] = 1
        mask[SHIFT_ROW + j, j] = 1
        for d in range(DK):
            for product, part in enumerate((0, 1, 0)):
                row = 32 * product + DK * j + d
                place[h * DK + d, part, g, row] = 1
                mask[row, j] = 1
    a["head_mask"] = mask
    a["place"], a["place_m"] = place, place_m
    a["head_sum"] = np.repeat(np.eye(HEADS, dtype=np.float32), DK, axis=0)

    blank = np.zeros
    f = np.float32
    a["L1_ffn_Wm"], a["L1_ffn_bm"] = c(get("L1_ffn_Wm")), c(get("L1_ffn_bm")[:, None])
    emb, emb_bd = get("L1_ffn_expert_emb"), blank((H1, HD1, H1, E1), f)
    w1, w_up = get("L1_ffn_W1").reshape(PAIRS, 2, HD1, I1), blank((2, 4, HD1, 2, PAIRS, 2, I1), f)
    w2, w_down = get("L1_ffn_W2").reshape(PAIRS, 2, I1, HD1), blank((2, I1, PAIRS, 2, HD1), f)
    place_t, place_g = blank((H1, HD1, 2, HP, 2, 4, HD1), f), blank((2, H1 // 2, E1, H1 // 2, 2, E1 // 2, HD1), f)
    for h in range(H1):
        emb_bd[h, :, h] = emb
        for d in range(HD1):
            for product in range(4):
                place_t[h, d, product % 2, h // 2, h % 2, product, d] = 1
        for e in range(E1):
            place_g[:, h % (H1 // 2), e, h % (H1 // 2), e // 8, e % 8, :] = 1
    for s in range(2):
        for product in range(4):
            w_up[s, product, :, s] = w1.transpose(2, 0, 1, 3)
        w_down[s, :, :, s] = w2[:, s].transpose(1, 0, 2)
    a["L1_ffn_emb"] = emb_bd.reshape(P, P)
    a["L1_ffn_w_up"] = w_up.reshape(P, 2, PAIRS, P)
    a["L1_ffn_w_down"] = w_down.reshape(P, PAIRS, 32)
    a["place_t"], a["place_g"] = place_t.reshape(P, 2, HP, P), place_g.reshape(P, H1 // 2, 2, P)
    low = np.tile(np.repeat(np.array([0, 0, 1, 1], f), HD1), 2)
    a["L1_ffn_part"] = -low[:, None]
    a["L1_ffn_b_up"] = c(get("L1_ffn_b1").reshape(PAIRS, P).T)
    a["L1_ffn_b_down"] = c(get("L1_ffn_b2").reshape(2, P).T)
    a["L1_ffn_wo"] = c(np.tile(get("L1_ffn_Wo").reshape(H1, HD1, D).transpose(1, 0, 2), (8, 1, 1)))
    a["L1_ffn_bo"] = c(get("L1_ffn_bo"))
    a["order1"] = np.arange(E1, 0, -1, dtype=np.float32)
    return a, x.shape
```
